# Optimizing a Trainium2 kernel written in Bass

```python
import numpy as np
import jax
import jax.numpy as jnp

def _softmax(x, axis=-1):
    return jax.nn.softmax(x, axis=axis)

def _gelu(x):
    return jax.nn.gelu(x, approximate=True)

def _silu(x):
    return jax.nn.silu(x)

def _sigmoid(x):
    return jax.nn.sigmoid(x)

def _layernorm(x, axis=-1, eps=1e-05):
    m = jnp.mean(x, axis=axis, keepdims=True)
    v = jnp.var(x, axis=axis, keepdims=True)
    return (x - m) / jnp.sqrt(v + eps)

def _scatter_add(tgt, idx, src, axis=0):
    return tgt.at[idx].add(src)

def _segment_sum(src, seg, n):
    return jax.ops.segment_sum(src, seg, n)
kernel_name = 'mk_seq_postln_d2_jaxref_r8_691946'

def setup_inputs(seed: int=0):
    np.random.seed(seed)
    _w = jnp.asarray

    def _L0_attn_setup():
        import jax, jax.numpy as jnp
        from jax import lax
        import numpy as np
        D_MODEL = 128
        D_STATE = 64
        D_CONV = 4
        EXPAND = 2
        HEADDIM = 128
        NGROUPS = 1
        CHUNK = 32
        D_INNER = EXPAND * D_MODEL
        NHEADS = D_INNER // HEADDIM
        CONV_DIM = D_INNER + 2 * NGROUPS * D_STATE
        D_IN_PROJ = D_INNER + CONV_DIM + NHEADS

        def _segsum_exp(t):
            T = t.shape[-1]
            cs = jnp.cumsum(t, axis=-1)
            d = cs[..., :, None] - cs[..., None, :]
            mask = jnp.tril(jnp.ones((T, T), dtype=bool))
            return jnp.where(mask, jnp.exp(jnp.where(mask, d, 0.0)), 0.0)

        def _ssd_scan(x, dt, A, Bm, Cm, chunk):
            Bz, L, H, P = x.shape
            G, N = (Bm.shape[2], Bm.shape[3])
            nc = L // chunk
            rep = H // G
            Bh = jnp.repeat(Bm, rep, axis=2)
            Ch = jnp.repeat(Cm, rep, axis=2)
            xc = x.reshape(Bz, nc, chunk, H, P)
            dtc = dt.reshape(Bz, nc, chunk, H)
            Bc = Bh.reshape(Bz, nc, chunk, H, N)
            Cc = Ch.reshape(Bz, nc, chunk, H, N)
            dA = dtc * A[None, None, None, :]
            dAh = jnp.transpose(dA, (0, 1, 3, 2))
            A_cs = jnp.cumsum(dAh, axis=-1)
            Lmat = _segsum_exp(dAh)
            Y_diag = jnp.einsum('bcqhn,bckhn,bchqk,bckh,bckhp->bcqhp', Cc, Bc, Lmat, dtc, xc)
            decay_states = jnp.exp(A_cs[..., -1:] - A_cs)
            states = jnp.einsum('bckhn,bchk,bckh,bckhp->bchpn', Bc, decay_states, dtc, xc)
            chunk_total = jnp.transpose(A_cs[..., -1], (0, 2, 1))
            padded = jnp.pad(chunk_total, ((0, 0), (0, 0), (1, 0)))
            decay_chunk = _segsum_exp(padded)
            states_cat = jnp.concatenate([jnp.zeros_like(states[:, :1]), states], axis=1)
            new_states = jnp.einsum('bhzc,bchpn->bzhpn', decay_chunk, states_cat)
            prev = new_states[:, :-1]
            Y_off = jnp.einsum('bcqhn,bchpn,bchq->bcqhp', Cc, prev, jnp.exp(A_cs))
            return (Y_diag + Y_off).reshape(Bz, L, H, P)
        key = jax.random.key(seed)
        ks = jax.random.split(key, 8)
        x = jax.random.normal(ks[0], (2, 512, D_MODEL), dtype=jnp.float32)
        W_in = jax.random.normal(ks[1], (D_IN_PROJ, D_MODEL), dtype=jnp.float32) * 0.02
        conv_w = jax.random.normal(ks[2], (CONV_DIM, 1, D_CONV), dtype=jnp.float32) * 0.2
        conv_b = jnp.zeros((CONV_DIM,), dtype=jnp.float32)
        A_init = jax.random.uniform(ks[3], (NHEADS,), minval=1.0, maxval=16.0)
        A_log = jnp.log(A_init).astype(jnp.float32)
        dtv = jnp.exp(jax.random.uniform(ks[4], (NHEADS,)) * (np.log(0.1) - np.log(0.001)) + np.log(0.001))
        dtv = jnp.clip(dtv, 0.001, None)
        dt_bias = (dtv + jnp.log(-jnp.expm1(-dtv))).astype(jnp.float32)
        D_skip = jnp.ones((NHEADS,), dtype=jnp.float32)
        W_out = jax.random.normal(ks[5], (D_MODEL, D_INNER), dtype=jnp.float32) * 0.02
        return {'x': x, 'W_in': W_in, 'conv_w': conv_w, 'conv_b': conv_b, 'A_log': A_log, 'dt_bias': dt_bias, 'D_skip': D_skip, 'W_out': W_out}
    _L0_attn_in = _L0_attn_setup()

    def _L0_ffn_setup():
        import jax, jax.numpy as jnp
        import numpy as np
        D_MODEL = 128
        N_EXPERTS = 8
        TOP_K = 2
        BOTTLENECK = 64
        B, S = (2, 512)
        ADAPTER_SCALE = 0.5

        def _moe_forward(x, w_gate, w_noise, Wd, bd, Wu, bu):
            b, s, d = x.shape
            xf = x.reshape(-1, d)
            T = xf.shape[0]
            clean_logits = xf @ w_gate
            logits = clean_logits
            k1 = min(TOP_K + 1, N_EXPERTS)
            top_logits, top_idx = jax.lax.top_k(logits, k1)
            top_k_logits = top_logits[:, :TOP_K]
            top_k_idx = top_idx[:, :TOP_K]
            top_k_gates = jax.nn.softmax(top_k_logits, axis=-1)
            rows = jnp.arange(T)[:, None]
            gates = jnp.zeros((T, N_EXPERTS), dtype=top_k_gates.dtype)
            gates = gates.at[rows, top_k_idx].set(top_k_gates)
            h = jax.nn.relu(jnp.einsum('td,edb->teb', xf, Wd) + bd[None, :, :])
            y = jnp.einsum('teb,ebd->ted', h, Wu) + bu[None, :, :]
            y = ADAPTER_SCALE * y
            out = jnp.einsum('te,ted->td', gates, y)
            return out.reshape(b, s, d)
        key = jax.random.key(seed)
        ks = jax.random.split(key, 8)
        sd = 0.02
        x = jax.random.normal(ks[0], (B, S, D_MODEL), dtype=jnp.float32)
        w_gate = jax.random.normal(ks[1], (D_MODEL, N_EXPERTS), dtype=jnp.float32) * sd
        w_noise = jax.random.normal(ks[2], (D_MODEL, N_EXPERTS), dtype=jnp.float32) * sd
        Wd = jax.random.normal(ks[3], (N_EXPERTS, D_MODEL, BOTTLENECK), dtype=jnp.float32) * sd
        bd = jnp.zeros((N_EXPERTS, BOTTLENECK), dtype=jnp.float32)
        Wu = jax.random.normal(ks[4], (N_EXPERTS, BOTTLENECK, D_MODEL), dtype=jnp.float32) * sd
        bu = jnp.zeros((N_EXPERTS, D_MODEL), dtype=jnp.float32)
        return {'x': x, 'w_gate': w_gate, 'w_noise': w_noise, 'Wd': Wd, 'bd': bd, 'Wu': Wu, 'bu': bu}
    _L0_ffn_in = _L0_ffn_setup()

    def _L1_attn_setup():
        import jax, jax.numpy as jnp
        import numpy as np
        import math
        HIDDEN = 128
        NUM_LAYERS = 24
        INIT_RANGE = 0.02
        key = jax.random.key(seed)
        k1, k2 = jax.random.split(key)
        B, S, H = (4, 512, HIDDEN)
        hidden_states = jax.random.normal(k1, (B, S, H), dtype=jnp.float32)
        std = INIT_RANGE / math.sqrt(2.0 * NUM_LAYERS * H)
        W_q = jax.random.normal(k2, (H, H), dtype=jnp.float32) * std
        return {'hidden_states': hidden_states, 'W_q': W_q}
    _L1_attn_in = _L1_attn_setup()

    def _L1_ffn_setup():
        import jax, jax.numpy as jnp
        import numpy as np
        B, N, C, F, E, K = (4, 256, 128, 512, 8, 2)
        key = jax.random.key(seed)
        ks = jax.random.split(key, 6)
        x = jax.random.normal(ks[0], (B, N, C), dtype=jnp.float32)
        router_w = jax.random.normal(ks[1], (E, C), dtype=jnp.float32) * 0.01
        w1 = jax.random.normal(ks[2], (E, F, C), dtype=jnp.float32) * 0.02
        b1 = jnp.zeros((E, F), dtype=jnp.float32)
        w2 = jax.random.normal(ks[3], (E, C, F), dtype=jnp.float32) * 0.02
        b2 = jnp.zeros((E, C), dtype=jnp.float32)
        return {'x': x, 'router_w': router_w, 'w1': w1, 'b1': b1, 'w2': w2, 'b2': b2}
    _L1_ffn_in = _L1_ffn_setup()
    _d = {'L0_attn_x': _L0_attn_in['x'], 'L0_attn_W_in': _L0_attn_in['W_in'], 'L0_attn_conv_w': _L0_attn_in['conv_w'], 'L0_attn_conv_b': _L0_attn_in['conv_b'], 'L0_attn_A_log': _L0_attn_in['A_log'], 'L0_attn_dt_bias': _L0_attn_in['dt_bias'], 'L0_attn_D_skip': _L0_attn_in['D_skip'], 'L0_attn_W_out': _L0_attn_in['W_out'], 'L0_ffn_w_gate': _L0_ffn_in['w_gate'], 'L0_ffn_w_noise': _L0_ffn_in['w_noise'], 'L0_ffn_Wd': _L0_ffn_in['Wd'], 'L0_ffn_bd': _L0_ffn_in['bd'], 'L0_ffn_Wu': _L0_ffn_in['Wu'], 'L0_ffn_bu': _L0_ffn_in['bu'], 'L1_attn_W_q': _L1_attn_in['W_q'], 'L1_ffn_router_w': _L1_ffn_in['router_w'], 'L1_ffn_w1': _L1_ffn_in['w1'], 'L1_ffn_b1': _L1_ffn_in['b1'], 'L1_ffn_w2': _L1_ffn_in['w2'], 'L1_ffn_b2': _L1_ffn_in['b2']}
    _x0 = _d['L0_attn_x']
    _d['L0_attn_x'] = jax.random.normal(jax.random.fold_in(jax.random.key(seed), 1), (2, 2048, 128), dtype=_x0.dtype)
    del _x0
    return _d

def reference(L0_attn_x, L0_attn_W_in, L0_attn_conv_w, L0_attn_conv_b, L0_attn_A_log, L0_attn_dt_bias, L0_attn_D_skip, L0_attn_W_out, L0_ffn_w_gate, L0_ffn_w_noise, L0_ffn_Wd, L0_ffn_bd, L0_ffn_Wu, L0_ffn_bu, L1_attn_W_q, L1_ffn_router_w, L1_ffn_w1, L1_ffn_b1, L1_ffn_w2, L1_ffn_b2):

    def _L0_attn_ref(x, W_in, conv_w, conv_b, A_log, dt_bias, D_skip, W_out):
        import jax, jax.numpy as jnp
        from jax import lax
        import numpy as np
        D_MODEL = 128
        D_STATE = 64
        D_CONV = 4
        EXPAND = 2
        HEADDIM = 128
        NGROUPS = 1
        CHUNK = 32
        D_INNER = EXPAND * D_MODEL
        NHEADS = D_INNER // HEADDIM
        CONV_DIM = D_INNER + 2 * NGROUPS * D_STATE
        D_IN_PROJ = D_INNER + CONV_DIM + NHEADS

        def _segsum_exp(t):
            T = t.shape[-1]
            cs = jnp.cumsum(t, axis=-1)
            d = cs[..., :, None] - cs[..., None, :]
            mask = jnp.tril(jnp.ones((T, T), dtype=bool))
            return jnp.where(mask, jnp.exp(jnp.where(mask, d, 0.0)), 0.0)

        def _ssd_scan(x, dt, A, Bm, Cm, chunk):
            Bz, L, H, P = x.shape
            G, N = (Bm.shape[2], Bm.shape[3])
            nc = L // chunk
            rep = H // G
            Bh = jnp.repeat(Bm, rep, axis=2)
            Ch = jnp.repeat(Cm, rep, axis=2)
            xc = x.reshape(Bz, nc, chunk, H, P)
            dtc = dt.reshape(Bz, nc, chunk, H)
            Bc = Bh.reshape(Bz, nc, chunk, H, N)
            Cc = Ch.reshape(Bz, nc, chunk, H, N)
            dA = dtc * A[None, None, None, :]
            dAh = jnp.transpose(dA, (0, 1, 3, 2))
            A_cs = jnp.cumsum(dAh, axis=-1)
            Lmat = _segsum_exp(dAh)
            Y_diag = jnp.einsum('bcqhn,bckhn,bchqk,bckh,bckhp->bcqhp', Cc, Bc, Lmat, dtc, xc)
            decay_states = jnp.exp(A_cs[..., -1:] - A_cs)
            states = jnp.einsum('bckhn,bchk,bckh,bckhp->bchpn', Bc, decay_states, dtc, xc)
            chunk_total = jnp.transpose(A_cs[..., -1], (0, 2, 1))
            padded = jnp.pad(chunk_total, ((0, 0), (0, 0), (1, 0)))
            decay_chunk = _segsum_exp(padded)
            states_cat = jnp.concatenate([jnp.zeros_like(states[:, :1]), states], axis=1)
            new_states = jnp.einsum('bhzc,bchpn->bzhpn', decay_chunk, states_cat)
            prev = new_states[:, :-1]
            Y_off = jnp.einsum('bcqhn,bchpn,bchq->bcqhp', Cc, prev, jnp.exp(A_cs))
            return (Y_diag + Y_off).reshape(Bz, L, H, P)
        Bz, L, _ = x.shape
        proj = x @ W_in.T
        z = proj[..., :D_INNER]
        xBC = proj[..., D_INNER:D_INNER + CONV_DIM]
        dt_raw = proj[..., D_INNER + CONV_DIM:]
        xBC_t = jnp.transpose(xBC, (0, 2, 1))
        conv = lax.conv_general_dilated(xBC_t, conv_w, (1,), [(D_CONV - 1, 0)], dimension_numbers=('NCH', 'OIH', 'NCH'), feature_group_count=CONV_DIM)
        xBC = jnp.transpose(conv + conv_b[None, :, None], (0, 2, 1))
        xBC = jax.nn.silu(xBC)
        x_ssm = xBC[..., :D_INNER].reshape(Bz, L, NHEADS, HEADDIM)
        B_ssm = xBC[..., D_INNER:D_INNER + NGROUPS * D_STATE].reshape(Bz, L, NGROUPS, D_STATE)
        C_ssm = xBC[..., D_INNER + NGROUPS * D_STATE:].reshape(Bz, L, NGROUPS, D_STATE)
        dt = jax.nn.softplus(dt_raw + dt_bias[None, None, :])
        A = -jnp.exp(A_log)
        y = _ssd_scan(x_ssm, dt, A, B_ssm, C_ssm, CHUNK)
        y = y + x_ssm * D_skip[None, None, :, None]
        y = y.reshape(Bz, L, D_INNER)
        y = y * jax.nn.silu(z)
        return y @ W_out.T

    def _L0_ffn_ref(x, w_gate, w_noise, Wd, bd, Wu, bu):
        import jax, jax.numpy as jnp
        import numpy as np
        D_MODEL = 128
        N_EXPERTS = 8
        TOP_K = 2
        BOTTLENECK = 64
        B, S = (2, 512)
        ADAPTER_SCALE = 0.5

        def _moe_forward(x, w_gate, w_noise, Wd, bd, Wu, bu):
            b, s, d = x.shape
            xf = x.reshape(-1, d)
            T = xf.shape[0]
            clean_logits = xf @ w_gate
            logits = clean_logits
            k1 = min(TOP_K + 1, N_EXPERTS)
            top_logits, top_idx = jax.lax.top_k(logits, k1)
            top_k_logits = top_logits[:, :TOP_K]
            top_k_idx = top_idx[:, :TOP_K]
            top_k_gates = jax.nn.softmax(top_k_logits, axis=-1)
            rows = jnp.arange(T)[:, None]
            gates = jnp.zeros((T, N_EXPERTS), dtype=top_k_gates.dtype)
            gates = gates.at[rows, top_k_idx].set(top_k_gates)
            h = jax.nn.relu(jnp.einsum('td,edb->teb', xf, Wd) + bd[None, :, :])
            y = jnp.einsum('teb,ebd->ted', h, Wu) + bu[None, :, :]
            y = ADAPTER_SCALE * y
            out = jnp.einsum('te,ted->td', gates, y)
            return out.reshape(b, s, d)
        return _moe_forward(x, w_gate, w_noise, Wd, bd, Wu, bu)

    def _L1_attn_ref(hidden_states, W_q):
        import jax, jax.numpy as jnp
        import numpy as np
        import math
        HIDDEN = 128
        NUM_LAYERS = 24
        INIT_RANGE = 0.02
        q = jnp.einsum('bsh,oh->bso', hidden_states, W_q)
        pre_attn = jnp.einsum('bso,bto->bst', q, hidden_states)
        attention = jnp.einsum('bst,bth->bsh', pre_attn, hidden_states)
        return attention

    def _L1_ffn_ref(x, router_w, w1, b1, w2, b2):
        import jax, jax.numpy as jnp
        import numpy as np
        B, N, C, F, E, K = (4, 256, 128, 512, 8, 2)
        Bx, Nx, Cx = x.shape
        x_flat = x.reshape(-1, Cx)
        router_logits = x_flat @ router_w.T
        router_probs = jax.nn.softmax(router_logits, axis=-1)
        expert_weights, expert_indices = jax.lax.top_k(router_probs, K)
        expert_weights = expert_weights / (jnp.sum(expert_weights, axis=-1, keepdims=True) + 1e-09)
        out = jnp.zeros_like(x_flat)
        for e in range(E):
            w_e = jnp.sum(jnp.where(expert_indices == e, expert_weights, 0.0), axis=-1)
            h = jax.nn.relu(x_flat @ w1[e].T + b1[e])
            y = h @ w2[e].T + b2[e]
            out = out + w_e[:, None] * y
        return out.reshape(Bx, Nx, Cx)
    x = L0_attn_x
    x = _layernorm(x + _L0_attn_ref(x, L0_attn_W_in, L0_attn_conv_w, L0_attn_conv_b, L0_attn_A_log, L0_attn_dt_bias, L0_attn_D_skip, L0_attn_W_out), axis=-1)
    x = _layernorm(x + _L0_ffn_ref(x, L0_ffn_w_gate, L0_ffn_w_noise, L0_ffn_Wd, L0_ffn_bd, L0_ffn_Wu, L0_ffn_bu), axis=-1)
    x = _layernorm(x + _L1_attn_ref(x, L1_attn_W_q), axis=-1)
    x = _layernorm(x + _L1_ffn_ref(x, L1_ffn_router_w, L1_ffn_w1, L1_ffn_b1, L1_ffn_w2, L1_ffn_b2), axis=-1)
    return x

_drawn_inputs = setup_inputs


def setup_inputs(seed=0):
    import zlib

    import numpy as np

    out = dict(_drawn_inputs(seed))
    spreads = {'L0_attn_conv_b': (0.0, 0.8),
     'L0_attn_D_skip': (1.0, 0.6),
     'L0_ffn_bd': (0.0, 0.8),
     'L0_ffn_bu': (0.0, 0.1),
     'L1_ffn_b1': (0.0, 0.359),
     'L1_ffn_b2': (0.0, 0.1)}
    factors = {'L0_attn_W_in': 8.0,
     'L0_attn_conv_w': 8.0,
     'L0_attn_A_log': 8.0,
     'L0_attn_dt_bias': 8.0,
     'L0_attn_W_out': 7.83,
     'L0_ffn_Wd': 4.869,
     'L0_ffn_Wu': 3.652}
    for name, (base, spread) in spreads.items():
        noise = np.random.default_rng([zlib.crc32(name.encode()), seed]).standard_normal(out[name].shape)
        drawn = base * np.exp(spread * noise) if base else spread * noise
        out[name] = jnp.asarray(drawn.astype(out[name].dtype))
    for name, factor in factors.items():
        out[name] = (out[name] * factor).astype(out[name].dtype)
    return out
```

```python
from contextlib import ExitStack

import concourse.bass as bass
from concourse import mybir

F32 = mybir.dt.float32
F32R = mybir.dt.float32r
ALU = mybir.AluOpType
ACT = mybir.ActivationFunctionType
AX = mybir.AxisListType

P = 128
TILE = 512
CH = TILE // P
NT = 8
NB = 2
NCHUNK = NT * CH
H = 2
N = 64
TAPS = 4
HIST = TAPS - 1
NE = 8
M0 = 4
FT = 4
EPS = 1e-5
SERIES = 9

C_ID, C_TRI, C_ONE, C_REV = 0, P, 2 * P, 3 * P
C_COLS = 3 * P + NE


class Steps:

    def __init__(self, sem, per):
        self.sem, self.per = sem, per

    def begin(self, t):
        self.base, self.k = t * self.per, 0

    def inc(self, ins):
        ins.then_inc(self.sem, 1)
        self.k += 1

    def wait(self, eng, back=0):
        eng.wait_ge(self.sem, self.base + self.k - back)

    def end(self):
        assert self.k == self.per, (self.sem, self.k, self.per)


def later(t, n):
    return not isinstance(t, int) or t >= n


def build_kernel(nc, x, xT, W_inT, conv_w, conv_b, A_log, dt_bias, D_skip, W_outT, w_gate, WdT, bd,
                 Wu, bu, Wq, router_wT, w1T, b1, w2T, b2, const, sel, out):
    ctx = ExitStack()
    with ctx:
        def sb(name, shape, dt=F32):
            return ctx.enter_context(nc.sbuf_tensor(name, shape, dt))

        def bank(name):
            return ctx.enter_context(nc.psum_tensor(name, [P, 512], F32))

        def sem(name):
            return ctx.enter_context(nc.semaphore(name))

        x_sb = sb("x_sb", [P, CH, P])
        xT_sb = sb("xT_sb", [P, NT, TILE])
        const_sb = sb("const_sb", [P, C_COLS])
        convw_sb = sb("convw_sb", [P, 3, TAPS])
        convb_sb = sb("convb_sb", [P, 3])
        small_sb = sb("small_sb", [P, 3, H])
        Wout_sb = sb("Wout_sb", [P, H, P])
        wgate_sb = sb("wgate_sb", [P, NE])
        bd_sb = sb("bd_sb", [P, M0])
        Wu_sb = sb("Wu_sb", [P, M0, P])
        bu_sb = sb("bu_sb", [2 * NE, P])
        Wq_sb = sb("Wq_sb", [P, P])
        rw_sb = sb("rw_sb", [P, NE])
        b1_sb = sb("b1_sb", [P, NE * FT])
        b2_sb = sb("b2_sb", [2 * NE, P])
        wraw = sb("wraw", [P, 2, TILE])
        ident = const_sb[:, C_ID:C_ID + P]
        tri = const_sb[:, C_TRI:C_TRI + P]
        ones = const_sb[:, C_ONE:C_ONE + P]
        rev = const_sb[:, C_REV:C_REV + NE]

        Win_hi, Win_lo = sb("Win_hi", [P, 640], F32R), sb("Win_lo", [P, 640], F32R)
        Wd_hi, Wd_lo = sb("Wd_hi", [P, M0 * P], F32R), sb("Wd_lo", [P, M0 * P], F32R)
        w_hi = sb("w_hi", [P, 2, NE * FT * P], F32R)
        w_lo = sb("w_lo", [P, 2, NE * FT * P], F32R)
        sel_r = sb("sel_r", [2 * NE, M0 * P + NE * P], F32R)
        bu_r = sb("bu_r", [2 * NE, 2, P], F32R)
        b2_r = sb("b2_r", [2 * NE, 2, P], F32R)

        dtv = sb("dtv", [P, NCHUNK, H])
        dA = sb("dA", [P, NCHUNK, H])
        sp = [sb(f"sp{i}", [P, NCHUNK, H]) for i in range(5)]
        expA = sb("expA", [P, H])
        K_DT, K_DA, K_NCS, K_REST, K_TOT = range(5)
        cols = sb("cols", [P, NCHUNK, H, 5])

        x_hi = [sb(f"x_hi{b}", [P, TILE], F32R) for b in range(NB)]
        x_lo = [sb(f"x_lo{b}", [P, TILE], F32R) for b in range(NB)]
        raw = sb("raw", [P, 3, HIST + TILE])
        hist = [sb(f"hist{b}", [P, 3, HIST]) for b in range(NB)]
        acc = sb("acc", [P, 3, TILE])
        BC = [sb(f"BC{b}", [P, TILE]) for b in range(NB)]
        xs = [sb(f"xs{b}", [P, H, TILE]) for b in range(NB)]
        z2 = [sb(f"z2{b}", [P, H, TILE]) for b in range(NB)]
        C0 = [sb("C0", [N, TILE])] * NB
        cur = [sb(f"cur{b}", [P, CH, H, 5]) for b in range(NB)]
        dAU = sb("dAU", [P, H, CH, P])
        E = sb("E", [P, H, CH, P])
        Cs = sb("Cs", [N, H, TILE])
        xdt = sb("xdt", [P, H, CH, P])
        Bw = sb("Bw", [P, H, CH, N])
        M = E
        state = sb("state", [N, H, CH, P])
        carry = [sb(f"carry{b}", [N, H, P]) for b in range(NB)]
        yd = xs
        yg = z2
        x1 = [sb(f"x1{b}", [P, CH, P]) for b in range(NB)]
        x1T = sb("x1T", [P, TILE])
        x1T_hi, x1T_lo = sb("x1T_hi", [P, TILE], F32R), sb("x1T_lo", [P, TILE], F32R)
        h0 = sb("h0", [P, M0, TILE])
        flat_h0 = h0[:, :, :].rearrange("p m q -> p (m q)")
        Win_sb, Wd_sb = flat_h0[:, 0:642], flat_h0[:, 1024:1024 + M0 * P]
        sel0_sb = xdt[0:2 * NE, 0, :, :].rearrange("p c q -> p (c q)")
        sel1_sb = E[0:2 * NE, :, :, :].rearrange("p h c q -> p (h c q)")
        x2 = sb("x2", [P, CH, P])
        x2T = xT_sb
        G = [sb(f"G{b}", [P, P]) for b in range(NB)]
        stats = {k: (sb(f"bn{k}", [P, CH, 6]), sb(f"mv{k}", [P, CH, 2]), sb(f"rstd{k}", [P, CH]))
                 for k in ("ln1", "ln2", "ln3", "ln4")}
        half = sb("half", [P, CH])
        route = {k: [sb(f"{k}{n}", s) for n, s in
                     (("lg", [P, CH, NE]), ("m1", [P, CH]), ("m2", [P, CH]), ("key", [P, CH, NE]),
                      ("kmax", [P, CH]), ("oh1", [P, CH, NE]), ("oh2", [P, CH, NE]),
                      ("d", [P, CH]), ("e2", [P, CH]), ("g", [P, CH, NE]), ("sum", [P, CH]))]
                 for k in ("ra", "rb")}
        g16 = {k: sb(f"g16{k}", [P, CH, 2 * NE], F32R) for k in ("ra", "rb")}
        gT = sb("gT", [2 * NE, TILE], F32R)

        KI = [sb(f"KI{b}", [P, P]) for b in range(NB)]
        x2T_cur = x1T
        x3 = x1
        x3T = acc[:, 0, :]
        x3T_hi, x3T_lo = x_hi, x_lo
        w16T = [gT, sb("w16T1", [2 * NE, TILE], F32R)]
        RH = 3
        h1 = h0
        h1_hi = [x1T_hi[:, :], Win_hi[:, 0:TILE], Wd_hi[:, :]]
        h1_lo = [x1T_lo[:, :], Win_lo[:, 0:TILE], Wd_lo[:, :]]
        wbc = E[:, :, :, :].rearrange("p h c q -> p h (c q)")
        yw = xdt[:, :, :, :].rearrange("p h c q -> p h (c q)")
        oT = [dAU[:, h, :, :].rearrange("p c q -> p (c q)") for h in range(H)]
        o_sb = x2

        ps = [bank(f"ps{i}") for i in range(8)]
        ps4 = [p[:, :].rearrange("p (c q) -> p c q", c=CH) for p in ps]

        s_in0 = sem("s_in0")
        s_in = sem("s_in")
        s_wraw, s_x = sem("s_wraw"), sem("s_x")
        s_prep = sem("s_prep")
        s_wd0, s_wd = sem("s_wd0"), sem("s_wd")
        s_w = Steps(sem("s_w"), 4)
        s_p0 = {e: sem(f"s_p0_{e}") for e in ("pe", "act", "dve")}
        s_absv = sem("s_absv")
        s_p0chain = sem("s_p0chain")
        s_xhi, s_xlo = sem("s_xhi"), sem("s_xlo")
        s_cur, s_dAU = sem("s_cur"), sem("s_dAU")
        s_proj = sem("s_proj")
        s_hist, s_raw, s_zt = sem("s_hist"), sem("s_raw"), sem("s_zt")
        s_tap = Steps(sem("s_tap"), 12)
        s_th = sem("s_th")
        s_conv = sem("s_conv")
        s_z = sem("s_z")
        s_C0 = sem("s_C0")
        s_ssd = sem("s_ssd")
        S_TX0, S_TX1, S_ROW0, S_TB, S_SC, S_ROW1, S_INC0, S_INC1, S_Y0, S_Y1, S_OUT = range(1, 12)
        s_diff = Steps(sem("s_diff"), CH * H)
        s_exp, s_mask, s_Cs = sem("s_exp"), sem("s_mask"), sem("s_Cs")
        s_xdt, s_Bw, s_M = sem("s_xdt"), sem("s_Bw"), sem("s_M")
        s_state = Steps(sem("s_state"), 1 + CH * H)
        s_yd, s_yg = sem("s_yd"), sem("s_yg")
        s_ln = {k: (Steps(sem(f"s_{k}"), 1 + CH + (CH - 1) + CH), sem(f"s_{k}v"), sem(f"s_{k}r"))
                for k in ("ln1", "ln2", "ln3", "ln4")}
        s_moe = sem("s_moe")
        (E_XT, E_LG, E_H0, E_H1, E_H2, E_H3, E_GT, E_B0, E_B1, E_B2, E_B3, E_OUT, E_X2T,
         E_G) = range(1, 15)
        s_moeA = sem("s_moeA")
        A_XT, A_H0, A_H1, A_H2, A_H3, A_GT, A_X2T = range(1, 8)
        s_moeD = sem("s_moeD")
        D_LG, D_B0, D_B1, D_B2, D_B3, D_G = range(1, 7)
        s_x1hi, s_x1lo = sem("s_x1hi"), sem("s_x1lo")
        s_rt = {"ra": Steps(sem("s_ra"), 19), "rb": Steps(sem("s_rb"), 23)}
        s_rexp = {k: sem(f"s_{k}e") for k in ("ra", "rb")}
        s_KI = sem("s_KI")
        s_KIp = sem("s_KIp")
        s_cur2 = sem("s_cur2")
        s_pre = sem("s_pre")
        Q_ATT, Q_XT, Q_LG, Q_GT, Q_B2 = range(1, 6)
        s_x3T, s_x3hi, s_x3lo, s_w16T, s_acc0 = (sem(n) for n in
                                                 ("s_x3T", "s_x3hi", "s_x3lo", "s_w16T", "s_acc0"))
        s_fin = sem("s_fin")
        s_up, s_relu, s_hhi, s_hlo, s_down = (sem(n) for n in
                                              ("s_up", "s_relu", "s_hhi", "s_hlo", "s_down"))
        s_wb, s_wbc, s_yw, s_sum = (sem(n) for n in ("s_wb", "s_wbc", "s_yw", "s_sum"))
        s_out = sem("s_out")
        s_apart = sem("s_apart")

        block = ctx.enter_context(nc.Block())

        def apart(eng):
            eng.sem_inc(s_apart, 1)

        def since(q):
            return RH if q >= RH else (2, 1, 3)[q]

        def mm3(pe, dst, a_hi, a_lo, b_hi, b_lo, start=True, stop=True):
            pe.matmul(dst, a_hi, b_hi, start=start, stop=False)
            pe.matmul(dst, a_hi, b_lo, start=False, stop=False)
            return pe.matmul(dst, a_lo, b_hi, start=False, stop=stop)

        @block.sync
        def _(sp_):
            sp_.dma_start(const_sb[:], const).then_inc(s_in0, 16)
            sp_.dma_start(small_sb[:, 0, :], A_log).then_inc(s_in0, 16)
            sp_.dma_start(small_sb[:, 1, :], dt_bias).then_inc(s_in0, 16)
            sp_.dma_start(small_sb[:, 2, :], D_skip).then_inc(s_in0, 16)
            sp_.dma_start(Win_sb, W_inT).then_inc(s_in0, 16)
            sp_.dma_start(xT_sb[:, 0:4, :], xT[:, 0:4, :]).then_inc(s_in0, 16)
            sp_.dma_start(xT_sb[:, 4:8, :], xT[:, 4:8, :]).then_inc(s_in0, 16)
            for dst, src in ((convw_sb, conv_w), (convb_sb, conv_b), (Wout_sb, W_outT),
                             (wgate_sb, w_gate), (bd_sb, bd), (Wu_sb, Wu),
                             (bu_sb, bu), (Wq_sb, Wq), (rw_sb, router_wT), (b1_sb, b1),
                             (b2_sb, b2)):
                sp_.dma_start(dst[:], src).then_inc(s_in, 16)
            sp_.dma_start(Wd_sb, WdT).then_inc(s_in, 16)
            sp_.dma_start(sel0_sb, sel[:, 0:M0 * P]).then_inc(s_in, 16)
            sp_.dma_start(sel1_sb, sel[:, M0 * P:]).then_inc(s_in, 16)

            def tile(t, b):
                if later(t, 1):
                    sp_.wait_ge(s_ln["ln1"][0].sem, s_ln["ln1"][0].per * (t - 1) + 1)
                sp_.dma_start(x_sb[:], x[:, bass.ds(CH * t, CH), :]).then_inc(s_x, 16)
                if later(t, 1):
                    sp_.wait_ge(s_w.sem, 4 * t)
                sp_.dma_start(wraw[:, 0, :], w1T[:, bass.ds(t * TILE, TILE)]).then_inc(s_wraw, 16)
                sp_.dma_start(wraw[:, 1, :], w2T[:, bass.ds(t * TILE, TILE)]).then_inc(s_wraw, 16)
                sp_.wait_ge(s_conv, 3 * t + 1)
                if later(t, 1):
                    sp_.wait_ge(s_ssd, 11 * (t - 1) + S_SC)
                    sp_.wait_ge(s_Cs, 2 * t)
                sp_.dma_start(C0[b][:], BC[b][N:2 * N, :]).then_inc(s_C0, 16)

            for t in range(NT):
                tile(t, t % NB)

            def store(u):
                sp_.wait_ge(s_ln["ln4"][0].sem, s_ln["ln4"][0].per * (u + 1))
                sp_.dma_start(out[:, bass.ds(CH * u, CH), :], o_sb[:]).then_inc(s_out, 16)

            for u in range(NT):
                store(u)
            sp_.wait_ge(s_out, 16 * NT)

        def ln_dve(dve, k, t, src, dst):
            st, rsem = s_ln[k][0], s_ln[k][2]
            bn, mv, rstd = stats[k]
            st.wait(dve)
            for c in range(CH):
                st.inc(nc.vector.bn_stats(bn[:, c, :], src[:, c, :]))
            for c in range(CH):
                st.wait(dve, back=CH - 1)
                apart(dve)
                if c == CH - 1:
                    nc.vector.bn_aggr(mv[:, c, :], bn[:, c, :]).then_inc(s_ln[k][1], 1)
                else:
                    st.inc(nc.vector.bn_aggr(mv[:, c, :], bn[:, c, :]))
            dve.wait_ge(rsem, 2 * (t + 1))
            for c in range(CH):
                i = nc.vector.tensor_scalar(dst[:, c, :], src[:, c, :], mv[:, c, 0:1],
                                            rstd[:, c:c + 1], ALU.subtract, ALU.mult)
                st.inc(i)
            st.end()

        def ln_pool(pool, k, t):
            bn, mv, rstd = stats[k]
            pool.wait_ge(s_ln[k][1], t + 1)
            apart(pool)
            nc.gpsimd.tensor_scalar(rstd[:], mv[:, :, 1], EPS, None, ALU.add).then_inc(s_ln[k][2], 1)
            pool.wait_ge(s_ln[k][2], 2 * t + 1)
            nc.gpsimd.tensor_tensor(rstd[:], rstd[:], half[:], ALU.pow).then_inc(s_ln[k][2], 1)

        def over_e(v):
            return v[:, :].unsqueeze(2).to_broadcast([P, CH, NE])

        def over_c(v):
            return v.unsqueeze(1).to_broadcast([P, CH, NE])

        def router_dve(dve, k, t, logits, emptied=None):
            st, e = s_rt[k], s_rexp[k]
            lg, m1, m2, key, kmax, oh1, oh2, d, e2, g, tot = route[k]
            V = nc.vector
            st.begin(t)

            def do(ins):
                st.inc(ins)
                st.wait(dve)

            ins = V.tensor_copy(lg[:], logits)
            if emptied is not None:
                ins.then_inc(emptied, 1)
                dve.wait_ge(emptied, 6 * t + D_LG)
                do(V.tensor_reduce(m1[:], lg[:], AX.X, ALU.max))
            else:
                do(ins)
                do(V.tensor_reduce(m1[:], lg[:], AX.X, ALU.max))

            def first_of(src, m, oh):
                do(V.tensor_tensor(key[:], src[:], over_e(m), ALU.is_equal))
                do(V.tensor_tensor(key[:], key[:], over_c(rev), ALU.mult))
                do(V.tensor_reduce(kmax[:], key[:], AX.X, ALU.max))
                do(V.tensor_tensor(oh[:], key[:], over_e(kmax), ALU.is_equal))

            first_of(lg, m1, oh1)
            do(V.scalar_tensor_tensor(out=g[:], in0=oh1[:], scalar=-3.0e38, in1=lg[:], op0=ALU.mult,
                                      op1=ALU.add))
            do(V.tensor_reduce(m2[:], g[:], AX.X, ALU.max))
            first_of(g, m2, oh2)
            do(V.tensor_tensor(d[:], m2[:], m1[:], ALU.subtract))
            if k == "ra":
                dve.wait_ge(e, t + 1)
                do(V.tensor_scalar(tot[:], e2[:], 1.0, 2.0, ALU.add, ALU.mult))
            else:
                do(V.tensor_tensor(g[:], lg[:], over_e(m1), ALU.subtract))
                dve.wait_ge(e, 2 * (t + 1))
                do(V.tensor_reduce(tot[:], g[:], AX.X, ALU.add))
                do(V.scalar_tensor_tensor(out=tot[:], in0=tot[:], scalar=1e-9, in1=e2[:],
                                          op0=ALU.mult, op1=ALU.add))
                do(V.tensor_scalar(tot[:], tot[:], 1.0, None, ALU.add))
            do(V.reciprocal(tot[:], tot[:]))
            do(V.tensor_tensor(oh2[:], oh2[:], over_e(e2), ALU.mult))
            do(V.tensor_tensor(g[:], oh1[:], oh2[:], ALU.add))
            do(V.tensor_tensor(g[:], g[:], over_e(tot), ALU.mult))
            do(V.tensor_copy(g16[k][:, :, 0:NE], g[:]))
            st.inc(V.tensor_tensor(g16[k][:, :, NE:2 * NE], g[:],
                                   g16[k][:, :, 0:NE].bitcast(F32), ALU.subtract))
            st.end()

        def router_act(act, k, t, d_at, g_at=None):
            e, d, e2, g = s_rexp[k], route[k][7], route[k][8], route[k][9]
            act.wait_ge(s_rt[k].sem, s_rt[k].per * t + d_at)
            nc.scalar.activation(e2[:], d[:], ACT.Exp).then_inc(e, 1)
            if g_at is not None:
                act.wait_ge(s_rt[k].sem, s_rt[k].per * t + g_at)
                nc.scalar.activation(g[:], g[:], ACT.Exp).then_inc(e, 1)

        @block.tensor
        def _(pe):
            pe.wait_ge(s_in0, 16 * 7)
            for n in range(NCHUNK):
                mm = pe.matmul(ps[7][:, n * H:(n + 1) * H], xT_sb[:, n // CH, (n % CH) * P:(n % CH + 1) * P],
                               Win_sb[:, 640:642], start=True, stop=True)
            mm.then_inc(s_p0["pe"], 1)
            pe.wait_ge(s_p0["dve"], 1)
            flat = dA[:, :, :].rearrange("p n h -> p (n h)")
            pe.matmul(ps[6][:, 0:H * NCHUNK], tri, flat, start=True, stop=True)
            pe.matmul(ps[5][:, 0:H * NCHUNK], ones, flat, start=True, stop=True).then_inc(s_p0["pe"], 1)
            pe.wait_ge(s_p0["act"], 4)
            pe.wait_ge(s_prep, 1)

            def front(t, b):
                pe.wait_ge(s_xhi, t + 1)
                pe.wait_ge(s_xlo, t + 1)
                for i, w in enumerate((4, 2, 3, 0, 1)):
                    if i < 2:
                        if later(t, 1):
                            pe.wait_ge(s_z, 2 * t - 1 + i)
                    elif i < 5:
                        pe.wait_ge(s_raw, 3 * t + i - 1)
                    c = slice(w * P, (w + 1) * P)
                    mm3(pe, ps[(b + i) % 2][:, :], Win_hi[:, c], Win_lo[:, c], x_hi[b][:], x_lo[b][:]
                        ).then_inc(s_proj, 1)

            def ssd(t, b):
                for h in range(H):
                    pe.wait_ge(s_conv, 3 * t + 2 + h)
                    if h == 0:
                        if later(t, 1):
                            pe.wait_ge(s_ln["ln1"][0].sem, s_ln["ln1"][0].per * (t - 1) + 1)
                    else:
                        pe.wait_ge(s_xdt, 2 * t + h)
                    for c in range(CH):
                        mm = pe.transpose(ps4[3][:, c, :], xs[b][:, h, c * P:(c + 1) * P], ident)
                    mm.then_inc(s_ssd, 1)
                pe.wait_ge(s_dAU, 2 * t + 1)
                if later(t, 1):
                    pe.wait_ge(s_state.sem, s_state.per * t)
                pe.matmul(ps[2][:, :], ones, dAU[:, 0, :, :], start=True, stop=True).then_inc(s_ssd, 1)
                pe.wait_ge(s_xdt, 2 * t + 2)
                apart(pe)
                for c in range(CH):
                    mm = pe.transpose(ps4[3][:, c, 0:N], BC[b][0:N, c * P:(c + 1) * P], ident[0:N, 0:N])
                mm.then_inc(s_ssd, 1)
                pe.wait_ge(s_C0, 16 * (t + 1))
                if later(t, 1):
                    pe.wait_ge(s_M, 2 * t)
                for c in range(CH):
                    q = slice(c * P, (c + 1) * P)
                    mm = pe.matmul(ps4[4][:, c, :], BC[b][0:N, q], C0[b][:, q], start=True, stop=True)
                mm.then_inc(s_ssd, 1)
                pe.wait_ge(s_dAU, 2 * t + 2)
                pe.wait_ge(s_exp, 2 * t + 1)
                pe.matmul(ps[2][:, :], ones, dAU[:, 1, :, :], start=True, stop=True).then_inc(s_ssd, 1)
                for h in range(H):
                    pe.wait_ge(s_Bw, 2 * t + h + 1)
                    if h == 0:
                        pe.wait_ge(s_exp, 2 * t + 2)
                    else:
                        pe.wait_ge(s_state.sem, s_state.per * t + 1 + CH)
                    for c in range(CH):
                        mm = pe.matmul(ps4[2][0:N, c, :], Bw[:, h, c, :], xdt[:, h, c, :],
                                       start=True, stop=True)
                    mm.then_inc(s_ssd, 1)
                for h in range(H):
                    pe.wait_ge(s_M, 2 * t + h + 1)
                    pe.wait_ge(s_Cs, 2 * t + h + 1)
                    pe.wait_ge(s_state.sem, s_state.per * t + 1 + CH * (h + 1))
                    if h == 0:
                        if later(t, 1):
                            pe.wait_ge(s_yd, 2 * t)
                    else:
                        pe.wait_ge(s_yd, 2 * t + 1)
                    for c in range(CH):
                        pe.matmul(ps4[5][:, c, :], xdt[:, h, c, :], M[:, h, c, :], start=True, stop=False)
                        mm = pe.matmul(ps4[5][:, c, :], state[:, h, c, :],
                                       Cs[:, h, c * P:(c + 1) * P], start=False, stop=True)
                    mm.then_inc(s_ssd, 1)
                pe.wait_ge(s_yg, 2 * t + 2)
                for c in range(CH):
                    for h in range(H):
                        mm = pe.matmul(ps4[3][:, c, :], yg[b][:, h, c * P:(c + 1) * P], Wout_sb[:, h, :],
                                       start=h == 0, stop=h == 1)
                mm.then_inc(s_ssd, 1)

            def moe(t, b):
                A, B, A4, B4 = ps[6], ps[7], ps4[6], ps4[7]
                pe.wait_ge(s_ln["ln1"][0].sem, s_ln["ln1"][0].per * (t + 1))
                if later(t, 1):
                    pe.wait_ge(s_moeA, 7 * t)
                for c in range(CH):
                    mm = pe.transpose(A4[:, c, :], x1[b][:, c, :], ident)
                mm.then_inc(s_moe, 1)
                pe.wait_ge(s_moeA, 7 * t + A_XT)
                if later(t, 1):
                    pe.wait_ge(s_moeD, 6 * t)
                for c in range(CH):
                    mm = pe.matmul(B[:, c * NE:(c + 1) * NE], x1T[:, c * P:(c + 1) * P], wgate_sb[:],
                                   start=True, stop=True)
                mm.then_inc(s_moe, 1)
                pe.wait_ge(s_x1lo, t + 1)
                if not later(t, 1):
                    pe.wait_ge(s_wd, 1)
                for m in range(M0):
                    if m == 1:
                        pe.wait_ge(s_moeD, 6 * t + D_LG)
                    if m > 1:
                        pe.wait_ge(s_moeA, 7 * t + A_H0 + m - 2)
                    r = slice(m * P, (m + 1) * P)
                    mm3(pe, (A if m % 2 == 0 else B)[:, :], Wd_hi[:, r], Wd_lo[:, r], x1T_hi[:],
                        x1T_lo[:]).then_inc(s_moe, 1)
                pe.wait_ge(s_rt["ra"].sem, s_rt["ra"].per * (t + 1))
                pe.wait_ge(s_moeA, 7 * t + A_H2)
                for c in range(CH):
                    mm = pe.transpose(A4[0:2 * NE, c, :], g16["ra"][:, c, :].bitcast(F32), ident)
                mm.then_inc(s_moe, 1)
                for m in range(M0):
                    if m == 0:
                        pe.wait_ge(s_moeA, 7 * t + A_GT)
                    if m > 1:
                        pe.wait_ge(s_moeD, 6 * t + D_B0 + m - 2)
                    pe.matmul((B if m % 2 == 0 else A)[:, :], sel_r[:, m * P:(m + 1) * P], gT[:],
                              start=True, stop=True).then_inc(s_moe, 1)
                pe.wait_ge(s_moeD, 6 * t + D_B3)
                for c in range(CH):
                    q = slice(c * P, (c + 1) * P)
                    for m in range(M0):
                        pe.matmul(B4[:, c, :], h0[:, m, q], Wu_sb[:, m, :], start=m == 0, stop=False)
                    pe.matmul(B4[:, c, :], gT[:, q], bu_r[:, 0, :], start=False, stop=False)
                    mm = pe.matmul(B4[:, c, :], gT[:, q], bu_r[:, 1, :], start=False, stop=True)
                mm.then_inc(s_moe, 1)
                pe.wait_ge(s_ln["ln2"][0].sem, s_ln["ln2"][0].per * (t + 1))
                for c in range(CH):
                    mm = pe.transpose(A4[:, c, :], x2[:, c, :], ident)
                mm.then_inc(s_moe, 1)
                for c in range(CH):
                    mm = pe.matmul(B[:, 0:P], x2[:, c, :], x2[:, c, :], start=c == 0, stop=c == CH - 1)
                mm.then_inc(s_moe, 1)

            front(0, 0)
            front(1, 1)
            ssd(0, 0)
            front(2, 0)
            ssd(1, 1)
            moe(0, 0)
            front(3, 1)
            ssd(2, 0)
            moe(1, 1)
            with pe.Fori(2, NT // 2) as j:
                front(2 * j, 0)
                ssd(2 * j - 1, 1)
                moe(2 * j - 2, 0)
                front(2 * j + 1, 1)
                ssd(2 * j, 0)
                moe(2 * j - 1, 1)
            ssd(NT - 1, 1)
            moe(NT - 2, 0)
            moe(NT - 1, 1)

            pe.wait_ge(s_moeD, 6 * NT)
            for b in range(NB):
                mm = pe.matmul(ps[b][:, 0:P], Wq_sb[:], G[b][:], start=True, stop=True)
            mm.then_inc(s_KIp, 1)
            pe.wait_ge(s_KI, 1)

            def prepare(u, b, piece):
                A, B, A4, B4 = ps[6], ps[7], ps4[6], ps4[7]
                if piece == 0:
                    pe.wait_ge(s_cur2, u + 1)
                    if later(u, 1):
                        pe.wait_ge(s_acc0, u)
                    for c in range(CH):
                        mm = pe.matmul(A4[:, c, :], x2T_cur[:, c * P:(c + 1) * P], KI[b][:], start=True,
                                       stop=True)
                    mm.then_inc(s_pre, 1)
                elif piece == 1:
                    pe.wait_ge(s_ln["ln3"][0].sem, s_ln["ln3"][0].per * (u + 1))
                    if later(u, 2):
                        pe.wait_ge(s_ln["ln4"][0].sem, s_ln["ln4"][0].per * (u - 2) + 1)
                    for c in range(CH):
                        mm = pe.transpose(B4[:, c, :], x3[b][:, c, :], ident)
                    mm.then_inc(s_pre, 1)
                    pe.wait_ge(s_x3T, u + 1)
                    for c in range(CH):
                        mm = pe.matmul(A[:, c * NE:(c + 1) * NE], x3T[:, c * P:(c + 1) * P], rw_sb[:],
                                       start=True, stop=True)
                    mm.then_inc(s_pre, 1)
                elif piece == 2:
                    pe.wait_ge(s_rt["rb"].sem, s_rt["rb"].per * (u + 1))
                    for c in range(CH):
                        mm = pe.transpose(B4[0:2 * NE, c, :], g16["rb"][:, c, :].bitcast(F32), ident)
                    mm.then_inc(s_pre, 1)
                elif piece == 3:
                    pe.wait_ge(s_w16T, u + 1)
                    pe.matmul(A[:, :], b2_r[:, 0, :], w16T[b][:], start=True, stop=False)
                    pe.matmul(A[:, :], b2_r[:, 1, :], w16T[b][:], start=False, stop=True
                              ).then_inc(s_pre, 1)

            def finish(u, b):
                pe.wait_ge(s_sum, 8 * (u + 1))
                for c in range(CH):
                    mm = pe.transpose(ps4[7][:, c, :], oT[b][:, c * P:(c + 1) * P], ident)
                mm.then_inc(s_fin, 1)

            LAG = 2

            def experts(u, b, last=False, first=False):
                def up(q):
                    e, f = divmod(q, FT)
                    if q >= RH or later(u, 1):
                        pe.wait_ge(s_relu, 32 * u + q + 1 - since(q))
                    r = slice(q * P, (q + 1) * P)
                    mm3(pe, ps[q % RH][:, :], w_hi[:, 0, r], w_lo[:, 0, r],
                        x3T_hi[b][:], x3T_lo[b][:]).then_inc(s_up, 1)
                    if f == 0:
                        if e > 0 or later(u, 1):
                            pe.wait_ge(s_wbc, 8 * u + e)
                        pe.matmul(ps[5][:, :], sel_r[:, M0 * P + e * P:M0 * P + (e + 1) * P], w16T[b][:],
                                  start=True, stop=True).then_inc(s_wb, 1)

                def down(q):
                    e, f = divmod(q, FT)
                    pe.wait_ge(s_hlo, 32 * u + q + 1)
                    if f == 0 and (e >= 2 or later(u, 1)):
                        pe.wait_ge(s_yw, 8 * u + e - 1)
                    r = slice(q * P, (q + 1) * P)
                    i = q % RH
                    mm = mm3(pe, ps[3 + e % 2][:, :], w_hi[:, 1, r], w_lo[:, 1, r], h1_hi[i],
                             h1_lo[i], start=f == 0, stop=f == FT - 1)
                    mm.then_inc(s_down, 1)

                pe.wait_ge(s_x3lo, u + 1)
                pe.wait_ge(s_acc0, u + 1)
                for q in range(LAG):
                    up(q)
                for q in range(NE * FT):
                    if q + LAG < NE * FT:
                        up(q + LAG)
                    down(q)
                    if q == 2 and not first:
                        finish(u - 1, 1 - b)
                    if q in (7, 12, 20, 27) and not last:
                        prepare(u + 1, 1 - b, (7, 12, 20, 27).index(q))

            for piece in range(4):
                prepare(0, 0, piece)
            pe.wait_ge(s_w.sem, 4 * NT)
            experts(0, 0, first=True)
            with pe.Fori(0, NT // 2 - 1) as v:
                experts(2 * v + 1, 1)
                experts(2 * v + 2, 0)
            experts(NT - 1, 1, last=True)
            finish(NT - 1, 1)

        @block.scalar
        def _(act):
            S = nc.scalar
            act.wait_ge(s_in0, 16 * 7)
            S.activation(expA[:], small_sb[:, 0, :], ACT.Exp).then_inc(s_p0["act"], 1)
            act.wait_ge(s_absv, 1)
            S.activation(sp[1][:], sp[1][:], ACT.Exp, scale=-1.0).then_inc(s_p0["act"], 1)
            act.wait_ge(s_p0["pe"], 2)
            ps6v = ps[6][:, 0:H * NCHUNK].rearrange("p (n h) -> p n h", h=H)
            ps5v = ps[5][:, 0:H * NCHUNK].rearrange("p (n h) -> p n h", h=H)
            S.activation(cols[:, :, :, K_NCS], ps6v, ACT.Copy, scale=-1.0).then_inc(s_p0["act"], 1)
            S.activation(cols[:, :, :, K_TOT], ps5v, ACT.Copy).then_inc(s_p0["act"], 1)
            act.wait_ge(s_p0["dve"], 2)
            S.activation(cols[:, :, :, K_REST], cols[:, :, :, K_REST], ACT.Exp).then_inc(s_p0["act"], 1)
            S.activation(cols[:, :, :, K_TOT], cols[:, :, :, K_TOT], ACT.Exp).then_inc(s_p0["act"], 1)

            def split(t, b):
                if later(t, 2):
                    act.wait_ge(s_proj, 5 * (t - 1))
                S.activation(x_hi[b][:], xT_sb[:, bass.ds(t, 1), :].rearrange("p o q -> p (o q)"),
                             ACT.Copy).then_inc(s_xhi, 1)

            def front(t, b):
                if later(t, 1):
                    act.wait_ge(s_tap.sem, 12 * t)
                S.activation(raw[:, :, 0:HIST], hist[b][:, :, :], ACT.Copy).then_inc(s_hist, 1)
                for i in range(3):
                    act.wait_ge(s_proj, 5 * t + i + 1)
                    S.activation(raw[:, i, HIST:], ps[(b + i) % 2][:, :], ACT.Copy).then_inc(s_raw, 1)
                act.wait_ge(s_raw, 3 * t + 3)
                act.wait_ge(s_hist, 2 * t + 1)
                S.activation(hist[b][:, :, :], raw[:, :, TILE:TILE + HIST], ACT.Copy).then_inc(s_hist, 1)
                for i in range(H):
                    act.wait_ge(s_proj, 5 * t + i + 4)
                    if later(t, 2):
                        act.wait_ge(s_ssd, 11 * (t - 2) + S_OUT)
                    S.activation(z2[b][:, i, :], ps[(b + i + 3) % 2][:, :], ACT.Tanh, scale=0.5
                                 ).then_inc(s_zt, 1)
                for i in range(3):
                    act.wait_ge(s_tap.sem, 12 * t + 4 * (i + 1))
                    if later(t, 2):
                        act.wait_ge(s_ssd, 11 * (t - 2) + S_SC)
                        act.wait_ge(s_C0, 16 * (t - 1))
                        act.wait_ge(s_yg, 2 * (t - 1))
                    S.activation(BC[b][:, :] if i == 0 else xs[b][:, i - 1, :], acc[:, i, :], ACT.Tanh).then_inc(s_th, 1)

            def ssd(t, b):
                for h in range(H):
                    act.wait_ge(s_diff.sem, 8 * t + 4 * h + 4)
                    S.activation(Cs[:, h, :], ps[2][0:N, :], ACT.Exp)
                    S.activation(E[:, h, :, :], E[:, h, :, :], ACT.Exp).then_inc(s_exp, 1)

            def moe(t, b):
                A, B = ps[6], ps[7]
                act.wait_ge(s_moe, 14 * t + E_XT)
                if later(t, 1):
                    act.wait_ge(s_moe, 14 * (t - 1) + E_H3)
                    act.wait_ge(s_x1lo, t)
                S.activation(x1T[:], A[:, :], ACT.Copy).then_inc(s_moeA, 1)
                for m in range(M0):
                    act.wait_ge(s_moe, 14 * t + E_H0 + m)
                    if m == 0 and later(t, 1):
                        act.wait_ge(s_moe, 14 * (t - 1) + E_OUT)
                    S.activation(h0[:, m, :], (A if m % 2 == 0 else B)[:, :], ACT.Relu,
                                 bias=bd_sb[:, m:m + 1]).then_inc(s_moeA, 1)
                router_act(act, "ra", t, 12)
                act.wait_ge(s_moe, 14 * t + E_GT)
                S.activation(gT[:], A[0:2 * NE, :], ACT.Copy).then_inc(s_moeA, 1)
                act.wait_ge(s_moe, 14 * t + E_X2T)
                S.activation(x2T[:, bass.ds(t, 1), :].rearrange("p o q -> p (o q)"), A[:, :], ACT.Copy
                             ).then_inc(s_moeA, 1)

            act.wait_ge(s_in, 16 * 14)
            act.wait_ge(s_prep, 1)
            split(0, 0)
            split(1, 1)
            front(0, 0)
            front(1, 1)
            ssd(0, 0)
            split(2, 0)
            split(3, 1)
            front(2, 0)
            ssd(1, 1)
            moe(0, 0)
            front(3, 1)
            ssd(2, 0)
            moe(1, 1)
            with act.Fori(2, NT // 2) as j:
                split(2 * j, 0)
                split(2 * j + 1, 1)
                front(2 * j, 0)
                ssd(2 * j - 1, 1)
                moe(2 * j - 2, 0)
                front(2 * j + 1, 1)
                ssd(2 * j, 0)
                moe(2 * j - 1, 1)
            ssd(NT - 1, 1)
            moe(NT - 2, 0)
            moe(NT - 1, 1)

            def prepare(u, b, piece):
                A, B = ps[6], ps[7]
                if piece == 1:
                    act.wait_ge(s_pre, 5 * u + Q_XT)
                    if later(u, 1):
                        act.wait_ge(s_x3lo, u)
                    S.activation(x3T, B[:, :], ACT.Copy).then_inc(s_x3T, 1)
                elif piece == 2:
                    router_act(act, "rb", u, 13, 14)
                elif piece == 3:
                    act.wait_ge(s_pre, 5 * u + Q_GT)
                    S.activation(w16T[b][:], B[0:2 * NE, :], ACT.Copy).then_inc(s_w16T, 1)
                elif piece == 4:
                    act.wait_ge(s_pre, 5 * u + Q_B2)
                    if later(u, 2):
                        act.wait_ge(s_fin, u - 1)
                    S.activation(oT[b], A[:, :], ACT.Copy).then_inc(s_acc0, 1)

            def experts(u, b, last=False, first=False):
                for q in range(NE * FT):
                    e, f = divmod(q, FT)
                    act.wait_ge(s_up, 32 * u + q + 1)
                    if q >= RH or later(u, 1):
                        act.wait_ge(s_hlo, 32 * u + q + 1 - since(q))
                    S.activation(h1[:, q % RH, :],
                                 ps[q % RH][:, :], ACT.Relu,
                                 bias=b1_sb[:, q:q + 1]).then_inc(s_relu, 1)
                    if f == 0:
                        act.wait_ge(s_wb, 8 * u + e + 1)
                        if e >= 2 or later(u, 1):
                            act.wait_ge(s_yw, 8 * u + e - 1)
                        S.activation(wbc[:, e % 2, :], ps[5][:, :], ACT.Copy).then_inc(s_wbc, 1)
                    if q in (14, 17, 21, 28) and not last:
                        prepare(u + 1, 1 - b, 1 + (14, 17, 21, 28).index(q))

            for piece in range(1, 5):
                prepare(0, 0, piece)
            experts(0, 0, first=True)
            with act.Fori(0, NT // 2 - 1) as v:
                experts(2 * v + 1, 1)
                experts(2 * v + 2, 0)
            experts(NT - 1, 1, last=True)

        @block.vector
        def _(dve):
            V = nc.vector
            p0 = Steps(s_p0chain, 0)
            p0.begin(0)

            def do(ins):
                p0.inc(ins)
                p0.wait(dve)

            for b in range(NB):
                V.memset(hist[b][:], 0.0)
                V.memset(carry[b][:], 0.0)
                V.memset(G[b][:], 0.0)
            v_, u_, s_, s2, q_ = sp
            dve.wait_ge(s_in0, 16 * 7)
            dve.wait_ge(s_p0["pe"], 1)
            raw_dt = ps[7][:, 0:H * NCHUNK].rearrange("p (n h) -> p n h", h=H)
            do(V.tensor_tensor(v_[:], raw_dt, small_sb[:, 1:2, :].to_broadcast([P, NCHUNK, H]), ALU.add))
            do(V.tensor_scalar(s2[:], v_[:], -1.0, None, ALU.mult))
            V.tensor_tensor(u_[:], s2[:], v_[:], ALU.max).then_inc(s_absv, 1)
            dve.wait_ge(s_p0["act"], 2)
            do(V.tensor_scalar(s2[:], u_[:], 2.0, None, ALU.add))
            do(V.reciprocal(s_[:], s2[:]))
            do(V.tensor_tensor(s_[:], s_[:], u_[:], ALU.mult))
            do(V.tensor_tensor(s2[:], s_[:], s_[:], ALU.mult))
            do(V.tensor_scalar(q_[:], s2[:], 1.0 / (2 * SERIES - 1), None, ALU.mult))
            for k in range(SERIES - 2, 0, -1):
                do(V.scalar_tensor_tensor(out=q_[:], in0=q_[:], scalar=1.0 / (2 * k + 1), in1=s2[:],
                                          op0=ALU.add, op1=ALU.mult))
            do(V.tensor_scalar(q_[:], q_[:], 1.0, 2.0, ALU.add, ALU.mult))
            do(V.tensor_tensor(q_[:], q_[:], s_[:], ALU.mult))
            do(V.scalar_tensor_tensor(out=dtv[:], in0=v_[:], scalar=0.0, in1=q_[:], op0=ALU.max,
                                      op1=ALU.add))
            do(V.scalar_tensor_tensor(out=dA[:], in0=dtv[:], scalar=-1.0,
                                      in1=expA[:, :].unsqueeze(1).to_broadcast([P, NCHUNK, H]),
                                      op0=ALU.mult, op1=ALU.mult))
            V.tensor_copy(cols[:, :, :, K_DT], dtv[:])
            V.tensor_copy(cols[:, :, :, K_DA], dA[:]).then_inc(s_p0["dve"], 1)

            do(V.tensor_copy(Win_hi[:], Win_sb[:, 0:640]))
            do(V.tensor_tensor(Win_lo[:], Win_sb[:, 0:640], Win_hi[:].bitcast(F32), ALU.subtract))
            dve.wait_ge(s_in, 16 * 14)
            do(V.tensor_scalar(convw_sb[:], convw_sb[:], 0.5, None, ALU.mult))
            do(V.tensor_scalar(convb_sb[:], convb_sb[:], 0.5, None, ALU.mult))
            do(V.tensor_scalar(Wout_sb[:], Wout_sb[:], 0.5, None, ALU.mult))
            V.tensor_copy(sel_r[:, 0:M0 * P], sel0_sb)
            V.tensor_copy(sel_r[:, M0 * P:], sel1_sb)
            for dst, src in ((bu_r, bu_sb), (b2_r, b2_sb)):
                do(V.tensor_copy(dst[:, 0, :], src[:]))
                do(V.tensor_tensor(dst[:, 1, :], src[:], dst[:, 0, :].bitcast(F32), ALU.subtract))
            V.memset(half[:], -0.5).then_inc(s_prep, 1)
            dve.wait_ge(s_prep, 1)
            dve.wait_ge(s_p0["act"], 4)
            V.tensor_tensor(cols[:, :, :, K_REST], cols[:, :, :, K_TOT], cols[:, :, :, K_NCS], ALU.add
                            ).then_inc(s_p0["dve"], 1)

            def front(t, b):
                s_tap.begin(t)
                for i in range(3):
                    dve.wait_ge(s_raw, 3 * t + i + 1)
                    if i == 0:
                        dve.wait_ge(s_hist, 2 * t + 1)
                    if later(t, 1):
                        dve.wait_ge(s_conv, 3 * t - 2 + i)
                    a = acc[:, i, :]
                    s_tap.inc(V.tensor_scalar(a, raw[:, i, 0:TILE], convw_sb[:, i, 0:1],
                                              convb_sb[:, i:i + 1], ALU.mult, ALU.add))
                    for k in range(1, TAPS):
                        s_tap.wait(dve)
                        s_tap.inc(V.scalar_tensor_tensor(out=a, in0=raw[:, i, k:k + TILE],
                                                         scalar=convw_sb[:, i, k:k + 1], in1=a,
                                                         op0=ALU.mult, op1=ALU.add))
                s_tap.end()
                for i in range(H):
                    dve.wait_ge(s_zt, 2 * t + i + 1)
                    V.scalar_tensor_tensor(out=z2[b][:, i, :], in0=z2[b][:, i, :], scalar=1.0,
                                           in1=ps[(b + i + 3) % 2][:, :], op0=ALU.add, op1=ALU.mult
                                           ).then_inc(s_z, 1)
                for i in range(3):
                    dve.wait_ge(s_th, 3 * t + i + 1)
                    dst = BC[b][:, :] if i == 0 else xs[b][:, i - 1, :]
                    V.scalar_tensor_tensor(out=dst, in0=dst, scalar=1.0, in1=acc[:, i, :],
                                           op0=ALU.add, op1=ALU.mult).then_inc(s_conv, 1)

            def ssd(t, b):
                dve.wait_ge(s_cur, t + 1)
                for h in range(H):
                    dve.wait_ge(s_ssd, 11 * t + (S_TX0, S_TX1)[h])
                    if later(t, 1):
                        dve.wait_ge(s_ssd, 11 * (t - 1) + (S_Y0, S_Y1)[h])
                    V.tensor_tensor(xdt[:, h, :, :], ps4[3],
                                    cur[b][:, :, h, K_DT:K_DT + 1].to_broadcast([P, CH, P]), ALU.mult
                                    ).then_inc(s_xdt, 1)

                def differences(h):
                    dve.wait_ge(s_ssd, 11 * t + (S_ROW0, S_ROW1)[h])
                    if later(t, 1):
                        dve.wait_ge(s_ssd, 11 * (t - 1) + (S_Y0, S_Y1)[h])
                    for c in range(CH):
                        s_diff.inc(V.tensor_scalar(E[:, h, c, :], ps4[2][:, c, :],
                                                   cur[b][:, c, h, K_NCS:K_NCS + 1], 0.0, ALU.add,
                                                   ALU.min))

                s_diff.begin(t)
                differences(0)
                dve.wait_ge(s_ssd, 11 * t + S_TB)
                for h in range(H):
                    if later(t, 1):
                        dve.wait_ge(s_ssd, 11 * (t - 1) + (S_INC0, S_INC1)[h])
                    V.tensor_tensor(Bw[:, h, :, :], ps4[3][:, :, 0:N],
                                    cur[b][:, :, h, K_REST:K_REST + 1].to_broadcast([P, CH, N]), ALU.mult
                                    ).then_inc(s_Bw, 1)
                differences(1)
                s_diff.end()
                s_state.begin(t)
                if later(t, 1):
                    dve.wait_ge(s_ssd, 11 * (t - 1) + S_Y1)
                if later(t, 2):
                    dve.wait_ge(s_state.sem, s_state.per * (t - 1))
                s_state.inc(V.tensor_copy(state[:, :, 0, :], carry[b][:]))
                for h in range(H):
                    dve.wait_ge(s_ssd, 11 * t + S_SC)
                    dve.wait_ge(s_mask, 2 * t + h + 1)
                    V.tensor_tensor(M[:, h, :, :], ps4[4], E[:, h, :, :], ALU.mult).then_inc(s_M, 1)
                    dve.wait_ge(s_ssd, 11 * t + (S_INC0, S_INC1)[h])
                    for c in range(CH):
                        s_state.wait(dve)
                        s_state.inc(V.scalar_tensor_tensor(
                            out=state[:, h, c + 1, :] if c + 1 < CH else carry[b][:, h, :],
                            in0=state[:, h, c, :],
                            scalar=cur[b][0:N, c, h, K_TOT:K_TOT + 1], in1=ps4[2][0:N, c, :],
                            op0=ALU.mult, op1=ALU.add))
                s_state.end()
                for h in range(H):
                    dve.wait_ge(s_ssd, 11 * t + (S_Y0, S_Y1)[h])
                    V.scalar_tensor_tensor(out=yd[b][:, h, :], in0=xs[b][:, h, :],
                                           scalar=small_sb[:, 2, h:h + 1], in1=ps[5][:, :],
                                           op0=ALU.mult, op1=ALU.add).then_inc(s_yd, 1)
                st = s_ln["ln1"][0]
                st.begin(t)
                dve.wait_ge(s_ssd, 11 * t + S_OUT)
                dve.wait_ge(s_x, 16 * (t + 1))
                if later(t, 2):
                    dve.wait_ge(s_moe, 14 * (t - 2) + E_XT)
                    dve.wait_ge(s_ln["ln2"][0].sem, s_ln["ln2"][0].per * (t - 2) + 1)
                st.inc(V.tensor_tensor(x1[b][:], ps4[3], x_sb[:], ALU.add))
                ln_dve(dve, "ln1", t, x1[b], x1[b])

            def moe(t, b):
                dve.wait_ge(s_moe, 14 * t + E_LG)
                if later(t, 1):
                    dve.wait_ge(s_moe, 14 * (t - 1) + E_GT)
                router_dve(dve, "ra", t, ps[7][:, 0:CH * NE].rearrange("p (c e) -> p c e", c=CH), s_moeD)
                for m in range(M0):
                    dve.wait_ge(s_moe, 14 * t + E_B0 + m)
                    dve.wait_ge(s_moeA, 7 * t + A_H0 + m)
                    V.tensor_tensor(h0[:, m, :], h0[:, m, :], (ps[7] if m % 2 == 0 else ps[6])[:, :],
                                    ALU.mult).then_inc(s_moeD, 1)
                st = s_ln["ln2"][0]
                st.begin(t)
                dve.wait_ge(s_moe, 14 * t + E_OUT)
                if later(t, 1):
                    dve.wait_ge(s_moe, 14 * t)
                st.inc(V.tensor_tensor(x2[:], ps4[7], x1[b][:], ALU.add))
                ln_dve(dve, "ln2", t, x2, x2)
                dve.wait_ge(s_moe, 14 * t + E_G)
                V.tensor_tensor(G[b][:], G[b][:], ps[7][:, 0:P], ALU.add).then_inc(s_moeD, 1)

            front(0, 0)
            front(1, 1)
            ssd(0, 0)
            front(2, 0)
            ssd(1, 1)
            moe(0, 0)
            front(3, 1)
            ssd(2, 0)
            moe(1, 1)
            with dve.Fori(2, NT // 2) as j:
                front(2 * j, 0)
                ssd(2 * j - 1, 1)
                moe(2 * j - 2, 0)
                front(2 * j + 1, 1)
                ssd(2 * j, 0)
                moe(2 * j - 1, 1)
            ssd(NT - 1, 1)
            moe(NT - 2, 0)
            moe(NT - 1, 1)

            dve.wait_ge(s_KIp, 1)
            V.tensor_tensor(KI[0][:], ps[0][:, 0:P], ident, ALU.add)
            V.tensor_tensor(KI[1][:], ps[1][:, 0:P], ident, ALU.add).then_inc(s_KI, 1)

            def prepare(u, b, piece):
                if piece == 0:
                    st = s_ln["ln3"][0]
                    st.begin(u)
                    dve.wait_ge(s_pre, 5 * u + Q_ATT)
                    if later(u, 2):
                        dve.wait_ge(s_ln["ln4"][0].sem, s_ln["ln4"][0].per * (u - 2) + 1)
                    st.inc(V.tensor_copy(x3[b][:], ps4[6]))
                    ln_dve(dve, "ln3", u, x3[b], x3[b])
                elif piece == 1:
                    dve.wait_ge(s_pre, 5 * u + Q_LG)
                    router_dve(dve, "rb", u, ps[6][:, 0:CH * NE].rearrange("p (c e) -> p c e", c=CH))

            def finish(u, b):
                st = s_ln["ln4"][0]
                st.begin(u)
                dve.wait_ge(s_fin, u + 1)
                if later(u, 1):
                    dve.wait_ge(s_out, 16 * u)
                st.inc(V.tensor_tensor(o_sb[:], ps4[7], x3[b][:], ALU.add))
                ln_dve(dve, "ln4", u, o_sb, o_sb)

            def experts(u, b, last=False, first=False):
                for q in range(NE * FT):
                    e, f = divmod(q, FT)
                    i = q % RH
                    src = h1[:, q % RH, :]
                    dve.wait_ge(s_relu, 32 * u + q + 1)
                    if q >= RH or later(u, 1):
                        dve.wait_ge(s_down, 32 * u + q + 1 - since(q))
                    V.tensor_copy(h1_hi[i], src).then_inc(s_hhi, 1)
                    dve.wait_ge(s_hhi, 32 * u + q + 1)
                    V.tensor_tensor(h1_lo[i], src, h1_hi[i].bitcast(F32), ALU.subtract
                                    ).then_inc(s_hlo, 1)
                    if f == 3 and e >= 1:
                        gate(u, e - 1)
                    if q == 4 and not first:
                        finish(u - 1, 1 - b)
                    if q in (9, 16) and not last:
                        prepare(u + 1, 1 - b, (9, 16).index(q))
                gate(u, NE - 1)

            def gate(u, e):
                dve.wait_ge(s_down, 32 * u + FT * (e + 1))
                dve.wait_ge(s_wbc, 8 * u + e + 1)
                if e >= 2 or later(u, 1):
                    dve.wait_ge(s_sum, 8 * u + e - 1)
                V.tensor_tensor(yw[:, e % 2, :], ps[3 + e % 2][:, :], wbc[:, e % 2, :], ALU.mult
                                ).then_inc(s_yw, 1)

            for piece in range(2):
                prepare(0, 0, piece)
            experts(0, 0, first=True)
            with dve.Fori(0, NT // 2 - 1) as v:
                experts(2 * v + 1, 1)
                experts(2 * v + 2, 0)
            experts(NT - 1, 1, last=True)
            finish(NT - 1, 1)

        @block.gpsimd
        def _(pool):
            L = nc.gpsimd
            pool.wait_ge(s_in0, 16 * 7)
            pool.wait_ge(s_prep, 1)
            pool.wait_ge(s_p0["act"], 6)

            def split(t, b):
                xt = xT_sb[:, bass.ds(t, 1), :].rearrange("p o q -> p (o q)")
                pool.wait_ge(s_xhi, t + 1)
                L.tensor_tensor(x_lo[b][:], xt, x_hi[b][:].bitcast(F32), ALU.subtract).then_inc(s_xlo, 1)

            def decays(t, b):
                if later(t, 2):
                    pool.wait_ge(s_exp, 2 * (t - 1))
                    pool.wait_ge(s_state.sem, s_state.per * (t - 1))
                apart(pool)
                L.tensor_copy(cur[b][:], cols[:, bass.ds(CH * t, CH), :, :]).then_inc(s_cur, 1)
                pool.wait_ge(s_cur, t + 1)
                for h in range(H):
                    if later(t, 1):
                        pool.wait_ge(s_ssd, 11 * (t - 1) + (S_ROW0, S_ROW1)[h])
                    L.tensor_tensor(dAU[:, h, :, :], tri.unsqueeze(1).to_broadcast([P, CH, P]),
                                    cur[b][:, :, h, K_DA:K_DA + 1].to_broadcast([P, CH, P]), ALU.mult
                                    ).then_inc(s_dAU, 1)

            def ssd(t, b):
                for h in range(H):
                    pool.wait_ge(s_exp, 2 * t + h + 1)
                    apart(pool)
                    L.affine_select(out=E[:, h, :, :], in_=E[:, h, :, :], compare_op=ALU.is_ge, fill=0.0,
                                    base=0, pattern=[[0, CH], [1, P]], channel_multiplier=-1
                                    ).then_inc(s_mask, 1)
                    pool.wait_ge(s_C0, 16 * (t + 1))
                    L.tensor_tensor(Cs[:, h, :], C0[b][:], Cs[:, h, :], ALU.mult).then_inc(s_Cs, 1)
                for h in range(H):
                    pool.wait_ge(s_yd, 2 * t + h + 1)
                    pool.wait_ge(s_z, 2 * t + h + 1)
                    L.tensor_tensor(yg[b][:, h, :], yd[b][:, h, :], z2[b][:, h, :], ALU.mult).then_inc(s_yg, 1)
                ln_pool(pool, "ln1", t)

            def parts(src, hi, lo, hisem, losem, n):
                apart(pool)
                L.tensor_copy(hi, src).then_inc(hisem, 1)
                pool.wait_ge(hisem, n)
                L.tensor_tensor(lo, src, hi.bitcast(F32), ALU.subtract).then_inc(losem, 1)

            def moe(t, b):
                pool.wait_ge(s_moeA, 7 * t + A_XT)
                if later(t, 1):
                    pool.wait_ge(s_moe, 14 * (t - 1) + E_H3)
                parts(x1T[:], x1T_hi[:], x1T_lo[:], s_x1hi, s_x1lo, t + 1)
                ln_pool(pool, "ln2", t)

            def weights(t, b):
                s_w.begin(t)
                pool.wait_ge(s_wraw, 32 * (t + 1))
                apart(pool)
                for k in range(2):
                    c = bass.ds(t * TILE, TILE)
                    s_w.inc(L.tensor_copy(w_hi[:, k, c], wraw[:, k, :]))
                    s_w.wait(pool)
                    s_w.inc(L.tensor_tensor(w_lo[:, k, c], wraw[:, k, :], w_hi[:, k, c].bitcast(F32),
                                            ALU.subtract))
                s_w.end()

            split(0, 0)
            split(1, 1)
            pool.wait_ge(s_in, 16 * 14)
            parts(Wd_sb, Wd_hi[:], Wd_lo[:], s_wd0, s_wd, 1)
            decays(0, 0)
            decays(1, 1)
            ssd(0, 0)
            weights(0, 0)
            weights(1, 1)
            split(2, 0)
            split(3, 1)
            ssd(1, 1)
            decays(2, 0)
            moe(0, 0)
            weights(2, 0)
            ssd(2, 0)
            decays(3, 1)
            moe(1, 1)
            weights(3, 1)
            with pool.Fori(2, NT // 2) as j:
                split(2 * j, 0)
                split(2 * j + 1, 1)
                ssd(2 * j - 1, 1)
                decays(2 * j, 0)
                moe(2 * j - 2, 0)
                weights(2 * j, 0)
                ssd(2 * j, 0)
                decays(2 * j + 1, 1)
                moe(2 * j - 1, 1)
                weights(2 * j + 1, 1)
            ssd(NT - 1, 1)
            moe(NT - 2, 0)
            moe(NT - 1, 1)

            def prepare(u, b, piece):
                if piece == 0:
                    if later(u, 1):
                        pool.wait_ge(s_pre, 5 * (u - 1) + Q_ATT)
                    else:
                        pool.wait_ge(s_moeA, 7 * NT)
                    apart(pool)
                    L.tensor_copy(x2T_cur[:], x2T[:, bass.ds(u, 1), :].rearrange("p o q -> p (o q)")
                                  ).then_inc(s_cur2, 1)
                elif piece == 1:
                    ln_pool(pool, "ln3", u)
                elif piece == 2:
                    pool.wait_ge(s_x3T, u + 1)
                    if later(u, 2):
                        pool.wait_ge(s_up, 32 * (u - 1))
                    parts(x3T, x3T_hi[b][:], x3T_lo[b][:], s_x3hi, s_x3lo, u + 1)

            def experts(u, b, last=False, first=False):
                for e in range(NE):
                    if e == 0 and not first:
                        ln_pool(pool, "ln4", u - 1)
                    if e < 2 and not last:
                        prepare(u + 1, 1 - b, e)
                    if e == 3 and not last:
                        prepare(u + 1, 1 - b, 2)
                    pool.wait_ge(s_yw, 8 * u + e + 1)
                    if e == 0:
                        pool.wait_ge(s_acc0, u + 1)
                    else:
                        pool.wait_ge(s_sum, 8 * u + e)
                    L.tensor_tensor(oT[b], oT[b], yw[:, e % 2, :], ALU.add).then_inc(s_sum, 1)

            for piece in range(3):
                prepare(0, 0, piece)
            experts(0, 0, first=True)
            with pool.Fori(0, NT // 2 - 1) as v:
                experts(2 * v + 1, 1)
                experts(2 * v + 2, 0)
            experts(NT - 1, 1, last=True)
            ln_pool(pool, "ln4", NT - 1)


def layouts(i):
    import numpy as np

    f = {k: np.asarray(v) for k, v in i.items()}

    def rows(v, n=P):
        return np.ascontiguousarray(np.broadcast_to(v[None, :], (n,) + v.shape))

    x = f["L0_attn_x"].reshape(NB, NT // NB, CH, P, P)
    Win = f["L0_attn_W_in"]
    conv_rows = (np.arange(256, 384), np.arange(0, 128), np.arange(128, 256))
    cw = f["L0_attn_conv_w"].reshape(384, TAPS)
    cb = f["L0_attn_conv_b"]
    const = np.zeros((P, C_COLS), np.float32)
    const[:, C_ID:C_ID + P] = np.eye(P)
    const[:, C_TRI:C_TRI + P] = np.triu(np.ones((P, P)))
    const[:, C_ONE:C_ONE + P] = 1
    const[:, C_REV:] = NE - np.arange(NE)
    sel = np.zeros((2 * NE, M0 * P + NE * P), np.float32)
    for e in range(NE):
        for r in (e, e + NE):
            sel[r, e * 64:(e + 1) * 64] = 1
            sel[r, M0 * P + e * P:M0 * P + (e + 1) * P] = 1
    d = {
        "x": x.transpose(3, 1, 0, 2, 4).reshape(P, NCHUNK, P),
        "xT": x.transpose(4, 1, 0, 2, 3).reshape(P, NT, TILE),
        "W_inT": Win.T,
        "conv_w": np.stack([cw[r] for r in conv_rows], 1),
        "conv_b": np.stack([cb[r] for r in conv_rows], 1),
        "A_log": rows(f["L0_attn_A_log"]),
        "dt_bias": rows(f["L0_attn_dt_bias"]),
        "D_skip": rows(f["L0_attn_D_skip"]),
        "W_outT": f["L0_attn_W_out"].T.reshape(H, P, P).transpose(1, 0, 2),
        "w_gate": f["L0_ffn_w_gate"],
        "WdT": f["L0_ffn_Wd"].transpose(1, 0, 2).reshape(P, M0 * P),
        "bd": f["L0_ffn_bd"].reshape(M0, P).T,
        "Wu": f["L0_ffn_Wu"].reshape(M0, P, P).transpose(1, 0, 2),
        "bu": np.concatenate([f["L0_ffn_bu"]] * 2, 0),
        "Wq": f["L1_attn_W_q"],
        "router_wT": f["L1_ffn_router_w"].T,
        "w1T": f["L1_ffn_w1"].transpose(2, 0, 1).reshape(P, NE * FT * P),
        "b1": f["L1_ffn_b1"].reshape(NE * FT, P).T,
        "w2T": f["L1_ffn_w2"].reshape(NE, P, FT, P).transpose(3, 0, 2, 1).reshape(P, NE * FT * P),
        "b2": np.concatenate([f["L1_ffn_b2"]] * 2, 0),
        "const": const,
        "sel": sel,
    }
    return {k: np.ascontiguousarray(v) for k, v in d.items()}


def kernel(**inputs):
    import numpy as np
    import concourse.bacc as bacc
    from concourse.bass_utils import run_bass_kernel_spmd

    data = layouts(inputs)
    nc = bacc.Bacc("TRN2", target_bir_lowering=False, num_devices=1)
    arrays, args = {}, {}
    for name, a in data.items():
        arrays[f"in_{name}"] = a
        args[name] = nc.dram_tensor(f"in_{name}", a.shape, mybir.dt.from_np(a.dtype), kind="ExternalInput").ap()
    args["out"] = nc.dram_tensor("out_x", (P, NCHUNK, P), F32, kind="ExternalOutput").ap()
    build_kernel(nc, **args)
    r = run_bass_kernel_spmd(nc, [arrays], core_ids=[0])
    o = np.asarray(r.results[0]["out_x"]).reshape(P, NT // NB, NB, CH, P)
    return np.ascontiguousarray(o.transpose(2, 1, 3, 0, 4)).reshape(NB, NT // NB * TILE, P)
```

```python
from contextlib import ExitStack

import concourse.bass as bass
from concourse import mybir

F32 = mybir.dt.float32
F32R = mybir.dt.float32r
ALU = mybir.AluOpType
ACT = mybir.ActivationFunctionType
AX = mybir.AxisListType

P = 128
TILE = 512
CH = TILE // P
NT = 8
NB = 2
NCHUNK = NT * CH
H = 2
N = 64
TAPS = 4
HIST = TAPS - 1
NE = 8
M0 = 4
FT = 4
EPS = 1e-5
SERIES = 9

C_ID, C_TRI, C_ONE, C_REV = 0, P, 2 * P, 3 * P
C_COLS = 3 * P + NE


class Steps:

    def __init__(self, sem, per):
        self.sem, self.per = sem, per

    def begin(self, t, k=0):
        self.base, self.k = t * self.per, k

    def inc(self, ins):
        ins.then_inc(self.sem, 1)
        self.k += 1

    def wait(self, eng, back=0):
        eng.wait_ge(self.sem, self.base + self.k - back)

    def then(self, eng, op, *args, **named):
        if self.k:
            self.wait(eng)
        self.inc(op(*args, **named))

    def end(self):
        assert self.k == self.per, (self.sem, self.k, self.per)


def weave(*parts):
    parts = list(parts)
    while parts:
        for p in list(parts):
            if next(p, parts) is parts:
                parts.remove(p)


def advance(part, n):
    for _ in range(n):
        next(part, None)


FRONT, SSD, MOE, TAIL = range(4)
ROUND = (
    ((SSD, 0), (FRONT, 0), (TAIL, 0), (MOE, 0)),
    ((SSD, 1), (FRONT, 1), (TAIL, 1), (MOE, 1)),
    ((SSD, 2), (FRONT, 2), (MOE, 2)),
    ((SSD, 3), (FRONT, 3), (MOE, 3)),
    ((SSD, 4), (FRONT, 4), (MOE, 4)),
    ((SSD, 5), (MOE, 5)),
    ((SSD, 6), (MOE, 6)),
    ((SSD, 7), (MOE, 7)),
)


def rounds(fori, do):
    for i in range(4):
        do(i, i % 2)
    with fori(2, NT // 2) as j:
        do(2 * j, 0)
        do(2 * j + 1, 1)
    for i in range(NT, NT + 3):
        do(i, i % 2)


def in_round(i, b, stages):
    for group in ROUND:
        calls = []
        for stage, k in group:
            t = i - stage
            if isinstance(i, int) and not 0 <= t < NT:
                continue
            if stages[stage] is not None:
                calls.append((stages[stage], t, (b + stage) % 2, k))
        yield calls


def later(t, n):
    return not isinstance(t, int) or t >= n


def build_kernel(nc, x, xT, W_inT, conv_w, conv_b, A_log, dt_bias, D_skip, W_outT, w_gate, WdT, bd,
                 Wu, bu, Wq, router_wT, w1T, b1, w2T, b2, const, sel, out):
    ctx = ExitStack()
    with ctx:
        def sb(name, shape, dt=F32):
            return ctx.enter_context(nc.sbuf_tensor(name, shape, dt))

        def bank(name):
            return ctx.enter_context(nc.psum_tensor(name, [P, 512], F32))

        def sem(name):
            return ctx.enter_context(nc.semaphore(name))

        x_sb = sb("x_sb", [P, CH, P])
        xT_sb = sb("xT_sb", [P, NT, TILE])
        const_sb = sb("const_sb", [P, C_COLS])
        convw_sb = sb("convw_sb", [P, 3, TAPS])
        convb_sb = sb("convb_sb", [P, 3])
        small_sb = sb("small_sb", [P, 3, H])
        Wout_sb = sb("Wout_sb", [P, H, P])
        wgate_sb = sb("wgate_sb", [P, NE])
        bd_sb = sb("bd_sb", [P, M0])
        Wu_sb = sb("Wu_sb", [P, M0, P])
        bu_sb = sb("bu_sb", [2 * NE, P])
        Wq_sb = sb("Wq_sb", [P, P])
        rw_sb = sb("rw_sb", [P, NE])
        b1_sb = sb("b1_sb", [P, NE * FT])
        b2_sb = sb("b2_sb", [2 * NE, P])
        wraw = sb("wraw", [P, 2, TILE])
        ident = const_sb[:, C_ID:C_ID + P]
        tri = const_sb[:, C_TRI:C_TRI + P]
        ones = const_sb[:, C_ONE:C_ONE + P]
        rev = const_sb[:, C_REV:C_REV + NE]

        Win_hi, Win_lo = sb("Win_hi", [P, 640], F32R), sb("Win_lo", [P, 640], F32R)
        Wd_hi, Wd_lo = sb("Wd_hi", [P, M0 * P], F32R), sb("Wd_lo", [P, M0 * P], F32R)
        w_hi = sb("w_hi", [P, 2, NE * FT * P], F32R)
        w_lo = sb("w_lo", [P, 2, NE * FT * P], F32R)
        sel_r = sb("sel_r", [2 * NE, M0 * P + NE * P], F32R)
        bu_r = sb("bu_r", [2 * NE, 2, P], F32R)
        b2_r = sb("b2_r", [2 * NE, 2, P], F32R)

        dtv = sb("dtv", [P, NCHUNK, H])
        dA = sb("dA", [P, NCHUNK, H])
        sp = [sb(f"sp{i}", [P, NCHUNK, H]) for i in range(5)]
        expA = sb("expA", [P, H])
        K_DT, K_DA, K_NCS, K_REST, K_TOT = range(5)
        cols = sb("cols", [P, NCHUNK, H, 5])

        x_hi = [sb(f"x_hi{b}", [P, TILE], F32R) for b in range(NB)]
        x_lo = [sb(f"x_lo{b}", [P, TILE], F32R) for b in range(NB)]
        raw = sb("raw", [P, 3, HIST + TILE])
        hist = [sb(f"hist{b}", [P, 3, HIST]) for b in range(NB)]
        acc = sb("acc", [P, 3, TILE])
        BC = [sb(f"BC{b}", [P, TILE]) for b in range(NB)]
        xs = [sb(f"xs{b}", [P, H, TILE]) for b in range(NB)]
        z2 = [sb(f"z2{b}", [P, H, TILE]) for b in range(NB)]
        C0 = [sb("C0", [N, TILE])] * NB
        cur = [sb(f"cur{b}", [P, CH, H, 5]) for b in range(NB)]
        dAU = sb("dAU", [P, H, CH, P])
        E = sb("E", [P, H, CH, P])
        Cs = sb("Cs", [N, H, TILE])
        xdt = sb("xdt", [P, H, CH, P])
        Bw = sb("Bw", [P, H, CH, N])
        M = E
        state = sb("state", [N, H, CH, P])
        carry = [sb(f"carry{b}", [N, H, P]) for b in range(NB)]
        yd = xs
        yg = z2
        x1 = [sb(f"x1{b}", [P, CH, P]) for b in range(NB)]
        x1T = sb("x1T", [P, TILE])
        x1T_hi, x1T_lo = sb("x1T_hi", [P, TILE], F32R), sb("x1T_lo", [P, TILE], F32R)
        h0 = sb("h0", [P, M0, TILE])
        flat_h0 = h0[:, :, :].rearrange("p m q -> p (m q)")
        Win_sb, Wd_sb = flat_h0[:, 0:642], flat_h0[:, 1024:1024 + M0 * P]
        sel0_sb = xdt[0:2 * NE, 0, :, :].rearrange("p c q -> p (c q)")
        sel1_sb = E[0:2 * NE, :, :, :].rearrange("p h c q -> p (h c q)")
        x2 = sb("x2", [P, CH, P])
        x2T = xT_sb
        G = [sb(f"G{b}", [P, P]) for b in range(NB)]
        stats = {k: (sb(f"bn{k}", [P, CH, 6]), sb(f"mv{k}", [P, CH, 2]), sb(f"rstd{k}", [P, CH]))
                 for k in ("ln1", "ln2", "ln3", "ln4")}
        half = sb("half", [P, CH])
        route = {k: [sb(f"{k}{n}", s) for n, s in
                     (("lg", [P, CH, NE]), ("m1", [P, CH]), ("m2", [P, CH]), ("key", [P, CH, NE]),
                      ("kmax", [P, CH]), ("oh1", [P, CH, NE]), ("oh2", [P, CH, NE]),
                      ("d", [P, CH]), ("e2", [P, CH]), ("g", [P, CH, NE]), ("sum", [P, CH]))]
                 for k in ("ra", "rb")}
        g16 = {k: sb(f"g16{k}", [P, CH, 2 * NE], F32R) for k in ("ra", "rb")}
        gT = sb("gT", [2 * NE, TILE], F32R)

        KI = [sb(f"KI{b}", [P, P]) for b in range(NB)]
        x2T_cur = x1T
        x3 = x1
        x3T = acc[:, 0, :]
        x3T_hi, x3T_lo = x_hi, x_lo
        w16T = [gT, sb("w16T1", [2 * NE, TILE], F32R)]
        RH = 3
        h1 = h0
        h1_hi = [x1T_hi[:, :], Win_hi[:, 0:TILE], Wd_hi[:, :]]
        h1_lo = [x1T_lo[:, :], Win_lo[:, 0:TILE], Wd_lo[:, :]]
        wbc = E[:, :, :, :].rearrange("p h c q -> p h (c q)")
        yw = xdt[:, :, :, :].rearrange("p h c q -> p h (c q)")
        oT = [dAU[:, h, :, :].rearrange("p c q -> p (c q)") for h in range(H)]
        o_sb = x2

        ps = [bank(f"ps{i}") for i in range(8)]
        ps4 = [p[:, :].rearrange("p (c q) -> p c q", c=CH) for p in ps]

        s_in0 = sem("s_in0")
        s_in = sem("s_in")
        s_wraw, s_x = sem("s_wraw"), sem("s_x")
        s_prep = sem("s_prep")
        s_wd0, s_wd = sem("s_wd0"), sem("s_wd")
        s_w = Steps(sem("s_w"), 4)
        s_p0 = {e: sem(f"s_p0_{e}") for e in ("pe", "act", "dve")}
        s_absv = sem("s_absv")
        s_p0chain = sem("s_p0chain")
        s_xhi, s_xlo = sem("s_xhi"), sem("s_xlo")
        s_cur, s_dAU = sem("s_cur"), sem("s_dAU")
        s_proj = sem("s_proj")
        s_hist, s_raw, s_zt = sem("s_hist"), sem("s_raw"), sem("s_zt")
        s_tap = Steps(sem("s_tap"), 12)
        s_th = sem("s_th")
        s_conv = sem("s_conv")
        s_z = sem("s_z")
        s_C0 = sem("s_C0")
        s_ssd = sem("s_ssd")
        S_TX0, S_ROW0, S_TX1, S_ROW1, S_TB, S_SC, S_INC0, S_INC1, S_Y0, S_Y1, S_OUT = range(1, 12)
        s_diff = Steps(sem("s_diff"), CH * H)
        s_exp, s_mask, s_Cs = sem("s_exp"), sem("s_mask"), sem("s_Cs")
        s_xdt, s_Bw, s_M = sem("s_xdt"), sem("s_Bw"), sem("s_M")
        s_state = Steps(sem("s_state"), 1 + CH * H)
        s_yd, s_yg = sem("s_yd"), sem("s_yg")
        s_ln = {k: (Steps(sem(f"s_{k}"), 1 + CH + (CH - 1) + CH), sem(f"s_{k}v"), sem(f"s_{k}r"))
                for k in ("ln1", "ln2", "ln3", "ln4")}
        s_moe = sem("s_moe")
        E_XT, E_LG, E_H0, E_H1, E_H2, E_H3, E_GT, E_B0, E_B1, E_B2, E_B3, E_OUT = range(1, 13)
        s_moeA = sem("s_moeA")
        A_XT, A_H0, A_H1, A_H2, A_H3, A_GT = range(1, 7)
        s_moeD = sem("s_moeD")
        D_LG, D_B0, D_B1, D_B2, D_B3 = range(1, 6)
        s_tail = sem("s_tail")
        s_x2T, s_G = sem("s_x2T"), sem("s_G")
        s_x1hi, s_x1lo = sem("s_x1hi"), sem("s_x1lo")
        s_rt = {"ra": Steps(sem("s_ra"), 19), "rb": Steps(sem("s_rb"), 23)}
        s_rexp = {k: sem(f"s_{k}e") for k in ("ra", "rb")}
        s_KI = sem("s_KI")
        s_KIp = sem("s_KIp")
        s_cur2 = sem("s_cur2")
        s_pre = sem("s_pre")
        Q_ATT, Q_XT, Q_LG, Q_GT, Q_B2 = range(1, 6)
        s_x3T, s_x3hi, s_x3lo, s_w16T, s_acc0 = (sem(n) for n in
                                                 ("s_x3T", "s_x3hi", "s_x3lo", "s_w16T", "s_acc0"))
        s_fin = sem("s_fin")
        s_up, s_relu, s_hhi, s_hlo, s_down = (sem(n) for n in
                                              ("s_up", "s_relu", "s_hhi", "s_hlo", "s_down"))
        s_wb, s_wbc, s_yw, s_sum = (sem(n) for n in ("s_wb", "s_wbc", "s_yw", "s_sum"))
        s_out = sem("s_out")
        s_apart = sem("s_apart")

        block = ctx.enter_context(nc.Block())

        PE_AT = (4, 13, 15, 26, 28)
        ACT_AT = {14: 1, 21: 2, 27: 3, 29: 4}
        DVE_LN4 = {2: 1, 3: 3, 4: 3, 5: 2, 7: 2, 8: 2}
        DVE_LN3 = {6: 1, 7: 2, 8: 2, 9: 2, 10: 2, 12: 4}
        DVE_RT = {17: 4, 18: 4, 19: 4, 20: 2, 23: 3, 24: 3, 25: 3}

        def apart(eng):
            eng.sem_inc(s_apart, 1)

        def since(q):
            return RH if q >= RH else (2, 1, 3)[q]

        def mm3(pe, dst, a_hi, a_lo, b_hi, b_lo, start=True, stop=True):
            pe.matmul(dst, a_hi, b_hi, start=start, stop=False)
            pe.matmul(dst, a_hi, b_lo, start=False, stop=False)
            return pe.matmul(dst, a_lo, b_hi, start=False, stop=stop)

        @block.sync
        def _(sp_):
            sp_.dma_start(const_sb[:], const).then_inc(s_in0, 16)
            sp_.dma_start(small_sb[:, 0, :], A_log).then_inc(s_in0, 16)
            sp_.dma_start(small_sb[:, 1, :], dt_bias).then_inc(s_in0, 16)
            sp_.dma_start(small_sb[:, 2, :], D_skip).then_inc(s_in0, 16)
            sp_.dma_start(Win_sb, W_inT).then_inc(s_in0, 16)
            sp_.dma_start(xT_sb[:, 0:4, :], xT[:, 0:4, :]).then_inc(s_in0, 16)
            sp_.dma_start(xT_sb[:, 4:8, :], xT[:, 4:8, :]).then_inc(s_in0, 16)
            for dst, src in ((convw_sb, conv_w), (convb_sb, conv_b), (Wout_sb, W_outT),
                             (wgate_sb, w_gate), (bd_sb, bd), (Wu_sb, Wu),
                             (bu_sb, bu), (Wq_sb, Wq), (rw_sb, router_wT), (b1_sb, b1),
                             (b2_sb, b2)):
                sp_.dma_start(dst[:], src).then_inc(s_in, 16)
            sp_.dma_start(Wd_sb, WdT).then_inc(s_in, 16)
            sp_.dma_start(sel0_sb, sel[:, 0:M0 * P]).then_inc(s_in, 16)
            sp_.dma_start(sel1_sb, sel[:, M0 * P:]).then_inc(s_in, 16)

            def tile(t, b):
                if later(t, 1):
                    sp_.wait_ge(s_w.sem, 4 * t)
                sp_.dma_start(wraw[:, 0, :], w1T[:, bass.ds(t * TILE, TILE)]).then_inc(s_wraw, 16)
                sp_.dma_start(wraw[:, 1, :], w2T[:, bass.ds(t * TILE, TILE)]).then_inc(s_wraw, 16)
                sp_.wait_ge(s_conv, 3 * t + 1)
                if later(t, 1):
                    sp_.wait_ge(s_ssd, 11 * (t - 1) + S_SC)
                    sp_.wait_ge(s_Cs, 2 * t)
                sp_.dma_start(C0[b][:], BC[b][N:2 * N, :]).then_inc(s_C0, 16)
                if later(t, 1):
                    sp_.wait_ge(s_ln["ln1"][0].sem, s_ln["ln1"][0].per * (t - 1) + 1)
                sp_.dma_start(x_sb[:], x[:, bass.ds(CH * t, CH), :]).then_inc(s_x, 16)

            for t in range(NT):
                tile(t, t % NB)

            def store(u):
                sp_.wait_ge(s_ln["ln4"][0].sem, s_ln["ln4"][0].per * (u + 1))
                sp_.dma_start(out[:, bass.ds(CH * u, CH), :], o_sb[:]).then_inc(s_out, 16)

            for u in range(NT):
                store(u)
            sp_.wait_ge(s_out, 16 * NT)

        LN_RES = 1

        def ln_stats(dve, k, t, src):
            st = s_ln[k][0]
            bn, mv, _ = stats[k]
            for c in range(CH):
                if c == 0:
                    st.wait(dve)
                st.inc(nc.vector.bn_stats(bn[:, c, :], src[:, c, :]))
                yield
            for c in range(CH):
                st.wait(dve, back=CH - 1)
                apart(dve)
                ins = nc.vector.bn_aggr(mv[:, c, :], bn[:, c, :])
                if c == CH - 1:
                    ins.then_inc(s_ln[k][1], 1)
                else:
                    st.inc(ins)
                yield

        def ln_norm(dve, k, t, src, dst):
            st, rsem = s_ln[k][0], s_ln[k][2]
            _, mv, rstd = stats[k]
            st.begin(t, 1 + CH + CH - 1)
            dve.wait_ge(rsem, 2 * (t + 1))
            for c in range(CH):
                st.inc(nc.vector.tensor_scalar(dst[:, c, :], src[:, c, :], mv[:, c, 0:1],
                                               rstd[:, c:c + 1], ALU.subtract, ALU.mult))
                yield
            st.end()

        def ln_pool(pool, k, t):
            bn, mv, rstd = stats[k]
            pool.wait_ge(s_ln[k][1], t + 1)
            apart(pool)
            nc.gpsimd.tensor_scalar(rstd[:], mv[:, :, 1], EPS, None, ALU.add).then_inc(s_ln[k][2], 1)
            pool.wait_ge(s_ln[k][2], 2 * t + 1)
            nc.gpsimd.tensor_tensor(rstd[:], rstd[:], half[:], ALU.pow).then_inc(s_ln[k][2], 1)

        def over_e(v):
            return v[:, :].unsqueeze(2).to_broadcast([P, CH, NE])

        def over_c(v):
            return v.unsqueeze(1).to_broadcast([P, CH, NE])

        def router_dve(dve, k, t, logits, emptied=None):
            st, e = s_rt[k], s_rexp[k]
            lg, m1, m2, key, kmax, oh1, oh2, d, e2, g, tot = route[k]
            V = nc.vector
            st.begin(t)
            ins = V.tensor_copy(lg[:], logits)
            if emptied is not None:
                ins.then_inc(emptied, 1)
                dve.wait_ge(emptied, 5 * t + D_LG)
            else:
                st.inc(ins)
                yield
            st.then(dve, V.tensor_reduce, m1[:], lg[:], AX.X, ALU.max)
            yield

            def first_of(src, m, oh):
                st.then(dve, V.tensor_tensor, key[:], src[:], over_e(m), ALU.is_equal)
                yield
                st.then(dve, V.tensor_tensor, key[:], key[:], over_c(rev), ALU.mult)
                yield
                st.then(dve, V.tensor_reduce, kmax[:], key[:], AX.X, ALU.max)
                yield
                st.then(dve, V.tensor_tensor, oh[:], key[:], over_e(kmax), ALU.is_equal)
                yield

            yield from first_of(lg, m1, oh1)
            st.then(dve, V.scalar_tensor_tensor, out=g[:], in0=oh1[:], scalar=-3.0e38, in1=lg[:],
                    op0=ALU.mult, op1=ALU.add)
            yield
            st.then(dve, V.tensor_reduce, m2[:], g[:], AX.X, ALU.max)
            yield
            yield from first_of(g, m2, oh2)
            st.then(dve, V.tensor_tensor, d[:], m2[:], m1[:], ALU.subtract)
            yield
            if k == "ra":
                dve.wait_ge(e, t + 1)
                st.then(dve, V.tensor_scalar, tot[:], e2[:], 1.0, 2.0, ALU.add, ALU.mult)
                yield
            else:
                st.then(dve, V.tensor_tensor, g[:], lg[:], over_e(m1), ALU.subtract)
                yield
                dve.wait_ge(e, 2 * (t + 1))
                st.then(dve, V.tensor_reduce, tot[:], g[:], AX.X, ALU.add)
                yield
                st.then(dve, V.scalar_tensor_tensor, out=tot[:], in0=tot[:], scalar=1e-9, in1=e2[:],
                        op0=ALU.mult, op1=ALU.add)
                yield
                st.then(dve, V.tensor_scalar, tot[:], tot[:], 1.0, None, ALU.add)
                yield
            st.then(dve, V.reciprocal, tot[:], tot[:])
            yield
            st.then(dve, V.tensor_tensor, oh2[:], oh2[:], over_e(e2), ALU.mult)
            yield
            st.then(dve, V.tensor_tensor, g[:], oh1[:], oh2[:], ALU.add)
            yield
            st.then(dve, V.tensor_tensor, g[:], g[:], over_e(tot), ALU.mult)
            yield
            st.then(dve, V.tensor_copy, g16[k][:, :, 0:NE], g[:])
            yield
            st.then(dve, V.tensor_tensor, g16[k][:, :, NE:2 * NE], g[:],
                    g16[k][:, :, 0:NE].bitcast(F32), ALU.subtract)
            yield
            st.end()

        def router_act(act, k, t, d_at, g_at=None):
            e, d, e2, g = s_rexp[k], route[k][7], route[k][8], route[k][9]
            act.wait_ge(s_rt[k].sem, s_rt[k].per * t + d_at)
            nc.scalar.activation(e2[:], d[:], ACT.Exp).then_inc(e, 1)
            if g_at is not None:
                act.wait_ge(s_rt[k].sem, s_rt[k].per * t + g_at)
                nc.scalar.activation(g[:], g[:], ACT.Exp).then_inc(e, 1)

        @block.tensor
        def _(pe):
            pe.wait_ge(s_in0, 16 * 7)
            for n in range(NCHUNK):
                mm = pe.matmul(ps[7][:, n * H:(n + 1) * H], xT_sb[:, n // CH, (n % CH) * P:(n % CH + 1) * P],
                               Win_sb[:, 640:642], start=True, stop=True)
            mm.then_inc(s_p0["pe"], 1)
            pe.wait_ge(s_p0["dve"], 1)
            flat = dA[:, :, :].rearrange("p n h -> p (n h)")
            pe.matmul(ps[6][:, 0:H * NCHUNK], tri, flat, start=True, stop=True)
            pe.matmul(ps[5][:, 0:H * NCHUNK], ones, flat, start=True, stop=True).then_inc(s_p0["pe"], 1)
            pe.wait_ge(s_p0["act"], 4)
            pe.wait_ge(s_prep, 1)

            def front(t, b, i):
                w = (4, 2, 3, 0, 1)[i]
                if i == 0:
                    pe.wait_ge(s_xhi, t + 1)
                    pe.wait_ge(s_xlo, t + 1)
                if i >= 2:
                    pe.wait_ge(s_raw, 3 * t + i - 1)
                elif later(t, 1):
                    pe.wait_ge(s_z, 2 * t - 1 + i)
                c = slice(w * P, (w + 1) * P)
                mm3(pe, ps[(b + i) % 2][:, :], Win_hi[:, c], Win_lo[:, c], x_hi[b][:], x_lo[b][:]
                    ).then_inc(s_proj, 1)

            def ssd(t, b, k):
                if k < H:
                    h = k
                    pe.wait_ge(s_conv, 3 * t + 2 + h)
                    if h == 1:
                        pe.wait_ge(s_xdt, 2 * t + h)
                    elif later(t, 1):
                        pe.wait_ge(s_ln["ln1"][0].sem, s_ln["ln1"][0].per * (t - 1) + LN_RES)
                    for c in range(CH):
                        mm = pe.transpose(ps4[3][:, c, :], xs[b][:, h, c * P:(c + 1) * P], ident)
                    mm.then_inc(s_ssd, 1)
                    pe.wait_ge(s_dAU, 2 * t + h + 1)
                    if h == 1:
                        pe.wait_ge(s_exp, 2 * t + 1)
                    elif later(t, 1):
                        pe.wait_ge(s_state.sem, s_state.per * t)
                    pe.matmul(ps[2][:, :], ones, dAU[:, h, :, :], start=True, stop=True
                              ).then_inc(s_ssd, 1)
                elif k == 2:
                    pe.wait_ge(s_xdt, 2 * t + 2)
                    apart(pe)
                    for c in range(CH):
                        mm = pe.transpose(ps4[3][:, c, 0:N], BC[b][0:N, c * P:(c + 1) * P],
                                          ident[0:N, 0:N])
                    mm.then_inc(s_ssd, 1)
                    pe.wait_ge(s_C0, 16 * (t + 1))
                    if later(t, 1):
                        pe.wait_ge(s_M, 2 * t)
                    for c in range(CH):
                        q = slice(c * P, (c + 1) * P)
                        mm = pe.matmul(ps4[4][:, c, :], BC[b][0:N, q], C0[b][:, q], start=True, stop=True)
                    mm.then_inc(s_ssd, 1)
                elif k < 5:
                    h = k - 3
                    pe.wait_ge(s_Bw, 2 * t + h + 1)
                    if h == 0:
                        pe.wait_ge(s_exp, 2 * t + 2)
                    else:
                        pe.wait_ge(s_state.sem, s_state.per * t + 1 + CH)
                    for c in range(CH):
                        mm = pe.matmul(ps4[2][0:N, c, :], Bw[:, h, c, :], xdt[:, h, c, :],
                                       start=True, stop=True)
                    mm.then_inc(s_ssd, 1)
                elif k < 7:
                    h = k - 5
                    pe.wait_ge(s_M, 2 * t + h + 1)
                    pe.wait_ge(s_Cs, 2 * t + h + 1)
                    pe.wait_ge(s_state.sem, s_state.per * t + 1 + CH * (h + 1))
                    if h == 1:
                        pe.wait_ge(s_yd, 2 * t + 1)
                    elif later(t, 1):
                        pe.wait_ge(s_yd, 2 * t)
                    for c in range(CH):
                        pe.matmul(ps4[5][:, c, :], xdt[:, h, c, :], M[:, h, c, :], start=True, stop=False)
                        mm = pe.matmul(ps4[5][:, c, :], state[:, h, c, :],
                                       Cs[:, h, c * P:(c + 1) * P], start=False, stop=True)
                    mm.then_inc(s_ssd, 1)
                else:
                    pe.wait_ge(s_yg, 2 * t + 2)
                    for c in range(CH):
                        for h in range(H):
                            mm = pe.matmul(ps4[3][:, c, :], yg[b][:, h, c * P:(c + 1) * P],
                                           Wout_sb[:, h, :], start=h == 0, stop=h == 1)
                    mm.then_inc(s_ssd, 1)

            A, B, A4, B4 = ps[6], ps[7], ps4[6], ps4[7]

            def moe(t, b, k):
                if k == 0:
                    pe.wait_ge(s_ln["ln1"][0].sem, s_ln["ln1"][0].per * (t + 1))
                    if later(t, 1):
                        pe.wait_ge(s_moeD, 5 * t)
                    for c in range(CH):
                        mm = pe.transpose(A4[:, c, :], x1[b][:, c, :], ident)
                    mm.then_inc(s_moe, 1)
                elif k == 1:
                    pe.wait_ge(s_moeA, 6 * t + A_XT)
                    if later(t, 1):
                        pe.wait_ge(s_G, t)
                    for c in range(CH):
                        mm = pe.matmul(B[:, c * NE:(c + 1) * NE], x1T[:, c * P:(c + 1) * P], wgate_sb[:],
                                       start=True, stop=True)
                    mm.then_inc(s_moe, 1)
                elif k < 4:
                    for m in (0, 1) if k == 2 else (2, 3):
                        if m == 0:
                            pe.wait_ge(s_x1lo, t + 1)
                            if later(t, 1):
                                pe.wait_ge(s_x2T, t)
                            else:
                                pe.wait_ge(s_wd, 1)
                        elif m == 1:
                            pe.wait_ge(s_moeD, 5 * t + D_LG)
                        else:
                            pe.wait_ge(s_moeA, 6 * t + A_H0 + m - 2)
                        r = slice(m * P, (m + 1) * P)
                        mm3(pe, (A if m % 2 == 0 else B)[:, :], Wd_hi[:, r], Wd_lo[:, r], x1T_hi[:],
                            x1T_lo[:]).then_inc(s_moe, 1)
                elif k == 4:
                    pe.wait_ge(s_rt["ra"].sem, s_rt["ra"].per * (t + 1))
                    pe.wait_ge(s_moeA, 6 * t + A_H2)
                    for c in range(CH):
                        mm = pe.transpose(A4[0:2 * NE, c, :], g16["ra"][:, c, :].bitcast(F32), ident)
                    mm.then_inc(s_moe, 1)
                elif k < 7:
                    for m in (0, 1) if k == 5 else (2, 3):
                        if m == 0:
                            pe.wait_ge(s_moeA, 6 * t + A_GT)
                        if m > 1:
                            pe.wait_ge(s_moeD, 5 * t + D_B0 + m - 2)
                        pe.matmul((B if m % 2 == 0 else A)[:, :], sel_r[:, m * P:(m + 1) * P], gT[:],
                                  start=True, stop=True).then_inc(s_moe, 1)
                else:
                    pe.wait_ge(s_moeD, 5 * t + D_B3)
                    for c in range(CH):
                        q = slice(c * P, (c + 1) * P)
                        for m in range(M0):
                            pe.matmul(B4[:, c, :], h0[:, m, q], Wu_sb[:, m, :], start=m == 0, stop=False)
                        pe.matmul(B4[:, c, :], gT[:, q], bu_r[:, 0, :], start=False, stop=False)
                        mm = pe.matmul(B4[:, c, :], gT[:, q], bu_r[:, 1, :], start=False, stop=True)
                    mm.then_inc(s_moe, 1)

            def tail(t, b, k):
                if k == 1:
                    pe.wait_ge(s_ln["ln2"][0].sem, s_ln["ln2"][0].per * (t + 1))
                    if isinstance(t, int) and t == NT - 1:
                        pe.wait_ge(s_moeD, 5 * NT)
                    else:
                        pe.wait_ge(s_moeA, 6 * (t + 1) + A_XT)
                    for c in range(CH):
                        mm = pe.transpose(A4[:, c, :], x2[:, c, :], ident)
                    mm.then_inc(s_tail, 1)
                    for c in range(CH):
                        mm = pe.matmul(B[:, 0:P], x2[:, c, :], x2[:, c, :], start=c == 0,
                                       stop=c == CH - 1)
                    mm.then_inc(s_tail, 1)

            def round_(i, b):
                for calls in in_round(i, b, (front, ssd, moe, tail)):
                    for f, *a in calls:
                        f(*a)

            rounds(pe.Fori, round_)

            pe.wait_ge(s_G, NT)
            for b in range(NB):
                mm = pe.matmul(ps[b][:, 0:P], Wq_sb[:], G[b][:], start=True, stop=True)
            mm.then_inc(s_KIp, 1)
            pe.wait_ge(s_KI, 1)

            def prepare(u, b, piece):
                if piece == 0:
                    pe.wait_ge(s_cur2, u + 1)
                    if later(u, 1):
                        pe.wait_ge(s_acc0, u)
                    for c in range(CH):
                        mm = pe.matmul(A4[:, c, :], x2T_cur[:, c * P:(c + 1) * P], KI[b][:], start=True,
                                       stop=True)
                elif piece == 1:
                    pe.wait_ge(s_ln["ln3"][0].sem, s_ln["ln3"][0].per * (u + 1))
                    if later(u, 2):
                        pe.wait_ge(s_ln["ln4"][0].sem, s_ln["ln4"][0].per * (u - 2) + LN_RES)
                    for c in range(CH):
                        mm = pe.transpose(B4[:, c, :], x3[b][:, c, :], ident)
                elif piece == 2:
                    pe.wait_ge(s_x3T, u + 1)
                    for c in range(CH):
                        mm = pe.matmul(A[:, c * NE:(c + 1) * NE], x3T[:, c * P:(c + 1) * P], rw_sb[:],
                                       start=True, stop=True)
                elif piece == 3:
                    pe.wait_ge(s_rt["rb"].sem, s_rt["rb"].per * (u + 1))
                    for c in range(CH):
                        mm = pe.transpose(B4[0:2 * NE, c, :], g16["rb"][:, c, :].bitcast(F32), ident)
                else:
                    pe.wait_ge(s_w16T, u + 1)
                    pe.matmul(A[:, :], b2_r[:, 0, :], w16T[b][:], start=True, stop=False)
                    mm = pe.matmul(A[:, :], b2_r[:, 1, :], w16T[b][:], start=False, stop=True)
                mm.then_inc(s_pre, 1)

            def finish(u, b):
                pe.wait_ge(s_sum, 8 * (u + 1))
                for c in range(CH):
                    mm = pe.transpose(ps4[7][:, c, :], oT[b][:, c * P:(c + 1) * P], ident)
                mm.then_inc(s_fin, 1)

            LAG = 2

            def experts(u, b, last=False, first=False):
                def up(q):
                    e, f = divmod(q, FT)
                    if q >= RH or later(u, 1):
                        pe.wait_ge(s_hhi, 32 * u + q + 1 - since(q))
                    r = slice(q * P, (q + 1) * P)
                    mm3(pe, ps[q % RH][:, :], w_hi[:, 0, r], w_lo[:, 0, r],
                        x3T_hi[b][:], x3T_lo[b][:]).then_inc(s_up, 1)
                    if f == 0:
                        if e > 0 or later(u, 1):
                            pe.wait_ge(s_wbc, 8 * u + e)
                        pe.matmul(ps[5][:, :], sel_r[:, M0 * P + e * P:M0 * P + (e + 1) * P], w16T[b][:],
                                  start=True, stop=True).then_inc(s_wb, 1)

                def down(q):
                    e, f = divmod(q, FT)
                    pe.wait_ge(s_hlo, 32 * u + q + 1)
                    if f == 0 and (e >= 2 or later(u, 1)):
                        pe.wait_ge(s_yw, 8 * u + e - 1)
                    r = slice(q * P, (q + 1) * P)
                    i = q % RH
                    mm = mm3(pe, ps[3 + e % 2][:, :], w_hi[:, 1, r], w_lo[:, 1, r], h1_hi[i],
                             h1_lo[i], start=f == 0, stop=f == FT - 1)
                    mm.then_inc(s_down, 1)

                pe.wait_ge(s_x3lo, u + 1)
                pe.wait_ge(s_acc0, u + 1)
                for q in range(LAG):
                    up(q)
                for q in range(NE * FT):
                    if q + LAG < NE * FT:
                        up(q + LAG)
                    down(q)
                    if q == 1 and not first:
                        finish(u - 1, 1 - b)
                    if q in PE_AT and not last:
                        prepare(u + 1, 1 - b, PE_AT.index(q))

            for piece in range(5):
                prepare(0, 0, piece)
            pe.wait_ge(s_w.sem, 4 * NT)
            experts(0, 0, first=True)
            with pe.Fori(0, NT // 2 - 1) as v:
                experts(2 * v + 1, 1)
                experts(2 * v + 2, 0)
            experts(NT - 1, 1, last=True)
            finish(NT - 1, 1)

        @block.scalar
        def _(act):
            S = nc.scalar
            act.wait_ge(s_in0, 16 * 7)
            S.activation(expA[:], small_sb[:, 0, :], ACT.Exp).then_inc(s_p0["act"], 1)
            act.wait_ge(s_absv, 1)
            S.activation(sp[1][:], sp[1][:], ACT.Exp, scale=-1.0).then_inc(s_p0["act"], 1)
            act.wait_ge(s_p0["pe"], 2)
            ps6v = ps[6][:, 0:H * NCHUNK].rearrange("p (n h) -> p n h", h=H)
            ps5v = ps[5][:, 0:H * NCHUNK].rearrange("p (n h) -> p n h", h=H)
            S.activation(cols[:, :, :, K_NCS], ps6v, ACT.Copy, scale=-1.0).then_inc(s_p0["act"], 1)
            S.activation(cols[:, :, :, K_TOT], ps5v, ACT.Copy).then_inc(s_p0["act"], 1)
            act.wait_ge(s_p0["dve"], 2)
            S.activation(cols[:, :, :, K_REST], cols[:, :, :, K_REST], ACT.Exp).then_inc(s_p0["act"], 1)
            S.activation(cols[:, :, :, K_TOT], cols[:, :, :, K_TOT], ACT.Exp).then_inc(s_p0["act"], 1)

            def split(t, b):
                if later(t, 2):
                    act.wait_ge(s_proj, 5 * (t - 1))
                S.activation(x_hi[b][:], xT_sb[:, bass.ds(t, 1), :].rearrange("p o q -> p (o q)"),
                             ACT.Copy).then_inc(s_xhi, 1)

            def front(t, b, k):
                if k < 3:
                    act.wait_ge(s_proj, 5 * t + k + 1)
                    S.activation(raw[:, k, HIST:], ps[(b + k) % 2][:, :], ACT.Copy).then_inc(s_raw, 1)
                else:
                    act.wait_ge(s_proj, 5 * t + k + 1)
                    if later(t, 2):
                        act.wait_ge(s_ssd, 11 * (t - 2) + S_OUT)
                    S.activation(z2[b][:, k - 3, :], ps[(b + k) % 2][:, :], ACT.Tanh, scale=0.5
                                 ).then_inc(s_zt, 1)
                if k == 2:
                    act.wait_ge(s_raw, 3 * t + 3)
                    act.wait_ge(s_hist, 2 * t + 1)
                    S.activation(hist[b][:, :, :], raw[:, :, TILE:TILE + HIST], ACT.Copy
                                 ).then_inc(s_hist, 1)
                if 1 <= k < 4:
                    i = k - 1
                    act.wait_ge(s_tap.sem, 12 * t + 4 * (i + 1))
                    if later(t, 2):
                        act.wait_ge(s_ssd, 11 * (t - 2) + S_SC)
                        act.wait_ge(s_C0, 16 * (t - 1))
                        act.wait_ge(s_yg, 2 * (t - 1))
                    S.activation(BC[b][:, :] if i == 0 else xs[b][:, i - 1, :], acc[:, i, :], ACT.Tanh
                                 ).then_inc(s_th, 1)

            def ssd(t, b, k):
                if k < H:
                    act.wait_ge(s_diff.sem, 8 * t + 4 * k + 4)
                    S.activation(Cs[:, k, :], ps[2][0:N, :], ACT.Exp)
                    S.activation(E[:, k, :, :], E[:, k, :, :], ACT.Exp).then_inc(s_exp, 1)

            A, B = ps[6], ps[7]

            def moe(t, b, k):
                if k == 0:
                    act.wait_ge(s_moe, 12 * t + E_XT)
                    if later(t, 1):
                        act.wait_ge(s_moe, 12 * (t - 1) + E_H3)
                        act.wait_ge(s_x1lo, t)
                    S.activation(x1T[:], A[:, :], ACT.Copy).then_inc(s_moeA, 1)
                elif k in (2, 3):
                    for m in (0, 1) if k == 2 else (2, 3):
                        act.wait_ge(s_moe, 12 * t + E_H0 + m)
                        if m == 0 and later(t, 1):
                            act.wait_ge(s_moe, 12 * (t - 1) + E_OUT)
                        S.activation(h0[:, m, :], (A if m % 2 == 0 else B)[:, :], ACT.Relu,
                                     bias=bd_sb[:, m:m + 1]).then_inc(s_moeA, 1)
                    if k == 3:
                        router_act(act, "ra", t, 12)
                elif k == 4:
                    act.wait_ge(s_moe, 12 * t + E_GT)
                    S.activation(gT[:], A[0:2 * NE, :], ACT.Copy).then_inc(s_moeA, 1)

            def tail(t, b, k):
                if k == 1:
                    act.wait_ge(s_tail, 2 * t + 1)
                    S.activation(x2T[:, bass.ds(t, 1), :].rearrange("p o q -> p (o q)"), A[:, :],
                                 ACT.Copy).then_inc(s_x2T, 1)

            def history(t, b):
                if later(t, 1):
                    act.wait_ge(s_tap.sem, 12 * t)
                S.activation(raw[:, :, 0:HIST], hist[b][:, :, :], ACT.Copy).then_inc(s_hist, 1)

            act.wait_ge(s_in, 16 * 14)
            act.wait_ge(s_prep, 1)

            def round_(i, b):
                if not isinstance(i, int) or i < NT:
                    split(i, b)
                    history(i, b)
                for calls in in_round(i, b, (front, ssd, moe, tail)):
                    for f, *a in sorted(calls, key=lambda call: call[0] is not front):
                        f(*a)

            rounds(act.Fori, round_)

            def prepare(u, b, piece):
                A, B = ps[6], ps[7]
                if piece == 1:
                    act.wait_ge(s_pre, 5 * u + Q_XT)
                    if later(u, 1):
                        act.wait_ge(s_x3lo, u)
                    S.activation(x3T, B[:, :], ACT.Copy).then_inc(s_x3T, 1)
                elif piece == 2:
                    router_act(act, "rb", u, 13, 14)
                elif piece == 3:
                    act.wait_ge(s_pre, 5 * u + Q_GT)
                    S.activation(w16T[b][:], B[0:2 * NE, :], ACT.Copy).then_inc(s_w16T, 1)
                elif piece == 4:
                    act.wait_ge(s_pre, 5 * u + Q_B2)
                    if later(u, 2):
                        act.wait_ge(s_fin, u - 1)
                    S.activation(oT[b], A[:, :], ACT.Copy).then_inc(s_acc0, 1)

            def experts(u, b, last=False, first=False):
                for q in range(NE * FT):
                    e, f = divmod(q, FT)
                    bank, old = ps[q % RH], 32 * u + q + 1 - since(q)
                    act.wait_ge(s_up, 32 * u + q + 1)
                    if q >= RH or later(u, 1):
                        act.wait_ge(s_hlo, old)
                    S.activation(h1[:, q % RH, :], bank[:, :], ACT.Relu, bias=b1_sb[:, q:q + 1]
                                 ).then_inc(s_relu, 1)
                    if q >= RH or later(u, 1):
                        act.wait_ge(s_down, old)
                    S.activation(h1_hi[q % RH], bank[:, :], ACT.Relu, bias=b1_sb[:, q:q + 1]
                                 ).then_inc(s_hhi, 1)
                    if q in ACT_AT and not last:
                        prepare(u + 1, 1 - b, ACT_AT[q])

            for piece in range(1, 5):
                prepare(0, 0, piece)
            experts(0, 0, first=True)
            with act.Fori(0, NT // 2 - 1) as v:
                experts(2 * v + 1, 1)
                experts(2 * v + 2, 0)
            experts(NT - 1, 1, last=True)

        @block.vector
        def _(dve):
            V = nc.vector
            p0 = Steps(s_p0chain, 0)
            p0.begin(0)

            def do(ins):
                p0.inc(ins)
                p0.wait(dve)

            for b in range(NB):
                V.memset(hist[b][:], 0.0)
                V.memset(carry[b][:], 0.0)
                V.memset(G[b][:], 0.0)
            v_, u_, s_, s2, q_ = sp
            dve.wait_ge(s_in0, 16 * 7)
            dve.wait_ge(s_p0["pe"], 1)
            raw_dt = ps[7][:, 0:H * NCHUNK].rearrange("p (n h) -> p n h", h=H)
            do(V.tensor_tensor(v_[:], raw_dt, small_sb[:, 1:2, :].to_broadcast([P, NCHUNK, H]), ALU.add))
            do(V.tensor_scalar(s2[:], v_[:], -1.0, None, ALU.mult))
            V.tensor_tensor(u_[:], s2[:], v_[:], ALU.max).then_inc(s_absv, 1)
            dve.wait_ge(s_p0["act"], 2)
            do(V.tensor_scalar(s2[:], u_[:], 2.0, None, ALU.add))
            do(V.reciprocal(s_[:], s2[:]))
            do(V.tensor_tensor(s_[:], s_[:], u_[:], ALU.mult))
            do(V.tensor_tensor(s2[:], s_[:], s_[:], ALU.mult))
            do(V.tensor_scalar(q_[:], s2[:], 1.0 / (2 * SERIES - 1), None, ALU.mult))
            for k in range(SERIES - 2, 0, -1):
                do(V.scalar_tensor_tensor(out=q_[:], in0=q_[:], scalar=1.0 / (2 * k + 1), in1=s2[:],
                                          op0=ALU.add, op1=ALU.mult))
            do(V.tensor_scalar(q_[:], q_[:], 1.0, 2.0, ALU.add, ALU.mult))
            do(V.tensor_tensor(q_[:], q_[:], s_[:], ALU.mult))
            do(V.scalar_tensor_tensor(out=dtv[:], in0=v_[:], scalar=0.0, in1=q_[:], op0=ALU.max,
                                      op1=ALU.add))
            do(V.scalar_tensor_tensor(out=dA[:], in0=dtv[:], scalar=-1.0,
                                      in1=expA[:, :].unsqueeze(1).to_broadcast([P, NCHUNK, H]),
                                      op0=ALU.mult, op1=ALU.mult))
            V.tensor_copy(cols[:, :, :, K_DT], dtv[:])
            V.tensor_copy(cols[:, :, :, K_DA], dA[:]).then_inc(s_p0["dve"], 1)

            do(V.tensor_copy(Win_hi[:], Win_sb[:, 0:640]))
            do(V.tensor_tensor(Win_lo[:], Win_sb[:, 0:640], Win_hi[:].bitcast(F32), ALU.subtract))
            dve.wait_ge(s_in, 16 * 14)
            do(V.tensor_scalar(convw_sb[:], convw_sb[:], 0.5, None, ALU.mult))
            do(V.tensor_scalar(convb_sb[:], convb_sb[:], 0.5, None, ALU.mult))
            do(V.tensor_scalar(Wout_sb[:], Wout_sb[:], 0.5, None, ALU.mult))
            V.tensor_copy(sel_r[:, 0:M0 * P], sel0_sb)
            V.tensor_copy(sel_r[:, M0 * P:], sel1_sb)
            for dst, src in ((bu_r, bu_sb), (b2_r, b2_sb)):
                do(V.tensor_copy(dst[:, 0, :], src[:]))
                do(V.tensor_tensor(dst[:, 1, :], src[:], dst[:, 0, :].bitcast(F32), ALU.subtract))
            V.memset(half[:], -0.5).then_inc(s_prep, 1)
            dve.wait_ge(s_prep, 1)
            dve.wait_ge(s_p0["act"], 4)
            V.tensor_tensor(cols[:, :, :, K_REST], cols[:, :, :, K_TOT], cols[:, :, :, K_NCS], ALU.add
                            ).then_inc(s_p0["dve"], 1)

            def taps(t, b, i):
                dve.wait_ge(s_raw, 3 * t + i + 1)
                if i == 0:
                    dve.wait_ge(s_hist, 2 * t + 1)
                    s_tap.begin(t)
                if later(t, 1):
                    dve.wait_ge(s_conv, 3 * t - 2 + i)
                a = acc[:, i, :]
                s_tap.inc(V.tensor_scalar(a, raw[:, i, 0:TILE], convw_sb[:, i, 0:1],
                                          convb_sb[:, i:i + 1], ALU.mult, ALU.add))
                yield
                for k in range(1, TAPS):
                    s_tap.wait(dve)
                    s_tap.inc(V.scalar_tensor_tensor(out=a, in0=raw[:, i, k:k + TILE],
                                                     scalar=convw_sb[:, i, k:k + 1], in1=a,
                                                     op0=ALU.mult, op1=ALU.add))
                    yield
                if i == 2:
                    s_tap.end()

            def front(t, b, k):
                if k >= 3:
                    i = k - 3
                    dve.wait_ge(s_zt, 2 * t + i + 1)
                    V.scalar_tensor_tensor(out=z2[b][:, i, :], in0=z2[b][:, i, :], scalar=1.0,
                                           in1=ps[(b + k) % 2][:, :], op0=ALU.add, op1=ALU.mult
                                           ).then_inc(s_z, 1)
                    yield
                if k < 3:
                    yield from taps(t, b, k)
                if 1 <= k < 4:
                    i = k - 1
                    dve.wait_ge(s_th, 3 * t + i + 1)
                    dst = BC[b][:, :] if i == 0 else xs[b][:, i - 1, :]
                    V.scalar_tensor_tensor(out=dst, in0=dst, scalar=1.0, in1=acc[:, i, :],
                                           op0=ALU.add, op1=ALU.mult).then_inc(s_conv, 1)
                    yield

            def ssd(t, b, k):
                if k < H:
                    h = k
                    if h == 0:
                        dve.wait_ge(s_cur, t + 1)
                        s_diff.begin(t)
                    dve.wait_ge(s_ssd, 11 * t + (S_TX0, S_TX1)[h])
                    if later(t, 1):
                        dve.wait_ge(s_ssd, 11 * (t - 1) + (S_Y0, S_Y1)[h])
                    V.tensor_tensor(xdt[:, h, :, :], ps4[3],
                                    cur[b][:, :, h, K_DT:K_DT + 1].to_broadcast([P, CH, P]), ALU.mult
                                    ).then_inc(s_xdt, 1)
                    yield
                    dve.wait_ge(s_ssd, 11 * t + (S_ROW0, S_ROW1)[h])
                    for c in range(CH):
                        s_diff.inc(V.tensor_scalar(E[:, h, c, :], ps4[2][:, c, :],
                                                   cur[b][:, c, h, K_NCS:K_NCS + 1], 0.0, ALU.add,
                                                   ALU.min))
                        yield
                    if h == 1:
                        s_diff.end()
                elif k == 2:
                    s_state.begin(t)
                    if later(t, 1):
                        dve.wait_ge(s_ssd, 11 * (t - 1) + S_Y1)
                    s_state.inc(V.tensor_copy(state[:, :, 0, :], carry[b][:]))
                    yield
                    dve.wait_ge(s_ssd, 11 * t + S_TB)
                    for h in range(H):
                        V.tensor_tensor(Bw[:, h, :, :], ps4[3][:, :, 0:N],
                                        cur[b][:, :, h, K_REST:K_REST + 1].to_broadcast([P, CH, N]),
                                        ALU.mult).then_inc(s_Bw, 1)
                        yield
                    dve.wait_ge(s_ssd, 11 * t + S_SC)
                    for h in range(H):
                        dve.wait_ge(s_mask, 2 * t + h + 1)
                        V.tensor_tensor(M[:, h, :, :], ps4[4], E[:, h, :, :], ALU.mult
                                        ).then_inc(s_M, 1)
                        yield
                elif k < 5:
                    h = k - 3
                    dve.wait_ge(s_ssd, 11 * t + (S_INC0, S_INC1)[h])
                    for c in range(CH):
                        s_state.wait(dve)
                        s_state.inc(V.scalar_tensor_tensor(
                            out=state[:, h, c + 1, :] if c + 1 < CH else carry[b][:, h, :],
                            in0=state[:, h, c, :],
                            scalar=cur[b][0:N, c, h, K_TOT:K_TOT + 1], in1=ps4[2][0:N, c, :],
                            op0=ALU.mult, op1=ALU.add))
                        yield
                    if h == 1:
                        s_state.end()
                elif k < 7:
                    h = k - 5
                    dve.wait_ge(s_ssd, 11 * t + (S_Y0, S_Y1)[h])
                    V.scalar_tensor_tensor(out=yd[b][:, h, :], in0=xs[b][:, h, :],
                                           scalar=small_sb[:, 2, h:h + 1], in1=ps[5][:, :],
                                           op0=ALU.mult, op1=ALU.add).then_inc(s_yd, 1)
                    yield
                else:
                    st = s_ln["ln1"][0]
                    st.begin(t)
                    dve.wait_ge(s_ssd, 11 * t + S_OUT)
                    dve.wait_ge(s_x, 16 * (t + 1))
                    if later(t, 2):
                        dve.wait_ge(s_moe, 12 * (t - 2) + E_XT)
                        dve.wait_ge(s_ln["ln2"][0].sem, s_ln["ln2"][0].per * (t - 2) + LN_RES)
                    st.inc(V.tensor_tensor(x1[b][:], ps4[3], x_sb[:], ALU.add))
                    yield
                    yield from ln_stats(dve, "ln1", t, x1[b])

            def moe(t, b, k):
                if k == 0:
                    yield from ln_norm(dve, "ln1", t, x1[b], x1[b])
                elif k == 1:
                    dve.wait_ge(s_moe, 12 * t + E_LG)
                    if later(t, 1):
                        dve.wait_ge(s_moe, 12 * (t - 1) + E_GT)
                    route_a[0] = router_dve(dve, "ra", t,
                                            ps[7][:, 0:CH * NE].rearrange("p (c e) -> p c e", c=CH),
                                            s_moeD)
                    for _ in range(6):
                        next(route_a[0])
                        yield
                elif k in (2, 3):
                    for _ in range(6 if k == 2 else 7):
                        next(route_a[0])
                        yield
                    if k == 3:
                        advance(route_a[0], 1)
                elif k in (5, 6):
                    for m in (0, 1) if k == 5 else (2, 3):
                        dve.wait_ge(s_moe, 12 * t + E_B0 + m)
                        dve.wait_ge(s_moeA, 6 * t + A_H0 + m)
                        V.tensor_tensor(h0[:, m, :], h0[:, m, :], (ps[7] if m % 2 == 0 else ps[6])[:, :],
                                        ALU.mult).then_inc(s_moeD, 1)
                        yield
                elif k == 7:
                    st = s_ln["ln2"][0]
                    st.begin(t)
                    dve.wait_ge(s_moe, 12 * t + E_OUT)
                    if later(t, 1):
                        dve.wait_ge(s_tail, 2 * t)
                    st.inc(V.tensor_tensor(x2[:], ps4[7], x1[b][:], ALU.add))
                    yield
                    yield from ln_stats(dve, "ln2", t, x2)

            route_a = [None]

            def tail(t, b, k):
                if k == 0:
                    yield from ln_norm(dve, "ln2", t, x2, x2)
                else:
                    dve.wait_ge(s_tail, 2 * t + 2)
                    V.tensor_tensor(G[b][:], G[b][:], ps[7][:, 0:P], ALU.add).then_inc(s_G, 1)
                    yield

            def round_(i, b):
                for calls in in_round(i, b, (front, ssd, moe, tail)):
                    weave(*(f(*a) for f, *a in calls))

            rounds(dve.Fori, round_)

            dve.wait_ge(s_KIp, 1)
            V.tensor_tensor(KI[0][:], ps[0][:, 0:P], ident, ALU.add)
            V.tensor_tensor(KI[1][:], ps[1][:, 0:P], ident, ALU.add).then_inc(s_KI, 1)

            def layernorm3(u, b):
                st = s_ln["ln3"][0]
                st.begin(u)
                dve.wait_ge(s_pre, 5 * u + Q_ATT)
                if later(u, 2):
                    dve.wait_ge(s_ln["ln4"][0].sem, s_ln["ln4"][0].per * (u - 2) + LN_RES)
                st.inc(V.tensor_copy(x3[b][:], ps4[6]))
                yield
                yield from ln_stats(dve, "ln3", u, x3[b])
                yield from ln_norm(dve, "ln3", u, x3[b], x3[b])

            def router(u):
                dve.wait_ge(s_pre, 5 * u + Q_LG)
                yield from router_dve(dve, "rb", u, ps[6][:, 0:CH * NE].rearrange("p (c e) -> p c e", c=CH))

            def finish(u, b):
                st = s_ln["ln4"][0]
                st.begin(u)
                dve.wait_ge(s_fin, u + 1)
                if later(u, 1):
                    dve.wait_ge(s_out, 16 * u)
                st.inc(V.tensor_tensor(o_sb[:], ps4[7], x3[b][:], ALU.add))
                yield
                yield from ln_stats(dve, "ln4", u, o_sb)
                yield from ln_norm(dve, "ln4", u, o_sb, o_sb)

            def experts(u, b, last=False, first=False):
                done = None if first else finish(u - 1, 1 - b)
                norm = None if last else layernorm3(u + 1, 1 - b)
                route = None if last else router(u + 1)
                for q in range(NE * FT):
                    e, f = divmod(q, FT)
                    i = q % RH
                    dve.wait_ge(s_hhi, 32 * u + q + 1)
                    V.tensor_tensor(h1_lo[i], h1[:, i, :], h1_hi[i].bitcast(F32), ALU.subtract
                                    ).then_inc(s_hlo, 1)
                    if f == 1:
                        dve.wait_ge(s_wb, 8 * u + e + 1)
                        if e >= 2 or later(u, 1):
                            dve.wait_ge(s_yw, 8 * u + e - 1)
                        V.tensor_copy(wbc[:, e % 2, :], ps[5][:, :]).then_inc(s_wbc, 1)
                    if f == 3 and e >= 1:
                        gate(u, e - 1)
                    for part, plan in ((done, DVE_LN4), (norm, DVE_LN3), (route, DVE_RT)):
                        if part is not None:
                            advance(part, plan.get(q, 0))
                for part in (done, norm, route):
                    assert part is None or next(part, None) is None
                gate(u, NE - 1)

            def gate(u, e):
                dve.wait_ge(s_down, 32 * u + FT * (e + 1))
                dve.wait_ge(s_wbc, 8 * u + e + 1)
                if e >= 2 or later(u, 1):
                    dve.wait_ge(s_sum, 8 * u + e - 1)
                V.tensor_tensor(yw[:, e % 2, :], ps[3 + e % 2][:, :], wbc[:, e % 2, :], ALU.mult
                                ).then_inc(s_yw, 1)

            for part in (layernorm3(0, 0), router(0)):
                weave(part)
            experts(0, 0, first=True)
            with dve.Fori(0, NT // 2 - 1) as v:
                experts(2 * v + 1, 1)
                experts(2 * v + 2, 0)
            experts(NT - 1, 1, last=True)
            weave(finish(NT - 1, 1))

        @block.gpsimd
        def _(pool):
            L = nc.gpsimd
            pool.wait_ge(s_in0, 16 * 7)
            pool.wait_ge(s_prep, 1)
            pool.wait_ge(s_p0["act"], 6)

            def split(t, b):
                xt = xT_sb[:, bass.ds(t, 1), :].rearrange("p o q -> p (o q)")
                pool.wait_ge(s_xhi, t + 1)
                L.tensor_tensor(x_lo[b][:], xt, x_hi[b][:].bitcast(F32), ALU.subtract).then_inc(s_xlo, 1)

            def decays(t, b):
                if later(t, 2):
                    pool.wait_ge(s_exp, 2 * (t - 1))
                    pool.wait_ge(s_state.sem, s_state.per * (t - 1))
                apart(pool)
                L.tensor_copy(cur[b][:], cols[:, bass.ds(CH * t, CH), :, :]).then_inc(s_cur, 1)
                pool.wait_ge(s_cur, t + 1)
                for h in range(H):
                    if later(t, 1):
                        pool.wait_ge(s_ssd, 11 * (t - 1) + (S_ROW0, S_ROW1)[h])
                    L.tensor_tensor(dAU[:, h, :, :], tri.unsqueeze(1).to_broadcast([P, CH, P]),
                                    cur[b][:, :, h, K_DA:K_DA + 1].to_broadcast([P, CH, P]), ALU.mult
                                    ).then_inc(s_dAU, 1)

            def parts(src, hi, lo, hisem, losem, n):
                apart(pool)
                L.tensor_copy(hi, src).then_inc(hisem, 1)
                pool.wait_ge(hisem, n)
                L.tensor_tensor(lo, src, hi.bitcast(F32), ALU.subtract).then_inc(losem, 1)

            def weights(t, k):
                if k == 0:
                    s_w.begin(t)
                    pool.wait_ge(s_wraw, 32 * (t + 1))
                apart(pool)
                c = bass.ds(t * TILE, TILE)
                s_w.inc(L.tensor_copy(w_hi[:, k, c], wraw[:, k, :]))
                s_w.wait(pool)
                s_w.inc(L.tensor_tensor(w_lo[:, k, c], wraw[:, k, :], w_hi[:, k, c].bitcast(F32),
                                        ALU.subtract))
                if k == 1:
                    s_w.end()

            def front(t, b, k):
                if k == 3:
                    decays(t, b)
                elif k == 4:
                    weights(t, 0)
                    weights(t, 1)

            def ssd(t, b, k):
                if k < H:
                    h = k
                    pool.wait_ge(s_exp, 2 * t + h + 1)
                    apart(pool)
                    L.affine_select(out=E[:, h, :, :], in_=E[:, h, :, :], compare_op=ALU.is_ge, fill=0.0,
                                    base=0, pattern=[[0, CH], [1, P]], channel_multiplier=-1
                                    ).then_inc(s_mask, 1)
                    pool.wait_ge(s_C0, 16 * (t + 1))
                    L.tensor_tensor(Cs[:, h, :], C0[b][:], Cs[:, h, :], ALU.mult).then_inc(s_Cs, 1)
                elif k in (5, 6):
                    h = k - 5
                    pool.wait_ge(s_yd, 2 * t + h + 1)
                    pool.wait_ge(s_z, 2 * t + h + 1)
                    L.tensor_tensor(yg[b][:, h, :], yd[b][:, h, :], z2[b][:, h, :], ALU.mult
                                    ).then_inc(s_yg, 1)
                elif k == 7:
                    ln_pool(pool, "ln1", t)

            def moe(t, b, k):
                if k == 0:
                    pool.wait_ge(s_moeA, 6 * t + A_XT)
                    if later(t, 1):
                        pool.wait_ge(s_moe, 12 * (t - 1) + E_H3)
                    parts(x1T[:], x1T_hi[:], x1T_lo[:], s_x1hi, s_x1lo, t + 1)
                elif k == 7:
                    ln_pool(pool, "ln2", t)

            pool.wait_ge(s_in, 16 * 14)
            parts(Wd_sb, Wd_hi[:], Wd_lo[:], s_wd0, s_wd, 1)

            def round_(i, b):
                if not isinstance(i, int) or i < NT:
                    split(i, b)
                for calls in in_round(i, b, (front, ssd, moe, None)):
                    for f, *a in calls:
                        f(*a)

            rounds(pool.Fori, round_)

            def prepare(u, b, piece):
                if piece == 0:
                    if later(u, 1):
                        pool.wait_ge(s_pre, 5 * (u - 1) + Q_ATT)
                    else:
                        pool.wait_ge(s_x2T, NT)
                    apart(pool)
                    L.tensor_copy(x2T_cur[:], x2T[:, bass.ds(u, 1), :].rearrange("p o q -> p (o q)")
                                  ).then_inc(s_cur2, 1)
                elif piece == 1:
                    ln_pool(pool, "ln3", u)
                elif piece == 2:
                    pool.wait_ge(s_x3T, u + 1)
                    if later(u, 2):
                        pool.wait_ge(s_up, 32 * (u - 1))
                    parts(x3T, x3T_hi[b][:], x3T_lo[b][:], s_x3hi, s_x3lo, u + 1)

            def experts(u, b, last=False, first=False):
                for e in range(NE):
                    if e == 0 and not first:
                        ln_pool(pool, "ln4", u - 1)
                    if e < 2 and not last:
                        prepare(u + 1, 1 - b, e)
                    if e == 2 and not last:
                        prepare(u + 1, 1 - b, 2)
                    pool.wait_ge(s_yw, 8 * u + e + 1)
                    if e == 0:
                        pool.wait_ge(s_acc0, u + 1)
                    else:
                        pool.wait_ge(s_sum, 8 * u + e)
                    L.tensor_tensor(oT[b], oT[b], yw[:, e % 2, :], ALU.add).then_inc(s_sum, 1)

            for piece in range(3):
                prepare(0, 0, piece)
            experts(0, 0, first=True)
            with pool.Fori(0, NT // 2 - 1) as v:
                experts(2 * v + 1, 1)
                experts(2 * v + 2, 0)
            experts(NT - 1, 1, last=True)
            ln_pool(pool, "ln4", NT - 1)


def layouts(i):
    import numpy as np

    f = {k: np.asarray(v) for k, v in i.items()}

    def rows(v, n=P):
        return np.ascontiguousarray(np.broadcast_to(v[None, :], (n,) + v.shape))

    x = f["L0_attn_x"].reshape(NB, NT // NB, CH, P, P)
    Win = f["L0_attn_W_in"]
    conv_rows = (np.arange(256, 384), np.arange(0, 128), np.arange(128, 256))
    cw = f["L0_attn_conv_w"].reshape(384, TAPS)
    cb = f["L0_attn_conv_b"]
    const = np.zeros((P, C_COLS), np.float32)
    const[:, C_ID:C_ID + P] = np.eye(P)
    const[:, C_TRI:C_TRI + P] = np.triu(np.ones((P, P)))
    const[:, C_ONE:C_ONE + P] = 1
    const[:, C_REV:] = NE - np.arange(NE)
    sel = np.zeros((2 * NE, M0 * P + NE * P), np.float32)
    for e in range(NE):
        for r in (e, e + NE):
            sel[r, e * 64:(e + 1) * 64] = 1
            sel[r, M0 * P + e * P:M0 * P + (e + 1) * P] = 1
    d = {
        "x": x.transpose(3, 1, 0, 2, 4).reshape(P, NCHUNK, P),
        "xT": x.transpose(4, 1, 0, 2, 3).reshape(P, NT, TILE),
        "W_inT": Win.T,
        "conv_w": np.stack([cw[r] for r in conv_rows], 1),
        "conv_b": np.stack([cb[r] for r in conv_rows], 1),
        "A_log": rows(f["L0_attn_A_log"]),
        "dt_bias": rows(f["L0_attn_dt_bias"]),
        "D_skip": rows(f["L0_attn_D_skip"]),
        "W_outT": f["L0_attn_W_out"].T.reshape(H, P, P).transpose(1, 0, 2),
        "w_gate": f["L0_ffn_w_gate"],
        "WdT": f["L0_ffn_Wd"].transpose(1, 0, 2).reshape(P, M0 * P),
        "bd": f["L0_ffn_bd"].reshape(M0, P).T,
        "Wu": f["L0_ffn_Wu"].reshape(M0, P, P).transpose(1, 0, 2),
        "bu": np.concatenate([f["L0_ffn_bu"]] * 2, 0),
        "Wq": f["L1_attn_W_q"],
        "router_wT": f["L1_ffn_router_w"].T,
        "w1T": f["L1_ffn_w1"].transpose(2, 0, 1).reshape(P, NE * FT * P),
        "b1": f["L1_ffn_b1"].reshape(NE * FT, P).T,
        "w2T": f["L1_ffn_w2"].reshape(NE, P, FT, P).transpose(3, 0, 2, 1).reshape(P, NE * FT * P),
        "b2": np.concatenate([f["L1_ffn_b2"]] * 2, 0),
        "const": const,
        "sel": sel,
    }
    return {k: np.ascontiguousarray(v) for k, v in d.items()}


def kernel(**inputs):
    import numpy as np
    import concourse.bacc as bacc
    from concourse.bass_utils import run_bass_kernel_spmd

    data = layouts(inputs)
    nc = bacc.Bacc("TRN2", target_bir_lowering=False, num_devices=1)
    arrays, args = {}, {}
    for name, a in data.items():
        arrays[f"in_{name}"] = a
        args[name] = nc.dram_tensor(f"in_{name}", a.shape, mybir.dt.from_np(a.dtype), kind="ExternalInput").ap()
    args["out"] = nc.dram_tensor("out_x", (P, NCHUNK, P), F32, kind="ExternalOutput").ap()
    build_kernel(nc, **args)
    r = run_bass_kernel_spmd(nc, [arrays], core_ids=[0])
    o = np.asarray(r.results[0]["out_x"]).reshape(P, NT // NB, NB, CH, P)
    return np.ascontiguousarray(o.transpose(2, 1, 3, 0, 4)).reshape(NB, NT // NB * TILE, P)
```

```python
from contextlib import ExitStack

import concourse.bass as bass
from concourse import mybir

F32 = mybir.dt.float32
F32R = mybir.dt.float32r
ALU = mybir.AluOpType
ACT = mybir.ActivationFunctionType
AX = mybir.AxisListType

P = 128
TILE = 512
CH = TILE // P
NT = 8
NB = 2
NCHUNK = NT * CH
H = 2
N = 64
TAPS = 4
HIST = TAPS - 1
NE = 8
M0 = 4
FT = 4
EPS = 1e-5
SERIES = 9

C_ID, C_TRI, C_ONE, C_REV = 0, P, 2 * P, 3 * P
C_COLS = 3 * P + NE


class Steps:

    def __init__(self, sem, per):
        self.sem, self.per = sem, per

    def begin(self, t, k=0):
        self.base, self.k = t * self.per, k

    def inc(self, ins):
        ins.then_inc(self.sem, 1)
        self.k += 1

    def wait(self, eng, back=0):
        eng.wait_ge(self.sem, self.base + self.k - back)

    def then(self, eng, op, *args, **named):
        if self.k:
            self.wait(eng)
        self.inc(op(*args, **named))

    def end(self):
        assert self.k == self.per, (self.sem, self.k, self.per)


def weave(*parts):
    parts = list(parts)
    while parts:
        for p in list(parts):
            if next(p, parts) is parts:
                parts.remove(p)


def advance(part, n):
    for _ in range(n):
        next(part, None)


SPLIT, FRONT, SSD, MOE, TAIL = range(5)
PE_ROUND = (
    ((SSD, 0, 1), (SSD, 7, 2), (MOE, 6, 3), (SSD, 1, 1)),
    ((MOE, 7, 3), (FRONT, 0, 0)),
    ((MOE, 8, 3), (SSD, 2, 1), (FRONT, 1, 0)),
    ((SSD, 3, 1), (FRONT, 2, 0), (MOE, 9, 3), (MOE, 1, 2)),
    ((SSD, 4, 1), (MOE, 10, 3), (FRONT, 3, 0), (MOE, 2, 2)),
    ((SSD, 5, 1), (FRONT, 4, 0), (MOE, 3, 2)),
    ((MOE, 4, 2), (SSD, 6, 1)),
    ((TAIL, 1, 3),),
)
ACT_ROUND = (
    ((SPLIT, 0, 0), (SSD, 0, 1), (MOE, 6, 3)),
    ((SSD, 1, 1), (FRONT, 0, 0), (FRONT, 1, 0), (MOE, 0, 2)),
    (),
    ((FRONT, 2, 0), (MOE, 1, 2)),
    ((FRONT, 3, 0),),
    ((MOE, 3, 2), (FRONT, 4, 0)),
    ((MOE, 4, 2), (TAIL, 0, 3), (FRONT, 5, 0)),
    ((MOE, 5, 2), (TAIL, 1, 3), (FRONT, 6, 0)),
)
DVE_ROUND = (
    ((SSD, 0, 1),),
    ((MOE, 7, 3), (SSD, 1, 1), (SSD, 8, 2)),
    ((MOE, 8, 3), (SSD, 2, 1), (FRONT, 1, 0)),
    ((SSD, 3, 1), (FRONT, 2, 0)),
    ((SSD, 4, 1), (MOE, 10, 3), (FRONT, 3, 0), (MOE, 2, 2)),
    ((MOE, 11, 3), (SSD, 5, 1), (FRONT, 4, 0), (MOE, 3, 2)),
    ((FRONT, 5, 0), (MOE, 4, 2)),
    ((SSD, 6, 1), (MOE, 5, 2), (TAIL, 1, 3)),
)
POOL_ROUND = (
    ((SPLIT, 0, 0), (SSD, 0, 1)),
    ((SSD, 1, 1), (SSD, 8, 2)),
    (),
    ((MOE, 1, 2),),
    (),
    ((MOE, 11, 3), (SSD, 5, 1), (FRONT, 4, 0)),
    ((SSD, 6, 1), (FRONT, 5, 0)),
    ((FRONT, 6, 0),),
)

URGENT = ((MOE, 11), (SSD, 0), (SSD, 1), (SSD, 2), (SSD, 3), (SSD, 4), (SSD, 5), (SSD, 6), (TAIL, 1))


def rounds(fori, do, after_first):
    for i in range(4):
        do(i, i % 2)
        if i == 0:
            after_first()
    with fori(2, NT // 2) as j:
        do(2 * j, 0)
        do(2 * j + 1, 1)
    for i in range(NT, NT + 3):
        do(i, i % 2)


def in_round(table, i, b, stages):
    for group in table:
        calls = []
        for stage, k, behind in group:
            t = i - behind
            if isinstance(i, int) and not 0 <= t < NT:
                continue
            if stages[stage] is not None:
                calls.append((stages[stage], t, (b + behind) % 2, k))
        yield calls


def later(t, n):
    return not isinstance(t, int) or t >= n


def build_kernel(nc, x, xT, W_inT, conv_w, conv_b, A_log, dt_bias, D_skip, W_outT, w_gate, WdT, bd,
                 Wu, bu, Wq, router_wT, w1T, b1, w2T, b2, const, sel, out):
    ctx = ExitStack()
    with ctx:
        def sb(name, shape, dt=F32):
            return ctx.enter_context(nc.sbuf_tensor(name, shape, dt))

        def bank(name):
            return ctx.enter_context(nc.psum_tensor(name, [P, 512], F32))

        def sem(name):
            return ctx.enter_context(nc.semaphore(name))

        x_sb = sb("x_sb", [P, CH, P])
        xT_sb = sb("xT_sb", [P, NT, TILE])
        const_sb = sb("const_sb", [P, C_COLS])
        convw_sb = sb("convw_sb", [P, 3, TAPS])
        convb_sb = sb("convb_sb", [P, 3])
        small_sb = sb("small_sb", [P, 3, H])
        Wout_sb = sb("Wout_sb", [P, H, P])
        wgate_sb = sb("wgate_sb", [P, NE])
        bd_sb = sb("bd_sb", [P, M0])
        Wu_sb = sb("Wu_sb", [P, M0, P])
        bu_sb = sb("bu_sb", [2 * NE, P])
        Wq_sb = sb("Wq_sb", [P, P])
        rw_sb = sb("rw_sb", [P, NE])
        b1_sb = sb("b1_sb", [P, NE * FT])
        b2_sb = sb("b2_sb", [2 * NE, P])
        wraw = sb("wraw", [P, 2, TILE])
        ident = const_sb[:, C_ID:C_ID + P]
        tri = const_sb[:, C_TRI:C_TRI + P]
        ones = const_sb[:, C_ONE:C_ONE + P]
        rev = const_sb[:, C_REV:C_REV + NE]

        Win_hi, Win_lo = sb("Win_hi", [P, 640], F32R), sb("Win_lo", [P, 640], F32R)
        Wd_hi, Wd_lo = sb("Wd_hi", [P, M0 * P], F32R), sb("Wd_lo", [P, M0 * P], F32R)
        w_hi = sb("w_hi", [P, 2, NE * FT * P], F32R)
        w_lo = sb("w_lo", [P, 2, NE * FT * P], F32R)
        sel_r = sb("sel_r", [2 * NE, M0 * P + NE], F32R)
        bu_r = sb("bu_r", [2 * NE, 2, P], F32R)
        b2_r = sb("b2_r", [2 * NE, 2, P], F32R)

        dtv = sb("dtv", [P, NCHUNK, H])
        dA = sb("dA", [P, NCHUNK, H])
        sp = [sb(f"sp{i}", [P, NCHUNK, H]) for i in range(5)]
        expA = sb("expA", [P, H])
        K_DT, K_DA, K_CS, K_REST, K_TOT = range(5)
        cols = sb("cols", [P, NCHUNK, H, 5])

        x_hi = [sb(f"x_hi{b}", [P, TILE], F32R) for b in range(NB)]
        x_lo = [sb(f"x_lo{b}", [P, TILE], F32R) for b in range(NB)]
        raw = sb("raw", [P, 3, HIST + TILE])
        hist = [sb(f"hist{b}", [P, 3, HIST]) for b in range(NB)]
        acc = sb("acc", [P, 3, TILE])
        BC = [sb(f"BC{b}", [P, TILE]) for b in range(NB)]
        xs = [sb(f"xs{b}", [P, H, TILE]) for b in range(NB)]
        z2 = [sb(f"z2{b}", [P, H, TILE]) for b in range(NB)]
        C0 = [sb("C0", [N, TILE])] * NB
        cur = [sb(f"cur{b}", [P, CH, H, 5]) for b in range(NB)]
        dAU = sb("dAU", [P, H, CH, P])
        E = sb("E", [P, H, CH, P])
        Cs = sb("Cs", [N, H, TILE])
        xdt = sb("xdt", [P, H, CH, P])
        Bw = sb("Bw", [P, H, CH, N])
        M = E
        state = sb("state", [N, H, CH, P])
        carry = [sb(f"carry{b}", [N, H, P]) for b in range(NB)]
        yd = xs
        yg = z2
        x1 = [sb(f"x1{b}", [P, CH, P]) for b in range(NB)]
        x1T = sb("x1T", [P, TILE])
        x1T_hi, x1T_lo = sb("x1T_hi", [P, TILE], F32R), sb("x1T_lo", [P, TILE], F32R)
        h0 = sb("h0", [P, M0, TILE])
        flat_h0 = h0[:, :, :].rearrange("p m q -> p (m q)")
        Win_sb, Wd_sb = flat_h0[:, 0:642], flat_h0[:, 1024:1024 + M0 * P]
        sel_sb = xdt[0:2 * NE, :, :, :].rearrange("p h c q -> p (h c q)")[:, 0:M0 * P + NE]
        x2 = sb("x2", [P, CH, P])
        x2T = xT_sb
        G = [sb(f"G{b}", [P, P]) for b in range(NB)]
        stats = {k: (sb(f"bn{k}", [P, CH, 6]), sb(f"mv{k}", [P, CH, 2]), sb(f"rstd{k}", [P, CH]))
                 for k in ("ln1", "ln2", "ln3", "ln4")}
        shift = {k: sb(f"shift{k}", [P, CH]) for k in ("ln1", "ln2")}
        half = sb("half", [P, CH])
        route = {k: [sb(f"{k}{n}", s) for n, s in
                     (("lg", [P, CH, NE]), ("m1", [P, CH]), ("m2", [P, CH]), ("key", [P, CH, NE]),
                      ("kmax", [P, CH]), ("oh1", [P, CH, NE]), ("oh2", [P, CH, NE]),
                      ("d", [P, CH]), ("e2", [P, CH]), ("g", [P, CH, NE]), ("sum", [P, CH]))]
                 for k in ("ra", "rb")}
        g16 = {k: sb(f"g16{k}", [P, CH, 2 * NE], F32R) for k in ("ra", "rb")}
        gT = sb("gT", [2 * NE, TILE], F32R)

        KI = [sb(f"KI{b}", [P, P]) for b in range(NB)]
        x2T_cur = x1T
        x3 = x1
        x3T = acc[:, 0, :]
        x3T_hi, x3T_lo = x_hi, x_lo
        w16T = [gT, sb("w16T1", [2 * NE, TILE], F32R)]
        RH = 4
        h1 = h0
        h1_hi3, h1_lo3 = sb("h1_hi3", [P, TILE], F32R), sb("h1_lo3", [P, TILE], F32R)
        h1_hi = [x1T_hi[:, :], Win_hi[:, 0:TILE], Wd_hi[:, :], h1_hi3[:]]
        h1_lo = [x1T_lo[:, :], Win_lo[:, 0:TILE], Wd_lo[:, :], h1_lo3[:]]
        wbc = E[:, :, :, :].rearrange("p h c q -> p h (c q)")
        yw = xdt[:, :, :, :].rearrange("p h c q -> p h (c q)")
        oT = [dAU[:, h, :, :].rearrange("p c q -> p (c q)") for h in range(H)]
        o_sb = x2

        ps = [bank(f"ps{i}") for i in range(8)]
        ps4 = [p[:, :].rearrange("p (c q) -> p c q", c=CH) for p in ps]

        s_first = sem("s_first")
        s_in0 = sem("s_in0")
        s_prep0 = sem("s_prep0")
        s_in = sem("s_in")
        s_wraw, s_x = sem("s_wraw"), sem("s_x")
        s_prep = sem("s_prep")
        s_wd0, s_wd = sem("s_wd0"), sem("s_wd")
        s_whi, s_w = sem("s_whi"), sem("s_w")
        s_p0 = {e: sem(f"s_p0_{e}") for e in ("pe", "act", "dve")}
        s_absv = sem("s_absv")
        s_p0chain = sem("s_p0chain")
        s_xhi, s_xlo = sem("s_xhi"), sem("s_xlo")
        s_cur, s_dAU = sem("s_cur"), sem("s_dAU")
        s_proj = sem("s_proj")
        s_hist, s_raw, s_zt = sem("s_hist"), sem("s_raw"), sem("s_zt")
        s_tap = Steps(sem("s_tap"), 9)
        s_th = sem("s_th")
        s_conv = sem("s_conv")
        s_z = sem("s_z")
        s_C0 = sem("s_C0")
        s_scan = sem("s_scan")
        s_ssd = sem("s_ssd")
        S_TX0, S_ROW0, S_TX1, S_ROW1, S_TB, S_SC, S_INC0, S_INC1, S_Y0, S_Y1 = range(1, 11)
        s_cs = sem("s_cs")
        s_exp, s_mask, s_Cs = sem("s_exp"), sem("s_mask"), sem("s_Cs")
        s_xdt, s_Bw, s_M = sem("s_xdt"), sem("s_Bw"), sem("s_M")
        s_state = Steps(sem("s_state"), 1 + CH * H)
        s_yd, s_yg = sem("s_yd"), sem("s_yg")
        s_ln = {k: (Steps(sem(f"s_{k}"), 1 + CH + (CH - 1) + (CH if k in ("ln3", "ln4") else 0)),
                    sem(f"s_{k}v"), sem(f"s_{k}r")) for k in ("ln1", "ln2", "ln3", "ln4")}
        s_norm = {k: sem(f"s_{k}n") for k in ("ln1", "ln2")}
        s_moe = sem("s_moe")
        E_XT, E_LG, E_H0, E_H1, E_H2, E_H3, E_GT, E_B0, E_B1, E_B2, E_B3 = range(1, 12)
        s_moeO = sem("s_moeO")
        s_moeA = sem("s_moeA")
        A_XT, A_H0, A_H1, A_H2, A_H3, A_GT = range(1, 7)
        s_moeD = sem("s_moeD")
        D_LG, D_B0, D_B1, D_B2, D_B3 = range(1, 6)
        s_tail = sem("s_tail")
        s_x2T, s_G = sem("s_x2T"), sem("s_G")
        s_x1hi, s_x1lo = sem("s_x1hi"), sem("s_x1lo")
        s_rt = {"ra": Steps(sem("s_ra"), 19), "rb": Steps(sem("s_rb"), 23)}
        s_rexp = {k: sem(f"s_{k}e") for k in ("ra", "rb")}
        s_KIp, s_KI = sem("s_KIp"), sem("s_KI")
        s_cur2 = sem("s_cur2")
        s_pre = sem("s_pre")
        Q_ATT, Q_XT, Q_LG, Q_GT, Q_B2 = range(1, 6)
        s_x3T, s_x3hi, s_x3lo, s_w16T, s_acc0 = (sem(n) for n in
                                                 ("s_x3T", "s_x3hi", "s_x3lo", "s_w16T", "s_acc0"))
        s_fin = sem("s_fin")
        s_up, s_relu, s_hhi, s_hlo, s_down = (sem(n) for n in
                                              ("s_up", "s_relu", "s_hhi", "s_hlo", "s_down"))
        s_wb, s_wbc, s_yw, s_sum = (sem(n) for n in ("s_wb", "s_wbc", "s_yw", "s_sum"))
        s_out = sem("s_out")
        s_apart = sem("s_apart")

        block = ctx.enter_context(nc.Block())

        LAG = 3
        PE_AT = {4: 0, 12: 1, 15: 2, 28: 3, 29: 4}
        PE_FINISH = 3
        ACT_AT = {14: 1, 21: 2, 29: 3, 31: 4}
        DVE_LN4 = {5: 3, 6: 3, 7: 1, 8: 2, 9: 2, 10: 2}
        DVE_LN3 = {5: 2, 6: 1, 7: 1, 8: 3, 9: 2, 12: 4}
        DVE_RT = {17: 4, 18: 4, 19: 4, 20: 2, 23: 3, 24: 3, 25: 3}

        def apart(eng):
            eng.sem_inc(s_apart, 1)

        def mm3(pe, dst, a_hi, a_lo, b_hi, b_lo, start=True, stop=True):
            pe.matmul(dst, a_hi, b_hi, start=start, stop=False)
            pe.matmul(dst, a_hi, b_lo, start=False, stop=False)
            return pe.matmul(dst, a_lo, b_hi, start=False, stop=stop)

        @block.sync
        def _(sp_):
            sp_.dma_start(Win_sb, W_inT).then_inc(s_first, 16)
            sp_.dma_start(xT_sb[:, 0:1, :], xT[:, 0:1, :]).then_inc(s_first, 16)
            sp_.dma_start(convw_sb[:], conv_w).then_inc(s_first, 16)
            sp_.dma_start(convb_sb[:], conv_b).then_inc(s_first, 16)
            sp_.dma_start(xT_sb[:, 1:4, :], xT[:, 1:4, :]).then_inc(s_in0, 16)
            sp_.dma_start(const_sb[:], const).then_inc(s_in0, 16)
            sp_.dma_start(small_sb[:, 0, :], A_log).then_inc(s_in0, 16)
            sp_.dma_start(small_sb[:, 1, :], dt_bias).then_inc(s_in0, 16)
            sp_.dma_start(small_sb[:, 2, :], D_skip).then_inc(s_in0, 16)
            sp_.dma_start(xT_sb[:, 4:8, :], xT[:, 4:8, :]).then_inc(s_in0, 16)
            for dst, src in ((Wout_sb, W_outT), (wgate_sb, w_gate), (bd_sb, bd), (Wu_sb, Wu),
                             (bu_sb, bu), (Wq_sb, Wq), (rw_sb, router_wT), (b1_sb, b1),
                             (b2_sb, b2)):
                sp_.dma_start(dst[:], src).then_inc(s_in, 16)
            sp_.dma_start(Wd_sb, WdT).then_inc(s_in, 16)
            sp_.dma_start(sel_sb, sel).then_inc(s_in, 16)

            def tile(t, b):
                if later(t, 1):
                    sp_.wait_ge(s_w, 2 * t)
                sp_.dma_start(wraw[:, 0, :], w1T[:, bass.ds(t * TILE, TILE)]).then_inc(s_wraw, 16)
                sp_.dma_start(wraw[:, 1, :], w2T[:, bass.ds(t * TILE, TILE)]).then_inc(s_wraw, 16)
                sp_.wait_ge(s_conv, 3 * t + 1)
                if later(t, 1):
                    sp_.wait_ge(s_ssd, 10 * (t - 1) + S_SC)
                    sp_.wait_ge(s_Cs, 2 * t)
                sp_.dma_start(C0[b][:], BC[b][N:2 * N, :]).then_inc(s_C0, 16)
                if later(t, 1):
                    sp_.wait_ge(s_ln["ln1"][0].sem, s_ln["ln1"][0].per * (t - 1) + 1)
                sp_.dma_start(x_sb[:], x[:, bass.ds(CH * t, CH), :]).then_inc(s_x, 16)

            for t in range(NT):
                tile(t, t % NB)

            def store(u):
                sp_.wait_ge(s_ln["ln4"][0].sem, s_ln["ln4"][0].per * (u + 1))
                sp_.dma_start(out[:, bass.ds(CH * u, CH), :], o_sb[:]).then_inc(s_out, 16)

            for u in range(NT):
                store(u)
            sp_.wait_ge(s_out, 16 * NT)

        LN_RES = 1

        def ln_stats(dve, k, t, src):
            st = s_ln[k][0]
            bn, mv, _ = stats[k]
            if k in s_norm and later(t, 1):
                dve.wait_ge(s_ln[k][2], 4 * t)
            for c in range(CH):
                if c == 0:
                    st.wait(dve)
                st.inc(nc.vector.bn_stats(bn[:, c, :], src[:, c, :]))
                yield
            for c in range(CH):
                st.wait(dve, back=CH - 1)
                apart(dve)
                ins = nc.vector.bn_aggr(mv[:, c, :], bn[:, c, :])
                if c == CH - 1:
                    ins.then_inc(s_ln[k][1], 1)
                else:
                    st.inc(ins)
                yield

        def ln_norm(dve, k, t, src, dst):
            st, rsem = s_ln[k][0], s_ln[k][2]
            _, mv, rstd = stats[k]
            st.begin(t, 1 + CH + CH - 1)
            dve.wait_ge(rsem, 2 * (t + 1))
            for c in range(CH):
                st.inc(nc.vector.tensor_scalar(dst[:, c, :], src[:, c, :], mv[:, c, 0:1],
                                               rstd[:, c:c + 1], ALU.subtract, ALU.mult))
                yield
            st.end()

        def ln_pool(pool, k, t):
            bn, mv, rstd = stats[k]
            L, r, per = nc.gpsimd, s_ln[k][2], 4 if k in s_norm else 2
            pool.wait_ge(s_ln[k][1], t + 1)
            if k in s_norm and later(t, 1):
                pool.wait_ge(s_norm[k], t)
            apart(pool)
            L.tensor_scalar(rstd[:], mv[:, :, 1], EPS, None, ALU.add).then_inc(r, 1)
            if k in s_norm:
                L.tensor_scalar(shift[k][:], mv[:, :, 0], -1.0, None, ALU.mult).then_inc(r, 1)
            pool.wait_ge(r, per * t + 1)
            L.tensor_tensor(rstd[:], rstd[:], half[:], ALU.pow).then_inc(r, 1)
            if k in s_norm:
                pool.wait_ge(r, per * t + 3)
                L.tensor_tensor(shift[k][:], shift[k][:], rstd[:], ALU.mult).then_inc(r, 1)

        def ln_act(act, k, t, x):
            act.wait_ge(s_ln[k][2], 4 * (t + 1))
            apart(act)
            for c in range(CH):
                ins = nc.scalar.activation(x[:, c, :], x[:, c, :], ACT.Identity,
                                           scale=stats[k][2][:, c:c + 1], bias=shift[k][:, c:c + 1])
            ins.then_inc(s_norm[k], 1)

        def over_e(v):
            return v[:, :].unsqueeze(2).to_broadcast([P, CH, NE])

        def over_c(v):
            return v.unsqueeze(1).to_broadcast([P, CH, NE])

        def router_dve(dve, k, t, logits, emptied=None):
            st, e = s_rt[k], s_rexp[k]
            lg, m1, m2, key, kmax, oh1, oh2, d, e2, g, tot = route[k]
            V = nc.vector
            st.begin(t)
            ins = V.tensor_copy(lg[:], logits)
            if emptied is not None:
                ins.then_inc(emptied, 1)
                dve.wait_ge(emptied, 5 * t + D_LG)
            else:
                st.inc(ins)
                yield
            st.then(dve, V.tensor_reduce, m1[:], lg[:], AX.X, ALU.max)
            yield

            def first_of(src, m, oh):
                st.then(dve, V.tensor_tensor, key[:], src[:], over_e(m), ALU.is_equal)
                yield
                st.then(dve, V.tensor_tensor, key[:], key[:], over_c(rev), ALU.mult)
                yield
                st.then(dve, V.tensor_reduce, kmax[:], key[:], AX.X, ALU.max)
                yield
                st.then(dve, V.tensor_tensor, oh[:], key[:], over_e(kmax), ALU.is_equal)
                yield

            yield from first_of(lg, m1, oh1)
            st.then(dve, V.scalar_tensor_tensor, out=g[:], in0=oh1[:], scalar=-3.0e38, in1=lg[:],
                    op0=ALU.mult, op1=ALU.add)
            yield
            st.then(dve, V.tensor_reduce, m2[:], g[:], AX.X, ALU.max)
            yield
            yield from first_of(g, m2, oh2)
            st.then(dve, V.tensor_tensor, d[:], m2[:], m1[:], ALU.subtract)
            yield
            if k == "ra":
                dve.wait_ge(e, t + 1)
                st.then(dve, V.tensor_scalar, tot[:], e2[:], 1.0, 2.0, ALU.add, ALU.mult)
                yield
            else:
                st.then(dve, V.tensor_tensor, g[:], lg[:], over_e(m1), ALU.subtract)
                yield
                dve.wait_ge(e, 2 * (t + 1))
                st.then(dve, V.tensor_reduce, tot[:], g[:], AX.X, ALU.add)
                yield
                st.then(dve, V.scalar_tensor_tensor, out=tot[:], in0=tot[:], scalar=1e-9, in1=e2[:],
                        op0=ALU.mult, op1=ALU.add)
                yield
                st.then(dve, V.tensor_scalar, tot[:], tot[:], 1.0, None, ALU.add)
                yield
            st.then(dve, V.reciprocal, tot[:], tot[:])
            yield
            st.then(dve, V.tensor_tensor, oh2[:], oh2[:], over_e(e2), ALU.mult)
            yield
            st.then(dve, V.tensor_tensor, g[:], oh1[:], oh2[:], ALU.add)
            yield
            st.then(dve, V.tensor_tensor, g[:], g[:], over_e(tot), ALU.mult)
            yield
            st.then(dve, V.tensor_copy, g16[k][:, :, 0:NE], g[:])
            yield
            st.then(dve, V.tensor_tensor, g16[k][:, :, NE:2 * NE], g[:],
                    g16[k][:, :, 0:NE].bitcast(F32), ALU.subtract)
            yield
            st.end()

        def router_act(act, k, t, d_at, g_at=None):
            e, d, e2, g = s_rexp[k], route[k][7], route[k][8], route[k][9]
            act.wait_ge(s_rt[k].sem, s_rt[k].per * t + d_at)
            nc.scalar.activation(e2[:], d[:], ACT.Exp).then_inc(e, 1)
            if g_at is not None:
                act.wait_ge(s_rt[k].sem, s_rt[k].per * t + g_at)
                nc.scalar.activation(g[:], g[:], ACT.Exp).then_inc(e, 1)

        @block.tensor
        def _(pe):
            def front(t, b, i):
                if i >= 5:
                    return
                w = (4, 2, 3, 0, 1)[i]
                if i == 0:
                    pe.wait_ge(s_xhi, t + 1)
                    pe.wait_ge(s_xlo, t + 1)
                if i >= 2:
                    pe.wait_ge(s_raw, 3 * t + i - 1)
                elif later(t, 1):
                    pe.wait_ge(s_z, 2 * t - 1 + i)
                c = slice(w * P, (w + 1) * P)
                mm3(pe, ps[(b + i) % 2][:, :], Win_hi[:, c], Win_lo[:, c], x_hi[b][:], x_lo[b][:]
                    ).then_inc(s_proj, 1)

            def ssd(t, b, k):
                if k < H:
                    h = k
                    pe.wait_ge(s_conv, 3 * t + 2 + h)
                    if h == 1:
                        pe.wait_ge(s_xdt, 2 * t + h)
                    elif later(t, 1):
                        pe.wait_ge(s_Bw, 2 * t)
                    for c in range(CH):
                        mm = pe.transpose(ps4[3][:, c, :], xs[b][:, h, c * P:(c + 1) * P], ident)
                    mm.then_inc(s_ssd, 1)
                    pe.wait_ge(s_dAU, 2 * t + h + 1)
                    if h == 1:
                        if later(t, 1):
                            pe.wait_ge(s_yd, 2 * t)
                    else:
                        if later(t, 3):
                            pe.wait_ge(s_G, t - 2)
                        if later(t, 1):
                            pe.wait_ge(s_state.sem, s_state.per * t)
                    pe.matmul(ps[(2, 5)[h]][:, :], ones, dAU[:, h, :, :], start=True, stop=True
                              ).then_inc(s_ssd, 1)
                elif k == 2:
                    pe.wait_ge(s_xdt, 2 * t + 2)
                    apart(pe)
                    for c in range(CH):
                        mm = pe.transpose(ps4[3][:, c, 0:N], BC[b][0:N, c * P:(c + 1) * P],
                                          ident[0:N, 0:N])
                    mm.then_inc(s_ssd, 1)
                    pe.wait_ge(s_C0, 16 * (t + 1))
                    if later(t, 1):
                        pe.wait_ge(s_ln["ln1"][0].sem, s_ln["ln1"][0].per * (t - 1) + LN_RES)
                    for c in range(CH):
                        q = slice(c * P, (c + 1) * P)
                        mm = pe.matmul(ps4[4][:, c, :], BC[b][0:N, q], C0[b][:, q], start=True, stop=True)
                    mm.then_inc(s_ssd, 1)
                elif k < 5:
                    h = k - 3
                    pe.wait_ge(s_Bw, 2 * t + h + 1)
                    if h == 0:
                        pe.wait_ge(s_exp, 2 * t + 2)
                    else:
                        pe.wait_ge(s_state.sem, s_state.per * t + 1 + CH)
                    for c in range(CH):
                        mm = pe.matmul(ps4[2][0:N, c, :], Bw[:, h, c, :], xdt[:, h, c, :],
                                       start=True, stop=True)
                    mm.then_inc(s_ssd, 1)
                elif k < 7:
                    h = k - 5
                    pe.wait_ge(s_M, 2 * t + h + 1)
                    pe.wait_ge(s_Cs, 2 * t + h + 1)
                    pe.wait_ge(s_state.sem, s_state.per * t + 1 + CH * (h + 1))
                    if h == 1:
                        pe.wait_ge(s_yd, 2 * t + 1)
                    else:
                        if later(t, 1):
                            pe.wait_ge(s_yd, 2 * t)
                        if later(t, 2):
                            pe.wait_ge(s_ln["ln2"][0].sem, s_ln["ln2"][0].per * (t - 2) + LN_RES)
                    for c in range(CH):
                        pe.matmul(ps4[5][:, c, :], xdt[:, h, c, :], M[:, h, c, :], start=True, stop=False)
                        mm = pe.matmul(ps4[5][:, c, :], state[:, h, c, :],
                                       Cs[:, h, c * P:(c + 1) * P], start=False, stop=True)
                    mm.then_inc(s_ssd, 1)
                elif k == 7:
                    pe.wait_ge(s_yg, 2 * t + 2)
                    pe.wait_ge(s_M, 2 * t + 2)
                    if later(t, 2):
                        pe.wait_ge(s_x2T, t - 1)
                    for c in range(CH):
                        for h in range(H):
                            mm = pe.matmul(ps4[4][:, c, :], yg[b][:, h, c * P:(c + 1) * P],
                                           Wout_sb[:, h, :], start=h == 0, stop=h == 1)
                    mm.then_inc(s_scan, 1)

            A, B, A4, B4 = ps[6], ps[7], ps4[6], ps4[7]

            def moe(t, b, k):
                if k == 1:
                    pe.wait_ge(s_norm["ln1"], t + 1)
                    if later(t, 1):
                        pe.wait_ge(s_moeD, 5 * t)
                    for c in range(CH):
                        mm = pe.transpose(A4[:, c, :], x1[b][:, c, :], ident)
                    mm.then_inc(s_moe, 1)
                elif k == 2:
                    pe.wait_ge(s_moeA, 6 * t + A_XT)
                    if later(t, 1):
                        pe.wait_ge(s_moeD, 5 * t)
                    for c in range(CH):
                        mm = pe.matmul(B[:, c * NE:(c + 1) * NE], x1T[:, c * P:(c + 1) * P], wgate_sb[:],
                                       start=True, stop=True)
                    mm.then_inc(s_moe, 1)
                elif k in (3, 4):
                    for m in (0, 1) if k == 3 else (2, 3):
                        if m == 0:
                            pe.wait_ge(s_x1lo, t + 1)
                            pe.wait_ge(s_wd, 1)
                        elif m == 1:
                            pe.wait_ge(s_moeD, 5 * t + D_LG)
                        else:
                            pe.wait_ge(s_moeA, 6 * t + A_H0 + m - 2)
                        r = slice(m * P, (m + 1) * P)
                        mm3(pe, (A if m % 2 == 0 else B)[:, :], Wd_hi[:, r], Wd_lo[:, r], x1T_hi[:],
                            x1T_lo[:]).then_inc(s_moe, 1)
                elif k == 6:
                    pe.wait_ge(s_rt["ra"].sem, s_rt["ra"].per * (t + 1))
                    pe.wait_ge(s_moeA, 6 * t + A_H2)
                    for c in range(CH):
                        mm = pe.transpose(A4[0:2 * NE, c, :], g16["ra"][:, c, :].bitcast(F32), ident)
                    mm.then_inc(s_moe, 1)
                elif k in (7, 8):
                    for m in (0, 1) if k == 7 else (2, 3):
                        if m == 0:
                            pe.wait_ge(s_moeA, 6 * t + A_GT)
                        if m > 1:
                            pe.wait_ge(s_moeD, 5 * t + D_B0 + m - 2)
                        pe.matmul((B if m % 2 == 0 else A)[:, :], sel_r[:, m * P:(m + 1) * P], gT[:],
                                  start=True, stop=True).then_inc(s_moe, 1)
                elif k in (9, 10):
                    pe.wait_ge(s_moeD, 5 * t + D_B3)
                    pe.wait_ge(s_yd, 2 * (min(t + 2, NT) if isinstance(t, int) else t + 2))
                    pe.wait_ge(s_exp, 2 * (min(t + 3, NT) if isinstance(t, int) else t + 3))
                    for c in (0, 1) if k == 9 else (2, 3):
                        q = slice(c * P, (c + 1) * P)
                        for m in range(M0):
                            pe.matmul(ps4[5][:, c, :], h0[:, m, q], Wu_sb[:, m, :], start=m == 0, stop=False)
                        pe.matmul(ps4[5][:, c, :], gT[:, q], bu_r[:, 0, :], start=False, stop=False)
                        mm = pe.matmul(ps4[5][:, c, :], gT[:, q], bu_r[:, 1, :], start=False, stop=True)
                    if k == 10:
                        mm.then_inc(s_moeO, 1)

            def tail(t, b, k):
                if k == 1:
                    pe.wait_ge(s_norm["ln2"], t + 1)
                    if isinstance(t, int):
                        pe.wait_ge(s_ln["ln1"][0].sem, s_ln["ln1"][0].per * min(t + 2, NT))
                        pe.wait_ge(s_M, 2 * min(t + 3, NT))
                        pe.wait_ge(s_state.sem, s_state.per * min(t + 3, NT))
                    else:
                        pe.wait_ge(s_M, 2 * (t + 3))
                        pe.wait_ge(s_state.sem, s_state.per * (t + 3))
                    for c in range(CH):
                        mm = pe.transpose(ps4[4][:, c, :], x2[:, c, :], ident)
                    mm.then_inc(s_tail, 1)
                    for c in range(CH):
                        mm = pe.matmul(ps[2][:, 0:P], x2[:, c, :], x2[:, c, :], start=c == 0,
                                       stop=c == CH - 1)
                    mm.then_inc(s_tail, 1)


            def attention(b):
                pe.wait_ge(s_G, NT - NB + b + 1)
                if b == 1:
                    pe.wait_ge(s_KI, 1)
                pe.matmul(ps[3][:, 0:P], Wq_sb[:], G[b][:], start=True, stop=True).then_inc(s_KIp, 1)

            def prepare(u, b, piece, A=ps[6], B=ps[7]):
                A4, B4 = (v[:, :].rearrange("p (c q) -> p c q", c=CH) for v in (A, B))
                if piece == 0:
                    pe.wait_ge(s_cur2, u + 1)
                    pe.wait_ge(s_KI, (1 if isinstance(u, int) and u == 0 else NB))
                    if later(u, 1):
                        pe.wait_ge(s_acc0, u)
                    for c in range(CH):
                        mm = pe.matmul(A4[:, c, :], x2T_cur[:, c * P:(c + 1) * P], KI[b][:], start=True,
                                       stop=True)
                elif piece == 1:
                    pe.wait_ge(s_ln["ln3"][0].sem, s_ln["ln3"][0].per * (u + 1))
                    if later(u, 1):
                        pe.wait_ge(s_wbc, 8 * (u - 1) + 3)
                    for c in range(CH):
                        mm = pe.transpose(B4[:, c, :], x3[b][:, c, :], ident)
                elif piece == 2:
                    pe.wait_ge(s_x3T, u + 1)
                    for c in range(CH):
                        mm = pe.matmul(A[:, c * NE:(c + 1) * NE], x3T[:, c * P:(c + 1) * P], rw_sb[:],
                                       start=True, stop=True)
                elif piece == 3:
                    pe.wait_ge(s_rt["rb"].sem, s_rt["rb"].per * (u + 1))
                    if later(u, 1):
                        pe.wait_ge(s_wbc, 8 * (u - 1) + 7)
                    else:
                        pe.wait_ge(s_moeD, 5 * NT)
                    for c in range(CH):
                        mm = pe.transpose(B4[0:2 * NE, c, :], g16["rb"][:, c, :].bitcast(F32), ident)
                else:
                    pe.wait_ge(s_w16T, u + 1)
                    pe.matmul(A[:, :], b2_r[:, 0, :], w16T[b][:], start=True, stop=False)
                    mm = pe.matmul(A[:, :], b2_r[:, 1, :], w16T[b][:], start=False, stop=True)
                mm.then_inc(s_pre, 1)

            def finish(u, b, first_wb):
                pe.wait_ge(s_sum, 8 * (u + 1))
                pe.wait_ge(s_wbc, 8 * (u + 1) + first_wb)
                for c in range(CH):
                    mm = pe.transpose(B4[:, c, :], oT[b][:, c * P:(c + 1) * P], ident)
                mm.then_inc(s_fin, 1)

            def up(u, b, q):
                if q >= RH or later(u, 1):
                    pe.wait_ge(s_hhi, 32 * u + q + 1 - RH)
                r = slice(q * P, (q + 1) * P)
                mm3(pe, ps[q % RH][:, :], w_hi[:, 0, r], w_lo[:, 0, r],
                    x3T_hi[b][:], x3T_lo[b][:]).then_inc(s_up, 1)

            def experts(u, b, last=False, first=False):
                for q in range(NE * FT):
                    if q + LAG < NE * FT:
                        up(u, b, q + LAG)
                    elif not last:
                        if q + LAG == NE * FT:
                            pe.wait_ge(s_x3lo, u + 2)
                        up(u + 1, 1 - b, q + LAG - NE * FT)
                    e, f = divmod(q, FT)
                    if f == 2:
                        if e > 0 or later(u, 1):
                            pe.wait_ge(s_wbc, 8 * u + e)
                        if e == 0:
                            pe.wait_ge(s_w16T, u + 1)
                        if e == 1 and not first:
                            pe.wait_ge(s_ln["ln4"][0].sem, s_ln["ln4"][0].per * (u - 1) + LN_RES)
                        if e == 3 and not last:
                            pe.wait_ge(s_x3T, u + 2)
                        if e == 7 and not last:
                            pe.wait_ge(s_w16T, u + 2)
                        rows = sel_r[:, M0 * P + e:M0 * P + e + 1].to_broadcast([2 * NE, P])
                        pe.matmul(B[:, :], rows, w16T[b][:], start=True, stop=True).then_inc(s_wb, 1)
                    pe.wait_ge(s_hhi, 32 * u + q + 1)
                    if f == 0 and (e >= 2 or later(u, 1)):
                        pe.wait_ge(s_yw, 8 * u + e - 1)
                    r, i, dst = slice(q * P, (q + 1) * P), q % RH, ps[4 + e % 2][:, :]
                    pe.matmul(dst, w_hi[:, 1, r], h1_hi[i], start=f == 0, stop=False)
                    pe.matmul(dst, w_lo[:, 1, r], h1_hi[i], start=False, stop=False)
                    pe.wait_ge(s_hlo, 32 * u + q + 1)
                    pe.matmul(dst, w_hi[:, 1, r], h1_lo[i], start=False, stop=f == FT - 1
                              ).then_inc(s_down, 1)
                    if q == PE_FINISH and not first:
                        finish(u - 1, 1 - b, 1)
                    if q in PE_AT and not last:
                        prepare(u + 1, 1 - b, PE_AT[q])

            def ahead(g):
                if g == 0:
                    attention(0)
                elif g in (1, 3, 4):
                    prepare(0, 0, (1, 3, 4).index(g), A=ps[0], B=ps[1])

            def round_(i, b):
                for g, calls in enumerate(in_round(PE_ROUND, i, b, (None, front, ssd, moe, tail))):
                    for f, *a in calls:
                        f(*a)
                    if isinstance(i, int) and i == NT + 2:
                        ahead(g)

            def time_steps():
                pe.wait_ge(s_in0, 16 * 6)
                for n in range(NCHUNK):
                    mm = pe.matmul(ps[7][:, n * H:(n + 1) * H], xT_sb[:, n // CH, (n % CH) * P:(n % CH + 1) * P],
                                   Win_sb[:, 640:642], start=True, stop=True)
                mm.then_inc(s_p0["pe"], 1)
                pe.wait_ge(s_p0["dve"], 1)
                flat = dA[:, :, :].rearrange("p n h -> p (n h)")
                pe.matmul(ps[6][:, 0:H * NCHUNK], tri, flat, start=True, stop=True)
                pe.matmul(ps[5][:, 0:H * NCHUNK], ones, flat, start=True, stop=True).then_inc(s_p0["pe"], 1)
                pe.wait_ge(s_p0["act"], 4)
                pe.wait_ge(s_prep, 1)

            pe.wait_ge(s_prep0, 1)
            rounds(pe.Fori, round_, time_steps)
            attention(1)
            pe.wait_ge(s_rt["rb"].sem, s_rt["rb"].per)
            pe.wait_ge(s_x3lo, 1)
            pe.wait_ge(s_w, 2 * NT)
            for q in range(LAG):
                up(0, 0, q)
            prepare(0, 0, 3)
            prepare(0, 0, 4)
            pe.wait_ge(s_KI, NB)
            pe.wait_ge(s_x2T, NT)
            experts(0, 0, first=True)
            with pe.Fori(0, NT // 2 - 1) as v:
                experts(2 * v + 1, 1)
                experts(2 * v + 2, 0)
            experts(NT - 1, 1, last=True)
            finish(NT - 1, 1, 0)

        @block.scalar
        def _(act):
            S = nc.scalar
            def split(t, b, k):
                if isinstance(t, int) and t == 1 and k == 0:
                    return
                if later(t, 2):
                    act.wait_ge(s_proj, 5 * (t - 1))
                S.activation(x_hi[b][:], xT_sb[:, bass.ds(t, 1), :].rearrange("p o q -> p (o q)"),
                             ACT.Copy).then_inc(s_xhi, 1)
                if later(t, 1):
                    act.wait_ge(s_tap.sem, s_tap.per * t)
                S.activation(raw[:, :, 0:HIST], hist[b][:, :, :], ACT.Copy).then_inc(s_hist, 1)

            def front(t, b, k):
                if k < 3:
                    act.wait_ge(s_proj, 5 * t + k + 1)
                    if later(t, 1):
                        act.wait_ge(s_conv, 3 * t - 2 + k)
                    apart(act)
                    S.activation(acc[:, k, :], ps[(b + k) % 2][:, :], ACT.Identity,
                                 scale=convw_sb[:, k, HIST:TAPS], bias=convb_sb[:, k:k + 1])
                    S.activation(raw[:, k, HIST:], ps[(b + k) % 2][:, :], ACT.Copy).then_inc(s_raw, 1)
                elif k < 5:
                    act.wait_ge(s_proj, 5 * t + k + 1)
                    if later(t, 2):
                        act.wait_ge(s_scan, t - 1)
                    S.activation(z2[b][:, k - 3, :], ps[(b + k) % 2][:, :], ACT.Tanh, scale=0.5
                                 ).then_inc(s_zt, 1)
                if k == 2:
                    act.wait_ge(s_raw, 3 * t + 3)
                    act.wait_ge(s_hist, 2 * t + 1)
                    S.activation(hist[b][:, :, :], raw[:, :, TILE:TILE + HIST], ACT.Copy
                                 ).then_inc(s_hist, 1)
                if 2 <= k < 5:
                    i = k - 2
                    act.wait_ge(s_tap.sem, s_tap.per * t + (TAPS - 1) * (i + 1))
                    if later(t, 2):
                        act.wait_ge(s_ssd, 10 * (t - 2) + S_SC)
                        act.wait_ge(s_C0, 16 * (t - 1))
                        act.wait_ge(s_yg, 2 * (t - 1))
                    S.activation(BC[b][:, :] if i == 0 else xs[b][:, i - 1, :], acc[:, i, :], ACT.Tanh
                                 ).then_inc(s_th, 1)
                if k >= 5:
                    if k == 5:
                        act.wait_ge(s_wraw, 32 * (t + 1))
                    S.activation(w_hi[:, k - 5, bass.ds(t * TILE, TILE)], wraw[:, k - 5, :], ACT.Copy
                                 ).then_inc(s_whi, 1)

            def ssd(t, b, k):
                if k < H:
                    if k == 0:
                        act.wait_ge(s_cur, t + 1)
                    act.wait_ge(s_ssd, 10 * t + (S_ROW0, S_ROW1)[k])
                    if later(t, 1):
                        act.wait_ge(s_ssd, 10 * (t - 1) + (S_Y0, S_Y1)[k])
                    apart(act)
                    for c in range(CH):
                        ins = S.activation(E[:, k, c, :], ps4[(2, 5)[k]][:, c, :], ACT.Relu, scale=-1.0,
                                           bias=cur[b][:, c, k, K_CS:K_CS + 1])
                    ins.then_inc(s_cs, 1)
                    S.activation(Cs[:, k, :], ps[(2, 5)[k]][0:N, :], ACT.Exp)
                    act.wait_ge(s_cs, 2 * t + k + 1)
                    S.activation(E[:, k, :, :], E[:, k, :, :], ACT.Exp, scale=-1.0).then_inc(s_exp, 1)

            A, B = ps[6], ps[7]

            def moe(t, b, k):
                if k == 0:
                    ln_act(act, "ln1", t, x1[b])
                elif k == 1:
                    act.wait_ge(s_moe, 11 * t + E_XT)
                    if later(t, 1):
                        act.wait_ge(s_moe, 11 * (t - 1) + E_H3)
                        act.wait_ge(s_x1lo, t)
                    S.activation(x1T[:], A[:, :], ACT.Copy).then_inc(s_moeA, 1)
                    S.activation(x1T_hi[:], A[:, :], ACT.Copy).then_inc(s_x1hi, 1)
                elif k in (3, 4):
                    for m in (0, 1) if k == 3 else (2, 3):
                        act.wait_ge(s_moe, 11 * t + E_H0 + m)
                        if m == 0 and later(t, 1):
                            act.wait_ge(s_moeO, t)
                        S.activation(h0[:, m, :], (A if m % 2 == 0 else B)[:, :], ACT.Relu,
                                     bias=bd_sb[:, m:m + 1]).then_inc(s_moeA, 1)
                elif k == 5:
                    router_act(act, "ra", t, 12)
                elif k == 6:
                    act.wait_ge(s_moe, 11 * t + E_GT)
                    S.activation(gT[:], A[0:2 * NE, :], ACT.Copy).then_inc(s_moeA, 1)

            def tail(t, b, k):
                if k == 0:
                    ln_act(act, "ln2", t, x2)
                else:
                    act.wait_ge(s_tail, 2 * t + 1)
                    S.activation(x2T[:, bass.ds(t, 1), :].rearrange("p o q -> p (o q)"),
                                 ps[4][:, :], ACT.Copy).then_inc(s_x2T, 1)


            def prepare(u, b, piece, B=ps[7]):
                A = ps[6]
                if piece == 1:
                    act.wait_ge(s_pre, 5 * u + Q_XT)
                    if later(u, 1):
                        act.wait_ge(s_x3lo, u)
                    S.activation(x3T, B[:, :], ACT.Copy).then_inc(s_x3T, 1)
                elif piece == 2:
                    router_act(act, "rb", u, 13, 14)
                elif piece == 3:
                    act.wait_ge(s_pre, 5 * u + Q_GT)
                    if not later(u, 1):
                        act.wait_ge(s_moeO, NT)
                    S.activation(w16T[b][:], B[0:2 * NE, :], ACT.Copy).then_inc(s_w16T, 1)
                elif piece == 4:
                    act.wait_ge(s_pre, 5 * u + Q_B2)
                    if later(u, 2):
                        act.wait_ge(s_fin, u - 1)
                    S.activation(oT[b], A[:, :], ACT.Copy).then_inc(s_acc0, 1)

            def experts(u, b, last=False, first=False):
                if first:
                    prepare(0, 0, 3)
                    prepare(0, 0, 4)
                for q in range(NE * FT):
                    e, f = divmod(q, FT)
                    bank, old = ps[q % RH], 32 * u + q + 1 - RH
                    act.wait_ge(s_up, 32 * u + q + 1)
                    if q >= RH or later(u, 1):
                        act.wait_ge(s_hlo, old)
                    S.activation(h1[:, q % RH, :], bank[:, :], ACT.Relu, bias=b1_sb[:, q:q + 1]
                                 ).then_inc(s_relu, 1)
                    if q >= RH or later(u, 1):
                        act.wait_ge(s_down, old)
                    S.activation(h1_hi[q % RH], bank[:, :], ACT.Relu, bias=b1_sb[:, q:q + 1]
                                 ).then_inc(s_hhi, 1)
                    if q in ACT_AT and not last:
                        prepare(u + 1, 1 - b, ACT_AT[q])

            def ahead(g):
                if g == 3:
                    prepare(0, 0, 1, B=ps[1])
                elif g == 6:
                    prepare(0, 0, 2)

            def round_(i, b):
                for g, calls in enumerate(in_round(ACT_ROUND, i, b, (split, front, ssd, moe, tail))):
                    for f, *a in calls:
                        f(*a)
                    if isinstance(i, int) and i == NT + 2:
                        ahead(g)

            def time_steps():
                split(1, 1, None)
                act.wait_ge(s_in0, 16 * 6)
                S.activation(expA[:], small_sb[:, 0, :], ACT.Exp).then_inc(s_p0["act"], 1)
                act.wait_ge(s_absv, 1)
                S.activation(sp[1][:], sp[1][:], ACT.Exp, scale=-1.0).then_inc(s_p0["act"], 1)
                act.wait_ge(s_p0["pe"], 2)
                ps6v = ps[6][:, 0:H * NCHUNK].rearrange("p (n h) -> p n h", h=H)
                ps5v = ps[5][:, 0:H * NCHUNK].rearrange("p (n h) -> p n h", h=H)
                S.activation(cols[:, :, :, K_CS], ps6v, ACT.Copy).then_inc(s_p0["act"], 1)
                S.activation(cols[:, :, :, K_TOT], ps5v, ACT.Copy).then_inc(s_p0["act"], 1)
                act.wait_ge(s_p0["dve"], 2)
                S.activation(cols[:, :, :, K_REST], cols[:, :, :, K_REST], ACT.Exp).then_inc(s_p0["act"], 1)
                S.activation(cols[:, :, :, K_TOT], cols[:, :, :, K_TOT], ACT.Exp).then_inc(s_p0["act"], 1)
                act.wait_ge(s_in, 16 * 11)
                act.wait_ge(s_prep, 1)

            act.wait_ge(s_prep0, 1)
            rounds(act.Fori, round_, time_steps)
            experts(0, 0, first=True)
            with act.Fori(0, NT // 2 - 1) as v:
                experts(2 * v + 1, 1)
                experts(2 * v + 2, 0)
            experts(NT - 1, 1, last=True)

        @block.vector
        def _(dve):
            V = nc.vector
            p0 = Steps(s_p0chain, 0)
            p0.begin(0)

            def do(ins):
                p0.inc(ins)
                p0.wait(dve)

            for b in range(NB):
                V.memset(hist[b][:], 0.0)
                V.memset(carry[b][:], 0.0)
                V.memset(G[b][:], 0.0)
            dve.wait_ge(s_first, 16 * 4)
            do(V.tensor_copy(Win_hi[:], Win_sb[:, 0:640]))
            do(V.tensor_tensor(Win_lo[:], Win_sb[:, 0:640], Win_hi[:].bitcast(F32), ALU.subtract))
            do(V.tensor_scalar(convw_sb[:], convw_sb[:], 0.5, None, ALU.mult))
            V.tensor_scalar(convb_sb[:], convb_sb[:], 0.5, None, ALU.mult).then_inc(s_prep0, 1)
            dve.wait_ge(s_prep0, 1)

            def taps(t, b, i):
                dve.wait_ge(s_raw, 3 * t + i + 1)
                if i == 0:
                    dve.wait_ge(s_hist, 2 * t + 1)
                    s_tap.begin(t)
                a = acc[:, i, :]
                for k in range(TAPS - 1):
                    if k:
                        s_tap.wait(dve)
                    s_tap.inc(V.scalar_tensor_tensor(out=a, in0=raw[:, i, k:k + TILE],
                                                     scalar=convw_sb[:, i, k:k + 1], in1=a,
                                                     op0=ALU.mult, op1=ALU.add))
                    yield
                if i == 2:
                    s_tap.end()

            def front(t, b, k):
                if 1 <= k < 4:
                    yield from taps(t, b, k - 1)
                if 3 <= k < 6:
                    i = k - 3
                    dve.wait_ge(s_th, 3 * t + i + 1)
                    dst = BC[b][:, :] if i == 0 else xs[b][:, i - 1, :]
                    V.scalar_tensor_tensor(out=dst, in0=dst, scalar=1.0, in1=acc[:, i, :],
                                           op0=ALU.add, op1=ALU.mult).then_inc(s_conv, 1)
                    yield
                if 4 <= k < 6:
                    i = k - 4
                    dve.wait_ge(s_zt, 2 * t + i + 1)
                    V.scalar_tensor_tensor(out=z2[b][:, i, :], in0=z2[b][:, i, :], scalar=1.0,
                                           in1=ps[(b + i + 3) % 2][:, :], op0=ALU.add, op1=ALU.mult
                                           ).then_inc(s_z, 1)
                    yield

            def ssd(t, b, k):
                if k < H:
                    h = k
                    if h == 0:
                        dve.wait_ge(s_cur, t + 1)
                    dve.wait_ge(s_ssd, 10 * t + (S_TX0, S_TX1)[h])
                    if later(t, 1):
                        dve.wait_ge(s_ssd, 10 * (t - 1) + (S_Y0, S_Y1)[h])
                    V.tensor_tensor(xdt[:, h, :, :], ps4[3],
                                    cur[b][:, :, h, K_DT:K_DT + 1].to_broadcast([P, CH, P]), ALU.mult
                                    ).then_inc(s_xdt, 1)
                    yield
                elif k == 2:
                    s_state.begin(t)
                    if later(t, 1):
                        dve.wait_ge(s_ssd, 10 * (t - 1) + S_Y1)
                    s_state.inc(V.tensor_copy(state[:, :, 0, :], carry[b][:]))
                    yield
                    dve.wait_ge(s_ssd, 10 * t + S_TB)
                    for h in range(H):
                        V.tensor_tensor(Bw[:, h, :, :], ps4[3][:, :, 0:N],
                                        cur[b][:, :, h, K_REST:K_REST + 1].to_broadcast([P, CH, N]),
                                        ALU.mult).then_inc(s_Bw, 1)
                        yield
                    dve.wait_ge(s_ssd, 10 * t + S_SC)
                    for h in range(H):
                        dve.wait_ge(s_mask, 2 * t + h + 1)
                        V.tensor_tensor(M[:, h, :, :], ps4[4], E[:, h, :, :], ALU.mult
                                        ).then_inc(s_M, 1)
                        yield
                elif k < 5:
                    h = k - 3
                    dve.wait_ge(s_ssd, 10 * t + (S_INC0, S_INC1)[h])
                    for c in range(CH):
                        s_state.wait(dve)
                        s_state.inc(V.scalar_tensor_tensor(
                            out=state[:, h, c + 1, :] if c + 1 < CH else carry[b][:, h, :],
                            in0=state[:, h, c, :],
                            scalar=cur[b][0:N, c, h, K_TOT:K_TOT + 1], in1=ps4[2][0:N, c, :],
                            op0=ALU.mult, op1=ALU.add))
                        yield
                    if h == 1:
                        s_state.end()
                elif k < 7:
                    h = k - 5
                    dve.wait_ge(s_ssd, 10 * t + (S_Y0, S_Y1)[h])
                    V.scalar_tensor_tensor(out=yd[b][:, h, :], in0=xs[b][:, h, :],
                                           scalar=small_sb[:, 2, h:h + 1], in1=ps[5][:, :],
                                           op0=ALU.mult, op1=ALU.add).then_inc(s_yd, 1)
                    yield
                elif k == 8:
                    st = s_ln["ln1"][0]
                    st.begin(t)
                    dve.wait_ge(s_scan, t + 1)
                    dve.wait_ge(s_x, 16 * (t + 1))
                    if later(t, 2):
                        dve.wait_ge(s_moe, 11 * (t - 2) + E_XT)
                        dve.wait_ge(s_ln["ln2"][0].sem, s_ln["ln2"][0].per * (t - 2) + LN_RES)
                    st.inc(V.tensor_tensor(x1[b][:], ps4[4], x_sb[:], ALU.add))
                    yield
                    yield from ln_stats(dve, "ln1", t, x1[b])

            def moe(t, b, k):
                if k == 2:
                    dve.wait_ge(s_moe, 11 * t + E_LG)
                    if later(t, 1):
                        dve.wait_ge(s_moe, 11 * (t - 1) + E_GT)
                    route_a[0] = router_dve(dve, "ra", t,
                                            ps[7][:, 0:CH * NE].rearrange("p (c e) -> p c e", c=CH),
                                            s_moeD)
                    for _ in range(1):
                        next(route_a[0])
                        yield
                elif k in (3, 4, 5):
                    for _ in range({3: 6, 4: 5, 5: 7}[k]):
                        next(route_a[0])
                        yield
                    if k == 5:
                        advance(route_a[0], 1)
                elif k in (7, 8):
                    for m in (0, 1) if k == 7 else (2, 3):
                        dve.wait_ge(s_moe, 11 * t + E_B0 + m)
                        dve.wait_ge(s_moeA, 6 * t + A_H0 + m)
                        V.tensor_tensor(h0[:, m, :], h0[:, m, :], (ps[7] if m % 2 == 0 else ps[6])[:, :],
                                        ALU.mult).then_inc(s_moeD, 1)
                        yield
                elif k == 10:
                    st = s_ln["ln2"][0]
                    st.begin(t)
                    dve.wait_ge(s_moeO, t + 1)
                    if later(t, 1):
                        dve.wait_ge(s_tail, 2 * t)
                    st.inc(V.tensor_tensor(x2[:], ps4[5], x1[b][:], ALU.add))
                    yield
                elif k == 11:
                    s_ln["ln2"][0].begin(t, LN_RES)
                    yield from ln_stats(dve, "ln2", t, x2)

            route_a = [None]

            def tail(t, b, k):
                if k == 1:
                    dve.wait_ge(s_tail, 2 * t + 2)
                    V.tensor_tensor(G[b][:], G[b][:], ps[2][:, 0:P], ALU.add).then_inc(s_G, 1)
                    yield


            def attention(b):
                dve.wait_ge(s_KIp, b + 1)
                V.tensor_tensor(KI[b][:], ps[3][:, 0:P], ident, ALU.add).then_inc(s_KI, 1)
                yield

            def layernorm3(u, b, A=ps4[6]):
                st = s_ln["ln3"][0]
                st.begin(u)
                dve.wait_ge(s_pre, 5 * u + Q_ATT)
                if later(u, 2):
                    dve.wait_ge(s_ln["ln4"][0].sem, s_ln["ln4"][0].per * (u - 2) + LN_RES)
                st.inc(V.tensor_copy(x3[b][:], A))
                yield
                yield from ln_stats(dve, "ln3", u, x3[b])
                yield from ln_norm(dve, "ln3", u, x3[b], x3[b])

            def router(u, A=ps[6]):
                dve.wait_ge(s_pre, 5 * u + Q_LG)
                yield from router_dve(dve, "rb", u, A[:, 0:CH * NE].rearrange("p (c e) -> p c e", c=CH))

            def finish(u, b):
                st = s_ln["ln4"][0]
                st.begin(u)
                dve.wait_ge(s_fin, u + 1)
                if later(u, 1):
                    dve.wait_ge(s_out, 16 * u)
                st.inc(V.tensor_tensor(o_sb[:], ps4[7], x3[b][:], ALU.add))
                yield
                yield from ln_stats(dve, "ln4", u, o_sb)
                yield from ln_norm(dve, "ln4", u, o_sb, o_sb)

            def experts(u, b, last=False, first=False):
                done = None if first else finish(u - 1, 1 - b)
                norm = None if last else layernorm3(u + 1, 1 - b)
                route = None if last else router(u + 1)
                for q in range(NE * FT):
                    e, f = divmod(q, FT)
                    i = q % RH
                    dve.wait_ge(s_hhi, 32 * u + q + 1)
                    V.tensor_tensor(h1_lo[i], h1[:, i, :], h1_hi[i].bitcast(F32), ALU.subtract
                                    ).then_inc(s_hlo, 1)
                    if f == 3:
                        dve.wait_ge(s_wb, 8 * u + e + 1)
                        if e >= 2 or later(u, 1):
                            dve.wait_ge(s_yw, 8 * u + e - 1)
                        V.tensor_copy(wbc[:, e % 2, :], ps[7][:, :]).then_inc(s_wbc, 1)
                    if f == 1 and e >= 1:
                        gate(u, e - 1)
                    elif f == 1 and not first:
                        gate(u - 1, NE - 1)
                    for part, plan in ((done, DVE_LN4), (norm, DVE_LN3), (route, DVE_RT)):
                        if part is not None:
                            advance(part, plan.get(q, 0))
                for part in (done, norm, route):
                    assert part is None or next(part, None) is None

            def gate(u, e):
                dve.wait_ge(s_down, 32 * u + FT * (e + 1))
                dve.wait_ge(s_wbc, 8 * u + e + 1)
                if e >= 2 or later(u, 1):
                    dve.wait_ge(s_sum, 8 * u + e - 1)
                V.tensor_tensor(yw[:, e % 2, :], ps[4 + e % 2][:, :], wbc[:, e % 2, :], ALU.mult
                                ).then_inc(s_yw, 1)

            first = [layernorm3(0, 0, A=ps4[0]), router(0, A=ps[0])]

            def ahead(g):
                if g == 0:
                    yield from attention(0)
                elif g in (1, 2):
                    for _ in range((1 + CH + CH, CH)[g - 1]):
                        next(first[0])
                        yield
                elif g in (5, 7):
                    for _ in range(14 if g == 5 else 9):
                        next(first[1])
                        yield
                    if g == 7:
                        assert all(next(part, None) is None for part in first)

            def round_(i, b):
                for g, calls in enumerate(in_round(DVE_ROUND, i, b, (None, front, ssd, moe, tail))):
                    urgent = [({front: FRONT, ssd: SSD, moe: MOE, tail: TAIL}[f], a[-1]) in URGENT
                              for f, *a in calls]
                    weave(*(f(*a) for (f, *a), u in zip(calls, urgent) if u))
                    rest = [f(*a) for (f, *a), u in zip(calls, urgent) if not u]
                    if isinstance(i, int) and i == NT + 2:
                        rest.append(ahead(g))
                    weave(*rest)

            def time_steps():
                dve.wait_ge(s_in, 16 * 11)
                do(V.tensor_scalar(Wout_sb[:], Wout_sb[:], 0.5, None, ALU.mult))
                V.tensor_copy(sel_r[:], sel_sb)
                for dst, src in ((bu_r, bu_sb), (b2_r, b2_sb)):
                    do(V.tensor_copy(dst[:, 0, :], src[:]))
                    do(V.tensor_tensor(dst[:, 1, :], src[:], dst[:, 0, :].bitcast(F32), ALU.subtract))
                V.memset(half[:], -0.5).then_inc(s_prep, 1)
                v_, u_, s_, s2, q_ = sp
                dve.wait_ge(s_in0, 16 * 6)
                dve.wait_ge(s_p0["pe"], 1)
                raw_dt = ps[7][:, 0:H * NCHUNK].rearrange("p (n h) -> p n h", h=H)
                do(V.tensor_tensor(v_[:], raw_dt, small_sb[:, 1:2, :].to_broadcast([P, NCHUNK, H]), ALU.add))
                do(V.tensor_scalar(s2[:], v_[:], -1.0, None, ALU.mult))
                V.tensor_tensor(u_[:], s2[:], v_[:], ALU.max).then_inc(s_absv, 1)
                dve.wait_ge(s_p0["act"], 2)
                do(V.tensor_scalar(s2[:], u_[:], 2.0, None, ALU.add))
                do(V.reciprocal(s_[:], s2[:]))
                do(V.tensor_tensor(s_[:], s_[:], u_[:], ALU.mult))
                do(V.tensor_tensor(s2[:], s_[:], s_[:], ALU.mult))
                do(V.tensor_scalar(q_[:], s2[:], 1.0 / (2 * SERIES - 1), None, ALU.mult))
                for k in range(SERIES - 2, 0, -1):
                    do(V.scalar_tensor_tensor(out=q_[:], in0=q_[:], scalar=1.0 / (2 * k + 1), in1=s2[:],
                                              op0=ALU.add, op1=ALU.mult))
                do(V.tensor_scalar(q_[:], q_[:], 1.0, 2.0, ALU.add, ALU.mult))
                do(V.tensor_tensor(q_[:], q_[:], s_[:], ALU.mult))
                do(V.scalar_tensor_tensor(out=dtv[:], in0=v_[:], scalar=0.0, in1=q_[:], op0=ALU.max,
                                          op1=ALU.add))
                do(V.scalar_tensor_tensor(out=dA[:], in0=dtv[:], scalar=-1.0,
                                          in1=expA[:, :].unsqueeze(1).to_broadcast([P, NCHUNK, H]),
                                          op0=ALU.mult, op1=ALU.mult))
                V.tensor_copy(cols[:, :, :, K_DT], dtv[:])
                V.tensor_copy(cols[:, :, :, K_DA], dA[:]).then_inc(s_p0["dve"], 1)

                dve.wait_ge(s_prep, 1)
                dve.wait_ge(s_p0["act"], 4)
                V.tensor_tensor(cols[:, :, :, K_REST], cols[:, :, :, K_TOT], cols[:, :, :, K_CS], ALU.subtract
                                ).then_inc(s_p0["dve"], 1)

            rounds(dve.Fori, round_, time_steps)
            weave(attention(1))
            experts(0, 0, first=True)
            with dve.Fori(0, NT // 2 - 1) as v:
                experts(2 * v + 1, 1)
                experts(2 * v + 2, 0)
            experts(NT - 1, 1, last=True)
            gate(NT - 1, NE - 1)
            weave(finish(NT - 1, 1))

        @block.gpsimd
        def _(pool):
            L = nc.gpsimd
            def split(t, b, k):
                if isinstance(t, int) and t == 1 and k == 0:
                    return
                xt = xT_sb[:, bass.ds(t, 1), :].rearrange("p o q -> p (o q)")
                pool.wait_ge(s_xhi, t + 1)
                L.tensor_tensor(x_lo[b][:], xt, x_hi[b][:].bitcast(F32), ALU.subtract).then_inc(s_xlo, 1)

            def decays(t, b):
                if isinstance(t, int) and t == 0:
                    pool.wait_ge(s_prep, 1)
                    pool.wait_ge(s_p0["act"], 6)
                if later(t, 2):
                    pool.wait_ge(s_exp, 2 * (t - 1))
                    pool.wait_ge(s_state.sem, s_state.per * (t - 1))
                apart(pool)
                L.tensor_copy(cur[b][:], cols[:, bass.ds(CH * t, CH), :, :]).then_inc(s_cur, 1)
                pool.wait_ge(s_cur, t + 1)
                for h in range(H):
                    if later(t, 1):
                        pool.wait_ge(s_ssd, 10 * (t - 1) + (S_ROW0, S_ROW1)[h])
                    L.tensor_tensor(dAU[:, h, :, :], tri.unsqueeze(1).to_broadcast([P, CH, P]),
                                    cur[b][:, :, h, K_DA:K_DA + 1].to_broadcast([P, CH, P]), ALU.mult
                                    ).then_inc(s_dAU, 1)

            def parts(src, hi, lo, hisem, losem, n):
                apart(pool)
                L.tensor_copy(hi, src).then_inc(hisem, 1)
                pool.wait_ge(hisem, n)
                L.tensor_tensor(lo, src, hi.bitcast(F32), ALU.subtract).then_inc(losem, 1)

            def front(t, b, k):
                if k == 4:
                    if not isinstance(t, int) or t > 0:
                        decays(t, b)
                elif k >= 5:
                    pool.wait_ge(s_whi, 2 * t + k - 4)
                    c = bass.ds(t * TILE, TILE)
                    L.tensor_tensor(w_lo[:, k - 5, c], wraw[:, k - 5, :],
                                    w_hi[:, k - 5, c].bitcast(F32), ALU.subtract).then_inc(s_w, 1)

            def ssd(t, b, k):
                if k < H:
                    h = k
                    pool.wait_ge(s_exp, 2 * t + h + 1)
                    apart(pool)
                    L.affine_select(out=E[:, h, :, :], in_=E[:, h, :, :], compare_op=ALU.is_ge, fill=0.0,
                                    base=0, pattern=[[0, CH], [1, P]], channel_multiplier=-1
                                    ).then_inc(s_mask, 1)
                    pool.wait_ge(s_C0, 16 * (t + 1))
                    L.tensor_tensor(Cs[:, h, :], C0[b][:], Cs[:, h, :], ALU.mult).then_inc(s_Cs, 1)
                elif k in (5, 6):
                    h = k - 5
                    pool.wait_ge(s_yd, 2 * t + h + 1)
                    pool.wait_ge(s_z, 2 * t + h + 1)
                    L.tensor_tensor(yg[b][:, h, :], yd[b][:, h, :], z2[b][:, h, :], ALU.mult
                                    ).then_inc(s_yg, 1)
                elif k == 8:
                    ln_pool(pool, "ln1", t)

            def moe(t, b, k):
                if k == 1:
                    pool.wait_ge(s_x1hi, t + 1)
                    if later(t, 1):
                        pool.wait_ge(s_moe, 11 * (t - 1) + E_H3)
                    L.tensor_tensor(x1T_lo[:], x1T[:], x1T_hi[:].bitcast(F32), ALU.subtract
                                    ).then_inc(s_x1lo, 1)
                elif k == 11:
                    ln_pool(pool, "ln2", t)

            def between():
                split(1, 1, None)
                pool.wait_ge(s_in, 16 * 11)
                parts(Wd_sb, Wd_hi[:], Wd_lo[:], s_wd0, s_wd, 1)
                decays(0, 0)


            def prepare(u, b, piece):
                if piece == 0:
                    if later(u, 1):
                        pool.wait_ge(s_pre, 5 * (u - 1) + Q_ATT)
                        pool.wait_ge(s_x2T, NT)
                    else:
                        pool.wait_ge(s_x2T, 1)
                        pool.wait_ge(s_moe, 11 * (NT - 1) + E_H3)
                    apart(pool)
                    L.tensor_copy(x2T_cur[:], x2T[:, bass.ds(u, 1), :].rearrange("p o q -> p (o q)")
                                  ).then_inc(s_cur2, 1)
                elif piece == 1:
                    ln_pool(pool, "ln3", u)
                elif piece == 2:
                    pool.wait_ge(s_x3T, u + 1)
                    if later(u, 2):
                        pool.wait_ge(s_up, 32 * (u - 1))
                    parts(x3T, x3T_hi[b][:], x3T_lo[b][:], s_x3hi, s_x3lo, u + 1)

            def add(u, b, e):
                pool.wait_ge(s_yw, 8 * u + e + 1)
                if e == 0:
                    pool.wait_ge(s_acc0, u + 1)
                else:
                    pool.wait_ge(s_sum, 8 * u + e)
                L.tensor_tensor(oT[b], oT[b], yw[:, e % 2, :], ALU.add).then_inc(s_sum, 1)

            def experts(u, b, last=False, first=False):
                if not last:
                    prepare(u + 1, 1 - b, 0)
                if not first:
                    add(u - 1, 1 - b, NE - 1)
                    ln_pool(pool, "ln4", u - 1)
                for e in range(NE - 1):
                    if e == 1 and not last:
                        prepare(u + 1, 1 - b, 1)
                    if e == 2 and not last:
                        prepare(u + 1, 1 - b, 2)
                    add(u, b, e)

            def ahead(g):
                if g in (0, 1, 3):
                    prepare(0, 0, (0, 1, 3).index(g))

            def round_(i, b):
                for g, calls in enumerate(in_round(POOL_ROUND, i, b, (split, front, ssd, moe, None))):
                    for f, *a in calls:
                        f(*a)
                    if isinstance(i, int) and i == NT + 2:
                        ahead(g)

            rounds(pool.Fori, round_, between)
            experts(0, 0, first=True)
            with pool.Fori(0, NT // 2 - 1) as v:
                experts(2 * v + 1, 1)
                experts(2 * v + 2, 0)
            experts(NT - 1, 1, last=True)
            add(NT - 1, 1, NE - 1)
            ln_pool(pool, "ln4", NT - 1)


def layouts(i):
    import numpy as np

    f = {k: np.asarray(v) for k, v in i.items()}

    def rows(v, n=P):
        return np.ascontiguousarray(np.broadcast_to(v[None, :], (n,) + v.shape))

    x = f["L0_attn_x"].reshape(NB, NT // NB, CH, P, P)
    Win = f["L0_attn_W_in"]
    conv_rows = (np.arange(256, 384), np.arange(0, 128), np.arange(128, 256))
    cw = f["L0_attn_conv_w"].reshape(384, TAPS)
    cb = f["L0_attn_conv_b"]
    const = np.zeros((P, C_COLS), np.float32)
    const[:, C_ID:C_ID + P] = np.eye(P)
    const[:, C_TRI:C_TRI + P] = np.triu(np.ones((P, P)))
    const[:, C_ONE:C_ONE + P] = 1
    const[:, C_REV:] = NE - np.arange(NE)
    sel = np.concatenate([np.repeat(np.eye(NE, dtype=np.float32), 64, 1), np.eye(NE, dtype=np.float32)], 1)
    sel = np.concatenate([sel, sel], 0)
    d = {
        "x": x.transpose(3, 1, 0, 2, 4).reshape(P, NCHUNK, P),
        "xT": x.transpose(4, 1, 0, 2, 3).reshape(P, NT, TILE),
        "W_inT": Win.T,
        "conv_w": np.stack([cw[r] for r in conv_rows], 1),
        "conv_b": np.stack([cb[r] for r in conv_rows], 1),
        "A_log": rows(f["L0_attn_A_log"]),
        "dt_bias": rows(f["L0_attn_dt_bias"]),
        "D_skip": rows(f["L0_attn_D_skip"]),
        "W_outT": f["L0_attn_W_out"].T.reshape(H, P, P).transpose(1, 0, 2),
        "w_gate": f["L0_ffn_w_gate"],
        "WdT": f["L0_ffn_Wd"].transpose(1, 0, 2).reshape(P, M0 * P),
        "bd": f["L0_ffn_bd"].reshape(M0, P).T,
        "Wu": f["L0_ffn_Wu"].reshape(M0, P, P).transpose(1, 0, 2),
        "bu": np.concatenate([f["L0_ffn_bu"]] * 2, 0),
        "Wq": f["L1_attn_W_q"],
        "router_wT": f["L1_ffn_router_w"].T,
        "w1T": f["L1_ffn_w1"].transpose(2, 0, 1).reshape(P, NE * FT * P),
        "b1": f["L1_ffn_b1"].reshape(NE * FT, P).T,
        "w2T": f["L1_ffn_w2"].reshape(NE, P, FT, P).transpose(3, 0, 2, 1).reshape(P, NE * FT * P),
        "b2": np.concatenate([f["L1_ffn_b2"]] * 2, 0),
        "const": const,
        "sel": sel,
    }
    return {k: np.ascontiguousarray(v) for k, v in d.items()}


def kernel(**inputs):
    import numpy as np
    import concourse.bacc as bacc
    from concourse.bass_utils import run_bass_kernel_spmd

    data = layouts(inputs)
    nc = bacc.Bacc("TRN2", target_bir_lowering=False, num_devices=1)
    arrays, args = {}, {}
    for name, a in data.items():
        arrays[f"in_{name}"] = a
        args[name] = nc.dram_tensor(f"in_{name}", a.shape, mybir.dt.from_np(a.dtype), kind="ExternalInput").ap()
    args["out"] = nc.dram_tensor("out_x", (P, NCHUNK, P), F32, kind="ExternalOutput").ap()
    build_kernel(nc, **args)
    r = run_bass_kernel_spmd(nc, [arrays], core_ids=[0])
    o = np.asarray(r.results[0]["out_x"]).reshape(P, NT // NB, NB, CH, P)
    return np.ascontiguousarray(o.transpose(2, 1, 3, 0, 4)).reshape(NB, NT // NB * TILE, P)
```
